# Optimizing a Trainium2 kernel written in Bass

```python
import numpy as np
import jax
import jax.numpy as jnp

def _softmax(x, axis=-1):
    return jax.nn.softmax(x, axis=axis)

def _gelu(x):
    return jax.nn.gelu(x, approximate=True)

def _silu(x):
    return jax.nn.silu(x)

def _sigmoid(x):
    return jax.nn.sigmoid(x)

def _layernorm(x, axis=-1, eps=1e-05):
    m = jnp.mean(x, axis=axis, keepdims=True)
    v = jnp.var(x, axis=axis, keepdims=True)
    return (x - m) / jnp.sqrt(v + eps)

def _scatter_add(tgt, idx, src, axis=0):
    return tgt.at[idx].add(src)

def _segment_sum(src, seg, n):
    return jax.ops.segment_sum(src, seg, n)
kernel_name = 'mk_decoder_preln_d2_seqx_r8_1ef056'

def setup_inputs(seed: int=0):
    np.random.seed(seed)
    _w = jnp.asarray

    def _rec_inputs():
        import jax
        import jax.numpy as jnp
        _rk = jax.random.key(seed)
        x = 0.002226 + 0.9996 * jax.random.normal(jax.random.fold_in(_rk, 1), (4, 256, 128), jnp.float32)
        _lenS = 256 - jax.random.randint(jax.random.fold_in(_rk, 7), (4,), 0, max(1, 256 // 4) + 1, jnp.int32)
        _lenS2 = 256 - jax.random.randint(jax.random.fold_in(_rk, 8), (4,), 0, max(1, 256 // 4) + 1, jnp.int32)
        _ctx_1024P = jax.random.normal(jax.random.fold_in(_rk, 11), (4, 16, 128), jnp.float32)
        _ctx_1024c = jax.random.dirichlet(jax.random.fold_in(_rk, 511), 0.3 * jnp.ones((16,), jnp.float32), (4, 256))
        _ctx_1024t = jnp.einsum('bsk,bkd->bsd', _ctx_1024c, _ctx_1024P)
        _ctx_1024t = _ctx_1024t * jax.lax.rsqrt(jnp.mean(jnp.square(_ctx_1024t)) + 1e-12) * 0.953939
        ctx_1024 = -7.10856e-05 + 0.999911 * (_ctx_1024t + 0.3 * jax.random.normal(jax.random.fold_in(_rk, 611), (4, 256, 128), jnp.float32))
        _validS = jnp.arange(256)[None, :] < _lenS[:, None]
        _validS2 = jnp.arange(256)[None, :] < _lenS2[:, None]
        _causal = jnp.tril(jnp.ones((256, 256), dtype=bool))
        mask_BxS2_bk0 = jnp.logical_not(jnp.broadcast_to(_validS2[:, :], (4, 256)))
        return (x, ctx_1024, mask_BxS2_bk0)
    x, ctx_1024, mask_BxS2_bk0 = _rec_inputs()

    def _L0_attn_setup():
        import jax, jax.numpy as jnp
        import numpy as np
        D_MODEL = 128
        D_STATE = 128
        D_CONV = 4
        EXPAND = 2
        HEADDIM = 64
        CHUNK = 64
        D_INNER = EXPAND * D_MODEL
        NHEADS = D_INNER // HEADDIM
        D_IN_PROJ = 2 * D_INNER + 2 * D_STATE + NHEADS
        CONV_DIM = D_INNER + 2 * D_STATE
        B_SZ, L_SEQ = (2, 512)

        def _silu(v):
            return v * jax.nn.sigmoid(v)

        def _segsum(x):
            T = x.shape[-1]
            xr = jnp.broadcast_to(x[..., :, None], x.shape + (T,))
            m_strict = jnp.tril(jnp.ones((T, T), bool), -1)
            xs = jnp.cumsum(jnp.where(m_strict, xr, 0.0), axis=-2)
            m_incl = jnp.tril(jnp.ones((T, T), bool))
            return jnp.where(m_incl, xs, -jnp.inf)

        def _ssd(x, A, Bm, Cm):
            b, l, h, p = x.shape
            c = l // CHUNK
            x = x.reshape(b, c, CHUNK, h, p)
            Bm = Bm.reshape(b, c, CHUNK, D_STATE)
            Cm = Cm.reshape(b, c, CHUNK, D_STATE)
            A = A.reshape(b, c, CHUNK, h).transpose(0, 3, 1, 2)
            A_cumsum = jnp.cumsum(A, axis=-1)
            L = jnp.exp(_segsum(A))
            Y_diag = jnp.einsum('bcln,bcsn,bhcls,bcshp->bclhp', Cm, Bm, L, x)
            decay_states = jnp.exp(A_cumsum[..., -1:] - A_cumsum)
            states = jnp.einsum('bcln,bhcl,bclhp->bchpn', Bm, decay_states, x)
            states = jnp.concatenate([jnp.zeros_like(states[:, :1]), states], axis=1)
            pad_last = jnp.pad(A_cumsum[..., -1], ((0, 0), (0, 0), (1, 0)))
            decay_chunk = jnp.exp(_segsum(pad_last))
            new_states = jnp.einsum('bhzc,bchpn->bzhpn', decay_chunk, states)
            states = new_states[:, :-1]
            state_decay_out = jnp.exp(A_cumsum)
            Y_off = jnp.einsum('bcln,bchpn,bhcl->bclhp', Cm, states, state_decay_out)
            return (Y_diag + Y_off).reshape(b, l, h, p)
        key = jax.random.key(seed)
        ks = jax.random.split(key, 8)
        return {'u': jax.random.normal(ks[0], (B_SZ, L_SEQ, D_MODEL), jnp.float32), 'in_proj_w': jax.random.normal(ks[1], (D_MODEL, D_IN_PROJ), jnp.float32) * 0.02, 'conv_w': jax.random.normal(ks[2], (CONV_DIM, 1, D_CONV), jnp.float32) * 0.2, 'conv_b': jnp.zeros((CONV_DIM,), jnp.float32), 'dt_bias': jax.random.normal(ks[3], (NHEADS,), jnp.float32) * 0.1, 'A_log': jax.random.uniform(ks[4], (NHEADS,), jnp.float32, 0.0, 1.0), 'D': jax.random.normal(ks[5], (NHEADS,), jnp.float32) * 0.1, 'norm_w': jnp.ones((D_INNER,), jnp.float32), 'out_proj_w': jax.random.normal(ks[6], (D_INNER, D_MODEL), jnp.float32) * 0.02}
    _L0_attn_all = _L0_attn_setup()
    _L0_attn_in = {k: v for k, v in _L0_attn_all.items() if k in ('in_proj_w', 'conv_w', 'conv_b', 'dt_bias', 'A_log', 'D', 'norm_w', 'out_proj_w')}
    del _L0_attn_all

    def _L0_xattn_setup():
        import jax, jax.numpy as jnp
        import numpy as np
        DIM, DIM_HEAD, HEADS, SCALE = (128, 64, 8, 8.0)
        INNER = DIM_HEAD * HEADS
        LN_EPS = 1e-05
        L2_EPS = 1e-12

        def layer_norm(x, w, b):
            mu = jnp.mean(x, axis=-1, keepdims=True)
            var = jnp.mean(jnp.square(x - mu), axis=-1, keepdims=True)
            return (x - mu) * jax.lax.rsqrt(var + LN_EPS) * w + b

        def l2norm(t):
            n = jnp.sqrt(jnp.sum(jnp.square(t), axis=-1, keepdims=True))
            return t / jnp.maximum(n, L2_EPS)
        key = jax.random.key(seed)
        ks = jax.random.split(key, 8)
        b, n, m = (8, 1024, 64)
        x = jax.random.normal(ks[0], (b, n, DIM), dtype=jnp.float32)
        latents = jax.random.normal(ks[1], (b, m, DIM), dtype=jnp.float32)
        mask = jax.random.randint(ks[2], (b, n), 0, 2) > 0
        Wq = jax.random.normal(ks[3], (DIM, INNER), dtype=jnp.float32) * DIM ** (-0.5)
        Wkv = jax.random.normal(ks[4], (DIM, 2 * INNER), dtype=jnp.float32) * DIM ** (-0.5)
        Wo = jax.random.normal(ks[5], (INNER, DIM), dtype=jnp.float32) * INNER ** (-0.5)
        return {'x': x, 'latents': latents, 'mask': mask, 'ln_x_w': jnp.ones((DIM,)), 'ln_x_b': jnp.zeros((DIM,)), 'ln_l_w': jnp.ones((DIM,)), 'ln_l_b': jnp.zeros((DIM,)), 'Wq': Wq, 'Wkv': Wkv, 'q_scale': jnp.ones((DIM_HEAD,)), 'k_scale': jnp.ones((DIM_HEAD,)), 'Wo': Wo, 'ln_o_w': jnp.ones((DIM,)), 'ln_o_b': jnp.zeros((DIM,))}
    _L0_xattn_all = _L0_xattn_setup()
    _L0_xattn_in = {k: v for k, v in _L0_xattn_all.items() if k in ('ln_x_w', 'ln_x_b', 'ln_l_w', 'ln_l_b', 'Wq', 'Wkv', 'q_scale', 'k_scale', 'Wo', 'ln_o_w', 'ln_o_b')}
    del _L0_xattn_all

    def _L0_ffn_setup():
        import jax, jax.numpy as jnp
        import numpy as np
        from jax import lax
        T, B, I, M, O = (32, 64, 128, 128, 128)

        def _xavier(key, shape):
            fan_out, fan_in = shape
            limit = float(np.sqrt(6.0 / (fan_in + fan_out)))
            return jax.random.uniform(key, shape, jnp.float32, -limit, limit)
        key = jax.random.key(seed)
        ks = jax.random.split(key, 9)
        x = jax.random.normal(ks[0], (T, B, I), jnp.float32)
        return {'x': x, 'wf': _xavier(ks[1], (M, I)), 'uf': _xavier(ks[2], (M, M)), 'bf': jnp.zeros((M,), jnp.float32), 'wi': _xavier(ks[3], (M, I)), 'ui': _xavier(ks[4], (M, M)), 'bi': jnp.zeros((M,), jnp.float32), 'wc': _xavier(ks[5], (M, I)), 'uc': _xavier(ks[6], (M, M)), 'bc': jnp.zeros((M,), jnp.float32), 'wo': _xavier(ks[7], (O, I)), 'uo': _xavier(ks[8], (O, M)), 'bo': jnp.zeros((O,), jnp.float32), 'in_c': jnp.zeros((M,), jnp.float32)}
    _L0_ffn_all = _L0_ffn_setup()
    _L0_ffn_in = {k: v for k, v in _L0_ffn_all.items() if k in ('wf', 'uf', 'bf', 'wi', 'ui', 'bi', 'wc', 'uc', 'bc', 'wo', 'uo', 'bo', 'in_c')}
    del _L0_ffn_all

    def _L1_attn_setup():
        import jax, jax.numpy as jnp
        import numpy as np
        D_MODEL = 128
        N_HEADS = 16

        def get_freqs(seq, n_dim):
            inv = 1.0 / 10000.0 ** (jnp.arange(0, n_dim, 2, dtype=jnp.float32) / n_dim)
            pos = jnp.arange(seq, dtype=jnp.float32)
            return pos[:, None] * inv[None, :]

        def rope(x, freq):
            xf = x.astype(jnp.float32)
            x1 = xf[..., 0::2]
            x2 = xf[..., 1::2]
            cos = jnp.cos(freq)[None, :, None, :]
            sin = jnp.sin(freq)[None, :, None, :]
            r1 = x1 * cos - x2 * sin
            r2 = x1 * sin + x2 * cos
            out = jnp.stack([r1, r2], axis=-1).reshape(x.shape)
            return out.astype(x.dtype)
        key = jax.random.key(seed)
        k1, k2, k3, k4, k5 = jax.random.split(key, 5)
        batch, seq = (2, 256)
        x = jax.random.normal(k1, (batch, seq, D_MODEL), dtype=jnp.float16)
        scale = jnp.float16(0.02)
        qw = jax.random.normal(k2, (D_MODEL, D_MODEL), dtype=jnp.float16) * scale
        kw = jax.random.normal(k3, (D_MODEL, D_MODEL), dtype=jnp.float16) * scale
        vw = jax.random.normal(k4, (D_MODEL, D_MODEL), dtype=jnp.float16) * scale
        ow = jax.random.normal(k5, (D_MODEL, D_MODEL), dtype=jnp.float16) * scale
        return {'x': x, 'qw': qw, 'kw': kw, 'vw': vw, 'ow': ow}
    _L1_attn_all = _L1_attn_setup()
    _L1_attn_in = {k: v for k, v in _L1_attn_all.items() if k in ('qw', 'kw', 'vw', 'ow')}
    del _L1_attn_all

    def _L1_xattn_setup():
        import jax, jax.numpy as jnp
        import numpy as np
        import math
        D_MODEL = 128
        N_HEADS = 16
        C = 1
        B, L = (8, 256)

        def _glorot(key, fan):
            lim = np.sqrt(6.0 / (fan + fan)).astype(np.float32)
            return jax.random.uniform(key, (fan, fan), jnp.float32, -lim, lim)
        key = jax.random.key(seed)
        ks = jax.random.split(key, 7)
        queries = jax.random.normal(ks[0], (B, L, D_MODEL), jnp.float32)
        keys = jax.random.normal(ks[1], (B, L, D_MODEL), jnp.float32)
        values = jax.random.normal(ks[2], (B, L, D_MODEL), jnp.float32)
        wq = _glorot(ks[3], D_MODEL)
        wk = _glorot(ks[4], D_MODEL)
        wv = _glorot(ks[5], D_MODEL)
        wo = _glorot(ks[6], D_MODEL)
        return {'queries': queries, 'keys': keys, 'values': values, 'wq': wq, 'wk': wk, 'wv': wv, 'wo': wo}
    _L1_xattn_all = _L1_xattn_setup()
    _L1_xattn_in = {k: v for k, v in _L1_xattn_all.items() if k in ('wq', 'wk', 'wv', 'wo')}
    del _L1_xattn_all

    def _L1_ffn_setup():
        import jax, jax.numpy as jnp
        import numpy as np
        B, S, D, H, E, K = (2, 128, 128, 64, 16, 4)
        HS = 2 * H

        def silu(z):
            return z * jax.nn.sigmoid(z)
        key = jax.random.key(seed)
        ks = jax.random.split(key, 8)
        sc = lambda fan_in: 1.0 / np.sqrt(fan_in)
        x = jax.random.normal(ks[0], (B, S, D), jnp.float32)
        gate_w = jax.random.normal(ks[1], (E, D), jnp.float32) * sc(D)
        ws_in = jax.random.normal(ks[2], (D, HS), jnp.float32) * sc(D)
        vs_in = jax.random.normal(ks[3], (D, HS), jnp.float32) * sc(D)
        ws_out = jax.random.normal(ks[4], (HS, D), jnp.float32) * sc(HS)
        e_win = jax.random.normal(ks[5], (E, D, H), jnp.float32) * sc(D)
        e_vin = jax.random.normal(ks[6], (E, D, H), jnp.float32) * sc(D)
        e_wout = jax.random.normal(ks[7], (E, H, D), jnp.float32) * sc(H)
        return {'x': x, 'gate_w': gate_w, 'ws_in': ws_in, 'vs_in': vs_in, 'ws_out': ws_out, 'e_win': e_win, 'e_vin': e_vin, 'e_wout': e_wout}
    _L1_ffn_all = _L1_ffn_setup()
    _L1_ffn_in = {k: v for k, v in _L1_ffn_all.items() if k in ('gate_w', 'ws_in', 'vs_in', 'ws_out', 'e_win', 'e_vin', 'e_wout')}
    del _L1_ffn_all
    return {'x': x, 'ctx_1024': ctx_1024, 'mask_BxS2_bk0': mask_BxS2_bk0, 'L0_attn_in_proj_w': _L0_attn_in['in_proj_w'], 'L0_attn_conv_w': _L0_attn_in['conv_w'], 'L0_attn_conv_b': _L0_attn_in['conv_b'], 'L0_attn_dt_bias': _L0_attn_in['dt_bias'], 'L0_attn_A_log': _L0_attn_in['A_log'], 'L0_attn_D': _L0_attn_in['D'], 'L0_attn_norm_w': _L0_attn_in['norm_w'], 'L0_attn_out_proj_w': _L0_attn_in['out_proj_w'], 'L0_xattn_ln_x_w': _L0_xattn_in['ln_x_w'], 'L0_xattn_ln_x_b': _L0_xattn_in['ln_x_b'], 'L0_xattn_ln_l_w': _L0_xattn_in['ln_l_w'], 'L0_xattn_ln_l_b': _L0_xattn_in['ln_l_b'], 'L0_xattn_Wq': _L0_xattn_in['Wq'], 'L0_xattn_Wkv': _L0_xattn_in['Wkv'], 'L0_xattn_q_scale': _L0_xattn_in['q_scale'], 'L0_xattn_k_scale': _L0_xattn_in['k_scale'], 'L0_xattn_Wo': _L0_xattn_in['Wo'], 'L0_xattn_ln_o_w': _L0_xattn_in['ln_o_w'], 'L0_xattn_ln_o_b': _L0_xattn_in['ln_o_b'], 'L0_ffn_wf': _L0_ffn_in['wf'], 'L0_ffn_uf': _L0_ffn_in['uf'], 'L0_ffn_bf': _L0_ffn_in['bf'], 'L0_ffn_wi': _L0_ffn_in['wi'], 'L0_ffn_ui': _L0_ffn_in['ui'], 'L0_ffn_bi': _L0_ffn_in['bi'], 'L0_ffn_wc': _L0_ffn_in['wc'], 'L0_ffn_uc': _L0_ffn_in['uc'], 'L0_ffn_bc': _L0_ffn_in['bc'], 'L0_ffn_wo': _L0_ffn_in['wo'], 'L0_ffn_uo': _L0_ffn_in['uo'], 'L0_ffn_bo': _L0_ffn_in['bo'], 'L0_ffn_in_c': _L0_ffn_in['in_c'], 'L1_attn_qw': _L1_attn_in['qw'], 'L1_attn_kw': _L1_attn_in['kw'], 'L1_attn_vw': _L1_attn_in['vw'], 'L1_attn_ow': _L1_attn_in['ow'], 'L1_xattn_wq': _L1_xattn_in['wq'], 'L1_xattn_wk': _L1_xattn_in['wk'], 'L1_xattn_wv': _L1_xattn_in['wv'], 'L1_xattn_wo': _L1_xattn_in['wo'], 'L1_ffn_gate_w': _L1_ffn_in['gate_w'], 'L1_ffn_ws_in': _L1_ffn_in['ws_in'], 'L1_ffn_vs_in': _L1_ffn_in['vs_in'], 'L1_ffn_ws_out': _L1_ffn_in['ws_out'], 'L1_ffn_e_win': _L1_ffn_in['e_win'], 'L1_ffn_e_vin': _L1_ffn_in['e_vin'], 'L1_ffn_e_wout': _L1_ffn_in['e_wout']}

def reference(x, ctx_1024, mask_BxS2_bk0, L0_attn_in_proj_w, L0_attn_conv_w, L0_attn_conv_b, L0_attn_dt_bias, L0_attn_A_log, L0_attn_D, L0_attn_norm_w, L0_attn_out_proj_w, L0_xattn_ln_x_w, L0_xattn_ln_x_b, L0_xattn_ln_l_w, L0_xattn_ln_l_b, L0_xattn_Wq, L0_xattn_Wkv, L0_xattn_q_scale, L0_xattn_k_scale, L0_xattn_Wo, L0_xattn_ln_o_w, L0_xattn_ln_o_b, L0_ffn_wf, L0_ffn_uf, L0_ffn_bf, L0_ffn_wi, L0_ffn_ui, L0_ffn_bi, L0_ffn_wc, L0_ffn_uc, L0_ffn_bc, L0_ffn_wo, L0_ffn_uo, L0_ffn_bo, L0_ffn_in_c, L1_attn_qw, L1_attn_kw, L1_attn_vw, L1_attn_ow, L1_xattn_wq, L1_xattn_wk, L1_xattn_wv, L1_xattn_wo, L1_ffn_gate_w, L1_ffn_ws_in, L1_ffn_vs_in, L1_ffn_ws_out, L1_ffn_e_win, L1_ffn_e_vin, L1_ffn_e_wout):
    import jax
    import jax.numpy as jnp

    def _L0_attn_ref(u, in_proj_w, conv_w, conv_b, dt_bias, A_log, D, norm_w, out_proj_w):
        import jax, jax.numpy as jnp
        import numpy as np
        D_MODEL = 128
        D_STATE = 128
        D_CONV = 4
        EXPAND = 2
        HEADDIM = 64
        CHUNK = 64
        D_INNER = EXPAND * D_MODEL
        NHEADS = D_INNER // HEADDIM
        D_IN_PROJ = 2 * D_INNER + 2 * D_STATE + NHEADS
        CONV_DIM = D_INNER + 2 * D_STATE
        B_SZ, L_SEQ = (2, 512)

        def _silu(v):
            return v * jax.nn.sigmoid(v)

        def _segsum(x):
            T = x.shape[-1]
            xr = jnp.broadcast_to(x[..., :, None], x.shape + (T,))
            m_strict = jnp.tril(jnp.ones((T, T), bool), -1)
            xs = jnp.cumsum(jnp.where(m_strict, xr, 0.0), axis=-2)
            m_incl = jnp.tril(jnp.ones((T, T), bool))
            return jnp.where(m_incl, xs, -jnp.inf)

        def _ssd(x, A, Bm, Cm):
            b, l, h, p = x.shape
            c = l // CHUNK
            x = x.reshape(b, c, CHUNK, h, p)
            Bm = Bm.reshape(b, c, CHUNK, D_STATE)
            Cm = Cm.reshape(b, c, CHUNK, D_STATE)
            A = A.reshape(b, c, CHUNK, h).transpose(0, 3, 1, 2)
            A_cumsum = jnp.cumsum(A, axis=-1)
            L = jnp.exp(_segsum(A))
            Y_diag = jnp.einsum('bcln,bcsn,bhcls,bcshp->bclhp', Cm, Bm, L, x)
            decay_states = jnp.exp(A_cumsum[..., -1:] - A_cumsum)
            states = jnp.einsum('bcln,bhcl,bclhp->bchpn', Bm, decay_states, x)
            states = jnp.concatenate([jnp.zeros_like(states[:, :1]), states], axis=1)
            pad_last = jnp.pad(A_cumsum[..., -1], ((0, 0), (0, 0), (1, 0)))
            decay_chunk = jnp.exp(_segsum(pad_last))
            new_states = jnp.einsum('bhzc,bchpn->bzhpn', decay_chunk, states)
            states = new_states[:, :-1]
            state_decay_out = jnp.exp(A_cumsum)
            Y_off = jnp.einsum('bcln,bchpn,bhcl->bclhp', Cm, states, state_decay_out)
            return (Y_diag + Y_off).reshape(b, l, h, p)
        b, l, _ = u.shape
        zxbcdt = u @ in_proj_w
        z = zxbcdt[..., :D_INNER]
        xBC = zxbcdt[..., D_INNER:D_INNER + CONV_DIM]
        dt = jax.nn.softplus(zxbcdt[..., -NHEADS:] + dt_bias)
        xt = xBC.transpose(0, 2, 1)
        conv = jax.lax.conv_general_dilated(xt, conv_w, (1,), [(D_CONV - 1, 0)], dimension_numbers=('NCH', 'OIH', 'NCH'), feature_group_count=CONV_DIM) + conv_b[None, :, None]
        xBC = _silu(conv.transpose(0, 2, 1))
        x = xBC[..., :D_INNER].reshape(b, l, NHEADS, HEADDIM)
        Bm = xBC[..., D_INNER:D_INNER + D_STATE]
        Cm = xBC[..., D_INNER + D_STATE:]
        A = -jnp.exp(A_log)
        y = _ssd(x * dt[..., None], A * dt, Bm, Cm)
        y = y + x * D[..., None]
        y = y.reshape(b, l, D_INNER)
        y = y * _silu(z)
        y = y * jax.lax.rsqrt(jnp.mean(y * y, axis=-1, keepdims=True) + 1e-05) * norm_w
        return y @ out_proj_w

    def _L0_xattn_ref(x, latents, mask, ln_x_w, ln_x_b, ln_l_w, ln_l_b, Wq, Wkv, q_scale, k_scale, Wo, ln_o_w, ln_o_b):
        import jax, jax.numpy as jnp
        import numpy as np
        DIM, DIM_HEAD, HEADS, SCALE = (128, 64, 8, 8.0)
        INNER = DIM_HEAD * HEADS
        LN_EPS = 1e-05
        L2_EPS = 1e-12

        def layer_norm(x, w, b):
            mu = jnp.mean(x, axis=-1, keepdims=True)
            var = jnp.mean(jnp.square(x - mu), axis=-1, keepdims=True)
            return (x - mu) * jax.lax.rsqrt(var + LN_EPS) * w + b

        def l2norm(t):
            n = jnp.sqrt(jnp.sum(jnp.square(t), axis=-1, keepdims=True))
            return t / jnp.maximum(n, L2_EPS)
        b, n, _ = x.shape
        m = latents.shape[1]
        x = layer_norm(x, ln_x_w, ln_x_b)
        latents = layer_norm(latents, ln_l_w, ln_l_b)
        q = latents @ Wq
        kv_input = jnp.concatenate([x, latents], axis=1)
        kv = kv_input @ Wkv
        k, v = jnp.split(kv, 2, axis=-1)

        def to_heads(t):
            return t.reshape(t.shape[0], t.shape[1], HEADS, DIM_HEAD).transpose(0, 2, 1, 3)
        q, k, v = map(to_heads, (q, k, v))
        q = l2norm(q) * q_scale
        k = l2norm(k) * k_scale
        sim = jnp.einsum('bhid,bhjd->bhij', q, k) * SCALE
        full_mask = jnp.concatenate([mask, jnp.ones((b, m), dtype=bool)], axis=1)[:, None, None, :]
        max_neg = -jnp.finfo(sim.dtype).max
        sim = jnp.where(full_mask, sim, max_neg)
        attn = jax.nn.softmax(sim.astype(jnp.float32), axis=-1).astype(sim.dtype)
        out = jnp.einsum('bhij,bhjd->bhid', attn, v)
        out = out.transpose(0, 2, 1, 3).reshape(b, m, INNER)
        return layer_norm(out @ Wo, ln_o_w, ln_o_b)

    def _L0_ffn_ref(x, wf, uf, bf, wi, ui, bi, wc, uc, bc, wo, uo, bo, in_c):
        import jax, jax.numpy as jnp
        import numpy as np
        from jax import lax
        T, B, I, M, O = (32, 64, 128, 128, 128)

        def _xavier(key, shape):
            fan_out, fan_in = shape
            limit = float(np.sqrt(6.0 / (fan_in + fan_out)))
            return jax.random.uniform(key, shape, jnp.float32, -limit, limit)
        batch = x.shape[1]
        c0 = jnp.broadcast_to(in_c, (batch, in_c.shape[0]))

        def step(c, xt):
            ft = jax.nn.sigmoid(xt @ wf.T + c @ uf.T + bf)
            it = jax.nn.sigmoid(xt @ wi.T + c @ ui.T + bi)
            gt = jnp.tanh(xt @ wc.T + c @ uc.T + bc)
            c = ft * c + it * gt
            return (c, None)
        c_final, _ = lax.scan(step, c0, x)
        h = jnp.tanh(jnp.einsum('tbi,oi->tbo', x, wo) + c_final @ uo.T + bo)
        return h

    def _L1_attn_ref(x, qw, kw, vw, ow):
        import jax, jax.numpy as jnp
        import numpy as np
        D_MODEL = 128
        N_HEADS = 16

        def get_freqs(seq, n_dim):
            inv = 1.0 / 10000.0 ** (jnp.arange(0, n_dim, 2, dtype=jnp.float32) / n_dim)
            pos = jnp.arange(seq, dtype=jnp.float32)
            return pos[:, None] * inv[None, :]

        def rope(x, freq):
            xf = x.astype(jnp.float32)
            x1 = xf[..., 0::2]
            x2 = xf[..., 1::2]
            cos = jnp.cos(freq)[None, :, None, :]
            sin = jnp.sin(freq)[None, :, None, :]
            r1 = x1 * cos - x2 * sin
            r2 = x1 * sin + x2 * cos
            out = jnp.stack([r1, r2], axis=-1).reshape(x.shape)
            return out.astype(x.dtype)
        batch, seq, dim = x.shape
        n_heads = N_HEADS
        n_dim = dim // n_heads
        Q = (x @ qw).reshape(batch, seq, n_heads, n_dim)
        K = (x @ kw).reshape(batch, seq, n_heads, n_dim)
        V = (x @ vw).reshape(batch, seq, n_heads, n_dim)
        freq = get_freqs(seq, n_dim)
        Q = rope(Q, freq)
        K = rope(K, freq)
        Q = jnp.transpose(Q, (0, 2, 1, 3))
        K = jnp.transpose(K, (0, 2, 1, 3))
        V = jnp.transpose(V, (0, 2, 1, 3))
        score = Q @ jnp.swapaxes(K, -1, -2) / jnp.sqrt(jnp.float16(dim))
        score = score.astype(jnp.float32)
        mask = jnp.tril(jnp.ones((1, 1, seq, seq), dtype=jnp.float32))
        score = score - 10000000000.0 * (1.0 - mask)
        weights = jax.nn.softmax(score, axis=-1)
        attn = weights @ V.astype(jnp.float32)
        merged = jnp.transpose(attn, (0, 2, 1, 3)).reshape(batch, seq, dim)
        out = merged @ ow.astype(jnp.float32)
        return out

    def _L1_xattn_ref(queries, keys, values, wq, wk, wv, wo):
        import jax, jax.numpy as jnp
        import numpy as np
        import math
        D_MODEL = 128
        N_HEADS = 16
        C = 1
        B, L = (8, 256)

        def _glorot(key, fan):
            lim = np.sqrt(6.0 / (fan + fan)).astype(np.float32)
            return jax.random.uniform(key, (fan, fan), jnp.float32, -lim, lim)
        Bv, Lv, _ = queries.shape
        H = N_HEADS
        Dh = D_MODEL // N_HEADS
        Q = (queries @ wq).reshape(Bv, Lv, H, Dh).transpose(0, 2, 3, 1)
        K = (keys @ wk).reshape(Bv, Lv, H, Dh).transpose(0, 2, 3, 1)
        V = (values @ wv).reshape(Bv, Lv, H, Dh).transpose(0, 2, 3, 1)
        corr = jnp.fft.irfft(jnp.fft.rfft(Q, axis=-1) * jnp.conj(jnp.fft.rfft(K, axis=-1)), n=Lv, axis=-1)
        k_top = int(math.floor(C * math.log(Lv)))
        top_vals, top_idx = jax.lax.top_k(corr, k_top)
        w = jax.nn.softmax(top_vals, axis=-1)
        t = jnp.arange(Dh)
        out = jnp.zeros_like(V)
        for i in range(k_top):
            gather_idx = (t[None, None, :] - top_idx[..., i]) % Dh
            rolled = jnp.take_along_axis(V, gather_idx[..., None], axis=2)
            out = out + w[..., i, None] * rolled
        out = out.transpose(0, 2, 1, 3).reshape(Bv, Lv, D_MODEL)
        return out @ wo

    def _L1_ffn_ref(x, gate_w, ws_in, vs_in, ws_out, e_win, e_vin, e_wout):
        import jax, jax.numpy as jnp
        import numpy as np
        B, S, D, H, E, K = (2, 128, 128, 64, 16, 4)
        HS = 2 * H

        def silu(z):
            return z * jax.nn.sigmoid(z)
        b, s, d = x.shape
        T = b * s
        xf = x.reshape(T, d)
        g = jax.nn.sigmoid(xf @ gate_w.T)
        topv, topi = jax.lax.top_k(g, K)
        wn = topv / jnp.sum(topv, axis=-1, keepdims=True)
        combine = jnp.zeros_like(g).at[jnp.arange(T)[:, None], topi].add(wn)
        hin = jnp.einsum('td,edh->eth', xf, e_win)
        vin = jnp.einsum('td,edh->eth', xf, e_vin)
        h = silu(hin) * vin * combine.T[:, :, None]
        routed = jnp.einsum('eth,ehd->td', h, e_wout)
        shared = silu(xf @ ws_in) * (xf @ vs_in) @ ws_out
        return (shared + routed).reshape(b, s, d)
    x = x + _L0_attn_ref(_layernorm(x, axis=-1), L0_attn_in_proj_w, L0_attn_conv_w, L0_attn_conv_b, L0_attn_dt_bias, L0_attn_A_log, L0_attn_D, L0_attn_norm_w, L0_attn_out_proj_w)
    x = x + _L0_xattn_ref(ctx_1024, _layernorm(x, axis=-1), mask_BxS2_bk0, L0_xattn_ln_x_w, L0_xattn_ln_x_b, L0_xattn_ln_l_w, L0_xattn_ln_l_b, L0_xattn_Wq, L0_xattn_Wkv, L0_xattn_q_scale, L0_xattn_k_scale, L0_xattn_Wo, L0_xattn_ln_o_w, L0_xattn_ln_o_b)
    x = x + _L0_ffn_ref(_layernorm(x, axis=-1), L0_ffn_wf, L0_ffn_uf, L0_ffn_bf, L0_ffn_wi, L0_ffn_ui, L0_ffn_bi, L0_ffn_wc, L0_ffn_uc, L0_ffn_bc, L0_ffn_wo, L0_ffn_uo, L0_ffn_bo, L0_ffn_in_c)
    x = x + _L1_attn_ref(_layernorm(x, axis=-1), L1_attn_qw, L1_attn_kw, L1_attn_vw, L1_attn_ow)
    x = x + _L1_xattn_ref(_layernorm(x, axis=-1), ctx_1024, ctx_1024, L1_xattn_wq, L1_xattn_wk, L1_xattn_wv, L1_xattn_wo)
    x = x + _L1_ffn_ref(_layernorm(x, axis=-1), L1_ffn_gate_w, L1_ffn_ws_in, L1_ffn_vs_in, L1_ffn_ws_out, L1_ffn_e_win, L1_ffn_e_vin, L1_ffn_e_wout)
    return x

_drawn_inputs = setup_inputs


def setup_inputs(seed=0):
    import zlib

    import numpy as np

    out = dict(_drawn_inputs(seed))
    spreads = {'L0_attn_conv_b': (0.0, 0.1),
     'L0_attn_norm_w': (1.0, 0.2),
     'L0_xattn_ln_x_w': (1.0, 0.2),
     'L0_xattn_ln_x_b': (0.0, 0.1),
     'L0_xattn_ln_l_w': (1.0, 0.2),
     'L0_xattn_ln_l_b': (0.0, 0.1),
     'L0_xattn_q_scale': (1.0, 0.2),
     'L0_xattn_k_scale': (1.0, 0.2),
     'L0_xattn_ln_o_w': (1.0, 0.2),
     'L0_xattn_ln_o_b': (0.0, 0.1),
     'L0_ffn_bf': (0.0, 0.35),
     'L0_ffn_bi': (0.0, 0.333),
     'L0_ffn_bc': (0.0, 0.1),
     'L0_ffn_bo': (0.0, 0.1),
     'L0_ffn_in_c': (0.0, 0.1)}
    factors = {'L0_attn_dt_bias': 5.004,
     'L0_attn_A_log': 40.264,
     'L1_attn_qw': 45.25,
     'L1_attn_kw': 37.218}
    for name, (base, spread) in spreads.items():
        noise = np.random.default_rng([zlib.crc32(name.encode()), seed]).standard_normal(out[name].shape)
        drawn = base * np.exp(spread * noise) if base else spread * noise
        out[name] = jnp.asarray(drawn.astype(out[name].dtype))
    for name, factor in factors.items():
        out[name] = (out[name] * factor).astype(out[name].dtype)
    return out
```

```python
from contextlib import ExitStack

import concourse.bass as bass
from concourse import mybir

F32 = mybir.dt.float32
F16 = mybir.dt.float16
BF16 = mybir.dt.bfloat16
U8 = mybir.dt.uint8
U32 = mybir.dt.uint32
I32 = mybir.dt.int32
ALU = mybir.AluOpType
ACT = mybir.ActivationFunctionType
AX = mybir.AxisListType

P = 128
B = 4
S = 256
D = 128
NT = B * S // P
EPS = 1e-5

MH = 4
MC = 4
TAPS = 4
XH = 8
XD = 64
XC = 4
AH = 16
AD = 8
TOPC = 5
E = 16
TOPE = 4
HC = 9
PADE = E + 4

SPEC_M = [("in_w", 772), ("conv_w", 16), ("conv_b", 4), ("dt_bias", 4), ("a_log", 4), ("skip", 2), ("norm_w", 2), ("out_w", 256)]
SPEC_X = [("lnx_w", 1), ("lnx_b", 1), ("lnl_w", 1), ("lnl_b", 1), ("q_scale", 1), ("k_scale", 1), ("wq", 512), ("wkv", 1024), ("wo", 512),
          ("lno_w", 128), ("lno_b", 128), ("q_scale_row", 64), ("k_scale_row", 64)]
SPEC_F = [("wf", 128), ("uf", 128), ("wi", 128), ("ui", 128), ("wc", 128), ("uc", 128), ("wo", 128), ("uo", 128),
          ("bf", 1), ("bi", 1), ("bc", 1), ("bo", 1), ("in_c", 1)]
SPEC_A = [("qw", 128), ("kw", 128), ("vw", 128), ("ow", 128)]
SPEC_C = [("wq", 128), ("wk", 128), ("wv", 128), ("wo", 128)]
SPEC_E = [("gate", 16), ("ws_in", 128), ("vs_in", 128), ("e_win", 1024), ("e_vin", 1024), ("w_out", 1152)]
SPEC_K = [("ident", 128), ("ones", 128), ("tri", 128), ("gmask", 384), ("dft", 768), ("idft", 512), ("keep", 1), ("sixteen", 1),
          ("jmod", 8), ("bd", 128), ("permute", 128)]
SPEC_R = [("cos", 256), ("sin", 256)]
SPEC_H = [("ident", 128), ("selq1", 512), ("selq2", 512), ("selk1", 512), ("selk2", 512)]
SPEC_B = [("ident", 128), ("mask_row", 128), ("mask_col", 128), ("expand", 1024)]


def width(spec):
    return sum(n for _, n in spec)


def columns(tile, spec):
    at, out = 0, {}
    for name, n in spec:
        out[name] = tile[:, at:at + n]
        at += n
    return out


class Uses:

    def __init__(self, first):
        self.first = first
        self.number = {}

    def add(self, key):
        assert key not in self.number, key
        self.number[key] = len(self.number)
        return self.number[key]


def decoder(nc, io):
    ctx = ExitStack()
    with ctx:
        def sb(name, shape, dt=F32):
            return ctx.enter_context(nc.sbuf_tensor(name, shape, dt))[:]

        def sem(name):
            return ctx.enter_context(nc.semaphore(name))

        ps = ctx.enter_context(nc.psum_tensor("ps", [P, 8 * 512], F32))
        for_act, for_vec = Uses(0), Uses(4)

        def pbank(uses, key, n=512):
            b = uses.first + uses.number[key] % 4
            return ps[:, b * 512:b * 512 + n]

        w_m, w_x, w_f = sb("w_m", [P, width(SPEC_M)]), sb("w_x", [P, width(SPEC_X)]), sb("w_f", [P, width(SPEC_F)])
        w_a, w_c, w_k = sb("w_a", [P, width(SPEC_A)], F16), sb("w_c", [P, width(SPEC_C)]), sb("w_k", [P, width(SPEC_K)])
        w_r = sb("w_r", [P, width(SPEC_R)])
        R = columns(w_r, SPEC_R)
        w_h, w_b = sb("w_h", [P, width(SPEC_H)], F16), sb("w_b", [P, width(SPEC_B)], BF16)
        M, X0, F, A1, C1 = columns(w_m, SPEC_M), columns(w_x, SPEC_X), columns(w_f, SPEC_F), columns(w_a, SPEC_A), columns(w_c, SPEC_C)
        K, KH, KB = columns(w_k, SPEC_K), columns(w_h, SPEC_H), columns(w_b, SPEC_B)
        ident = K["ident"]
        mask8, maskf = sb("mask8", [P, NT], U8), sb("maskf", [P, NT])

        x = sb("x", [P, NT, D])
        urow = [sb(f"urow{i}", [P, NT, D]) for i in range(2)]
        uT = [sb(f"uT{i}", [P, B, S]) for i in range(2)]
        cx = sb("cx", [P, NT, D])
        cT = sb("cT", [P, B, S])
        cnT = sb("cnT", [P, B, S])
        stats = sb("stats", [P, 7, NT, 6])
        mv = sb("mv", [P, 7, NT, 2])
        rstd = sb("rstd", [P, 7, NT])
        rtmp = sb("rtmp", [P, 7, NT])
        half = sb("half", [P, 64])

        WA = 20992
        WB = 12288
        regA, regB = sb("regA", [P, WA]), sb("regB", [P, WB])

        class Carve:
            def __init__(self, region, size):
                self.region, self.size, self.at = region, size, 0

            def f32(self, n):
                a = self.region[:, self.at:self.at + n]
                self.at += n
                assert self.at <= self.size, (self.at, self.size)
                return a

            def f16(self, n):
                return self.f32(n // 2).bitcast(F16)

            def bf16(self, n):
                return self.f32(n // 2).bitcast(BF16)

        a = Carve(regA, WA)
        xc = a.f32(MC * 1024).rearrange("p (c t) -> p c t", c=MC)
        zs = a.f32(2 * 1024).rearrange("p (c t) -> p c t", c=2)
        dtx = a.f32(32).rearrange("p (t h) -> p t h", h=MH)
        dta = a.f32(32).rearrange("p (t h) -> p t h", h=MH)
        dte = a.f32(32).rearrange("p (t h) -> p t h", h=MH)
        dtl = a.f32(32).rearrange("p (t h) -> p t h", h=MH)
        dt = a.f32(32).rearrange("p (t h) -> p t h", h=MH)
        ea = a.f32(4)
        da = a.f32(32).rearrange("p (t h) -> p t h", h=MH)
        cum = a.f32(32).rearrange("p (t h) -> p t h", h=MH)
        gm = a.f32(2 * 384).rearrange("p (v n) -> p v n", v=2)
        eL = a.f32(2 * 4 * 384).rearrange("p (v h n) -> p v h n", v=2, h=MH)
        wL = a.f32(2 * 4 * 384).rearrange("p (v h n) -> p v h n", v=2, h=MH)
        xdt = a.f32(NT * 256).rearrange("p (t n) -> p t n", t=NT)
        yg = a.f32(2 * 512).rearrange("p (v c n) -> p v c n", v=2, c=2)
        ysq = a.f32(2 * 512).rearrange("p (v c n) -> p v c n", v=2, c=2)
        msq = a.f32(8)
        rms = a.f32(8)
        ow2 = a.f32(256).rearrange("p (c n) -> p c n", c=2)

        a = Carve(regA, WA)
        pT = a.f32(3 * 1024).rearrange("p (v k q) -> p v k q", v=3, k=4)
        qT = a.f32(XC * 1024).rearrange("p (c t) -> p c t", c=XC)
        klT = a.f32(XC * 1024).rearrange("p (c t) -> p c t", c=XC)
        val = a.f32(NT * XC * 192).rearrange("p (t c n) -> p t c n", t=NT, c=XC)
        den = a.f32(2 * 256).rearrange("p (v n) -> p v n", v=2)
        rec = a.f32(2 * 256).rearrange("p (v n) -> p v n", v=2)
        oT = a.f32(2 * XC * 256).rearrange("p (v c n) -> p v c n", v=2, c=XC)
        on = a.f32(256).rearrange("p (q n) -> p q n", q=2)
        ostat = a.f32(NT * 6).rearrange("p (t n) -> p t n", t=NT)
        omv = a.f32(NT * 2).rearrange("p (t n) -> p t n", t=NT)
        ort = a.f32(2 * NT).rearrange("p (v t) -> p v t", v=2)
        bb = Carve(regB, WB)
        kcT = bb.f32(XC * 1024).rearrange("p (c t) -> p c t", c=XC)
        vac = bb.f32(NT * XC * 192).rearrange("p (t c n) -> p t c n", t=NT, c=XC)
        sqr = bb.f32(2 * 512).rearrange("p (v n) -> p v n", v=2)
        knr = bb.f32(2 * 512).rearrange("p (v n) -> p v n", v=2)
        ssq = sb("ssq", [P, 3, NT, XH])
        rnk = sb("rnk", [P, 3, NT, XH])
        qks = sb("qks", [P, 64])
        shift = sb("shift", [P, 2])

        a = Carve(regA, WA)
        uh = a.f32(4 * 128).rearrange("p (g n) -> p g n", g=4)
        halfb = a.f32(2)
        cell = a.f32(2 * 256).rearrange("p (v n) -> p v n", v=2)
        gat = a.f32(2 * 3 * 256).rearrange("p (v g n) -> p v g n", v=2, g=3)
        mixa = a.f32(256)
        mixb = a.f32(256)
        hT = a.f32(1024).rearrange("p (t n) -> p t n", t=B)

        a = Carve(regA, WA)
        wa32 = a.f32(512)
        wrot = a.f32(256)
        rot = a.f32(2 * 2 * 512).rearrange("p (v s t) -> p v s t", v=2, s=2)
        qh = a.f16(2 * 2 * 1024).rearrange("p (k s t) -> p k s t", k=2, s=2)
        qst = a.f16(2 * 4 * 1024).rearrange("p (v j t) -> p v j t", v=2, j=4)
        kst = a.f16(4 * 1024).rearrange("p (j t) -> p j t", j=4)
        sixteen = a.f32(1)
        mx = a.f32(B * 2 * 16).rearrange("p (b q i j) -> p b q i j", b=B, q=2, i=4)
        mneg = a.f16(2 * 2 * 4 * 128).rearrange("p (v q j c) -> p v q j c", v=2, q=2, j=4)
        pT1 = a.f32(3 * 1536).rearrange("p (v n) -> p v n", v=3)
        oc1 = a.f32(2 * 256).rearrange("p (v n) -> p v n", v=2)
        or1 = a.f32(2 * 256).rearrange("p (v q n) -> p v q n", v=2, q=2)
        rec1 = a.f32(B * 32).rearrange("p (b q h) -> p b q h", b=B, q=2)
        oT1 = a.f32(2 * 256).rearrange("p (v n) -> p v n", v=2)

        a = Carve(regA, WA)
        qr = a.f32(3 * 2 * 512).rearrange("p (k h b n) -> p k h b n", k=3, h=2, b=B)
        vo = a.f32(1024).rearrange("p (b n) -> p b n", b=B)
        sab = a.f32(2 * 512).rearrange("p (f n) -> p f n", f=2)
        pr = a.f32(4 * 512).rearrange("p (f n) -> p f n", f=4)
        prod = a.f32(2 * 512).rearrange("p (f n) -> p f n", f=2)
        top = a.f32(B * 8).rearrange("p (b n) -> p b n", b=B)
        topi = a.f32(B * 8).rearrange("p (b n) -> p b n", b=B).bitcast(U32)
        topf = a.f32(B * 8).rearrange("p (b n) -> p b n", b=B)
        tope = a.f32(B * 8).rearrange("p (b n) -> p b n", b=B)
        ntop = a.f32(B)
        tsum = a.f32(B)
        trec = a.f32(B)
        delta = a.f32(B * 8).rearrange("p (b n) -> p b n", b=B)
        deli = a.f32(B * 8).rearrange("p (b n) -> p b n", b=B).bitcast(U32)
        delm = a.f32(B * 8).rearrange("p (b n) -> p b n", b=B).bitcast(U32)
        delf = a.f32(B * 8).rearrange("p (b n) -> p b n", b=B)
        hit = a.f32(B * 5 * 8).rearrange("p (b k j) -> p b k j", b=B, k=5)
        hitw = a.f32(B * 5 * 8).rearrange("p (b k j) -> p b k j", b=B, k=5)
        roll = a.f32(B * 8).rearrange("p (b j) -> p b j", b=B)
        mbd = a.f32(B * 128).rearrange("p (b h j) -> p b h j", b=B, h=16)
        place = a.f32(B * 512).rearrange("p (b t h r) -> p b t h r", b=B, t=2, h=2)

        a = Carve(regA, WA)
        hid = a.f32(HC * 1024).rearrange("p (c t) -> p c t", c=HC)
        sil = a.f32(2 * 512).rearrange("p (v n) -> p v n", v=2)
        hmul = a.f32(2 * 512).rearrange("p (v n) -> p v n", v=2)
        gex = a.f32(NT * E).rearrange("p (t e) -> p t e", t=NT)
        gde = a.f32(NT * E).rearrange("p (t e) -> p t e", t=NT)
        gpad = a.f32(NT * PADE).rearrange("p (t e) -> p t e", t=NT)
        grep = a.f32(NT * PADE).rearrange("p (t e) -> p t e", t=NT)
        gtop = a.f32(NT * 8).rearrange("p (t e) -> p t e", t=NT)
        gfind = a.f32(NT * 8).rearrange("p (t e) -> p t e", t=NT)
        gsum = a.f32(NT)
        grec = a.f32(NT)
        comb = a.f32(NT * E).rearrange("p (t e) -> p t e", t=NT)
        comr = a.f32(2 * NT * E).rearrange("p (v t e) -> p v t e", v=2, t=NT)
        comb3 = a.bf16(NT * 48).rearrange("p (t s e) -> p t s e", t=NT, s=3)
        combT = a.bf16(1024)
        bb = Carve(regB, WB)
        w_e = bb.f32(width(SPEC_E))
        G = columns(w_e, SPEC_E)
        va1 = bb.f32(NT * AH * 32).rearrange("p (t h n) -> p t h n", t=NT, h=AH)

        names = ["x_in", "m_in", "k_in", "c_in", "xw_in", "f_in", "a_in", "h_in", "r_in", "b_in", "c1_in", "e_in", "mask_in", "stored"]
        x_in, m_in, k_in, c_in, xw_in, f_in, a_in, h_in, r_in, b_in, c1_in, e_in, mask_in, stored = [sem(n) for n in names]
        act_full, act_free, vec_full, vec_free = sem("act_full"), sem("act_free"), sem("vec_full"), sem("vec_free")
        ln_var, ln_rstd, ln_rows, x_ready = sem("ln_var"), sem("ln_rstd"), sem("ln_rows"), sem("x_ready")
        half_set = sem("half_set")
        pool_step = sem("pool_step")
        vec_step = sem("vec_step")
        act_step = sem("act_step")

        block = ctx.enter_context(nc.Block())
        LN = {"mamba": 0, "ctx": 1, "lat": 2, "rec": 3, "attn": 4, "corr": 5, "moe": 6}
        ROW = {0: 0, 1: 1, 2: 0, 3: 1, 4: 0, 5: 1, 6: 0}
        UNITS = [(0, t) for t in range(NT)] + [(s, t) for b in range(B) for s in (1, 2) for t in (2 * b, 2 * b + 1)]
        MORDER = []
        for n, (p, c) in enumerate([(p, c) for p in range(2) for c in (2, 3, 4, 5, 0, 1)]):
            MORDER.append(("in", p, c))
            if n == 5:
                MORDER.append(("cum", 0, 0))
            MORDER.append(("context", n, 0) if n < B else ("value", 0, n - B))
        for b in range(B + 1):
            if b < B:
                MORDER += [("front", b, 0), ("head", 2 * b, 0), ("head", 2 * b + 1, 0), ("decay", b, 0), ("norm", 2 * b, 0), ("norm", 2 * b + 1, 0)]
            if b >= 1:
                MORDER += [("back", b - 1, 0)]
            if b < B:
                MORDER += [("turn", 2 * b, 0), ("turn", 2 * b + 1, 0)]
            if b >= 1:
                MORDER += [("out", b - 1, 0)]

        def prepare(b):
            u = NT + 4 * b
            heads = [[("head", v, 0), ("head", v + 1, 0), ("norm", v, 0), ("norm", v + 1, 0)] for v in (u, u + 2)]
            turns = [[("turn", v, 0), ("turn", v + 1, 0)] for v in (u, u + 2)]
            return [[("latent", b, 0)], heads[0], turns[0] + heads[1], turns[1] + [("value", 1, 2 * b), ("value", 1, 2 * b + 1)]]

        XORDER = [step for lot in prepare(0) for step in lot]
        for n in range(B * XH + 4):
            b, h = n // XH, n % XH
            if n < B * XH:
                XORDER.append(("sim", b, h))
            if 0 <= n - 2 < B * XH:
                XORDER.append(("pv", (n - 2) // XH, (n - 2) % XH))
            if n - 4 >= 0 and (n - 4) % XH == XH - 1:
                XORDER.append(("result", (n - 4) // XH, 0))
            if b + 1 < B and h % 2:
                XORDER += prepare(b + 1)[h // 2]
        AORDER = [("row", 0, i) for i in range(4)] + [("stack", 0, 0)]
        for n in range(4 * B + 4):
            b, i = n // 4, n % 4
            if b + 1 < B:
                AORDER.append(("row", b + 1, i))
            if b < B:
                AORDER.append(("col", b, i))
            if 0 <= n - 1 < 4 * B:
                AORDER.append(("pv", (n - 1) // 4, (n - 1) % 4))
            if 0 <= n - 2 < 4 * B:
                AORDER.append(("back", (n - 2) // 4, (n - 2) % 4))
            if b + 1 < B and i == 3:
                AORDER.append(("stack", b + 1, 0))
            if n >= 4 and i == 2:
                AORDER.append(("turn", b - 1, 0))
            if n >= 4 and i == 3:
                AORDER.append(("out", b - 1, 0))
        EORDER = [("up", 0, 8), ("turn", 0, 0)] + [("up", 0, c) for c in range(8)] + [("up", 1, c) for c in (8, 0, 1, 2)]
        EORDER += [("down", 0, 0), ("down", 0, 1)] + [("up", 1, c) for c in range(3, 8)] + [("down", 1, 2), ("down", 1, 3)]

        da_ready, conv_ready, w_ready, gated, ysq_ready = sem("da_ready"), sem("conv_ready"), sem("w_ready"), sem("gated"), sem("ysq_ready")
        tap_ready = sem("tap_ready")
        dt_abs, dt_log, ea_ready = sem("dt_abs"), sem("dt_log"), sem("ea_ready")
        den_ready, decay_ready, msq_ready, rms_ready = sem("den_ready"), sem("decay_ready"), sem("msq_ready"), sem("rms_ready")
        sq_ready, ssq_ready, rnk_ready = sem("sq_ready"), sem("ssq_ready"), sem("rnk_ready")
        val_ones, vac_mask, shift_ready = sem("val_ones"), sem("vac_mask"), sem("shift_ready")
        ovar_ready, orstd_ready = sem("ovar_ready"), sem("orstd_ready")
        cell_ready, gates_ready, halves_ready = sem("cell_ready"), sem("gates_ready"), sem("halves_ready")
        rope_ready, lead_ready, wa_ready, mneg_zero, mneg_ready, va1_ones = sem("rope_ready"), sem("lead_ready"), sem("wa_ready"), sem("mneg_zero"), sem("mneg_ready"), sem("va1_ones")
        place_zero, prod_ready, mbd_ready, corr_diff, corr_exp = sem("place_zero"), sem("prod_ready"), sem("mbd_ready"), sem("corr_diff"), sem("corr_exp")
        gpad_set, comb_ready = sem("gpad_set"), sem("comb_ready")
        res_ready, rest_ready = sem("res_ready"), sem("rest_ready")

        @block.tensor
        def _(pe):
            def act_bank(key):
                n = for_act.add(key)
                if n >= 4:
                    pe.wait_ge(act_free, n - 3)
                return pbank(for_act, key)

            def vec_bank(key):
                n = for_vec.add(key)
                if n >= 4:
                    pe.wait_ge(vec_free, n - 3)
                return pbank(for_vec, key)

            def act_has(key):
                pe.wait_ge(act_free, for_act.number[key] + 1)

            def vec_has(key):
                pe.wait_ge(vec_free, for_vec.number[key] + 1)

            def rows_turn(k, b):
                pe.wait_ge(ln_rows, 4 * k + b + 1)
                t = act_bank(("uT", k, b))
                for hf in range(2):
                    last = pe.transpose(t[:, hf * P:(hf + 1) * P], urow[ROW[k]][:, 2 * b + hf, :], ident)
                last.then_inc(act_full, 1)

            def values(s, tile):
                if s == 0:
                    act_has(("uT", 1, tile // 2))
                else:
                    vec_has(("uT", 2, tile // 2))
                t = act_bank(("xv", s, tile))
                pe.matmul(t, (cnT, uT[0])[s][:, tile // 2, tile % 2 * P:(tile % 2 + 1) * P], X0["wkv"][:, 512:1024],
                          start=True, stop=True).then_inc(act_full, 1)

            def head_rows(u):
                s, tile = UNITS[u]
                if s == 0:
                    act_has(("uT", 1, tile // 2))
                else:
                    vec_has(("uT", 2, tile // 2))
                t = vec_bank(("kr", u))
                w = X0["wq"] if s == 2 else X0["wkv"][:, 0:512]
                pe.matmul(t, (uT[0] if s else cnT)[:, tile // 2, tile % 2 * P:(tile % 2 + 1) * P], w, start=True, stop=True).then_inc(vec_full, 1)

            def head_turn(u):
                vec_has(("kr", u))
                t = act_bank(("kT", u))
                for c in range(XC):
                    last = pe.transpose(t[:, c * P:(c + 1) * P], knr[:, u % 2, c * P:(c + 1) * P], ident)
                last.then_inc(act_full, 1)

            pe.wait_ge(k_in, 16)
            for b in range(B):
                rows_turn(0, b)
            pe.wait_ge(m_in, 16)
            act_has(("uT", 0, B - 1))
            t = vec_bank("dt")
            for tile in range(NT):
                last = pe.matmul(t[:, tile * MH:(tile + 1) * MH], uT[0][:, tile // 2, tile % 2 * P:(tile % 2 + 1) * P],
                                 M["in_w"][:, 768:772], start=True, stop=True)
            last.then_inc(vec_full, 1)
            for kind, b, c in MORDER:
                if kind == "in":
                    t = vec_bank(("in", b, c)) if c >= 2 else act_bank(("in", b, c))
                    pe.matmul(t, M["in_w"][:, c * P:(c + 1) * P], uT[0][:, 2 * b:2 * b + 2, :], start=True, stop=True)\
                      .then_inc(vec_full if c >= 2 else act_full, 1)
                elif kind == "cum":
                    pe.wait_ge(da_ready, 1)
                    t = vec_bank("cum")[:, 0:NT * MH].rearrange("p (b s h) -> p b s h", b=B, s=2)
                    pe.matmul(t[:, :, 0, :], K["tri"], da[:, 0::2, :], start=True, stop=True)
                    pe.matmul(t[:, :, 1, :], K["tri"], da[:, 1::2, :], start=True, stop=False)
                    pe.matmul(t[:, :, 1, :], K["ones"], da[:, 0::2, :], start=False, stop=True).then_inc(vec_full, 1)
                elif kind == "context":
                    pe.wait_ge(c_in, 16)
                    t = act_bank(("cT", b))
                    for hf in range(2):
                        last = pe.transpose(t[:, hf * P:(hf + 1) * P], cx[:, 2 * b + hf, :], ident)
                    last.then_inc(act_full, 1)
                    rows_turn(1, b)
                elif kind == "value":
                    if c == 0:
                        pe.wait_ge(xw_in, 16)
                    values(0, c)
                elif kind == "head":
                    head_rows(b)
                elif kind == "turn":
                    head_turn(b)
                elif kind == "front":
                    pe.wait_ge(conv_ready, 4 * (b // 2) + 2)
                    t = vec_bank(("xrow", b))
                    for hf in range(2):
                        for c in range(2):
                            at = b * S + hf * P
                            last = pe.transpose(t[:, hf * 256 + c * P:hf * 256 + (c + 1) * P], xc[:, c, at:at + P], ident)
                    last.then_inc(vec_full, 1)
                    pe.wait_ge(conv_ready, 4 * (b // 2) + 4)
                    t = vec_bank(("G", b))
                    pe.matmul(t[:, 0:256], xc[:, 2, b * S:b * S + P], xc[:, 3, b * S:(b + 1) * S], start=True, stop=True)
                    pe.matmul(t[:, 256:384], xc[:, 2, b * S + P:(b + 1) * S], xc[:, 3, b * S + P:(b + 1) * S],
                              start=True, stop=True).then_inc(vec_full, 1)
                    vec_has("cum")
                    for hf in range(2):
                        t = vec_bank(("bc", b, hf))
                        for h in range(MH):
                            last = pe.transpose(t[:, h * P:(h + 1) * P], cum[:, 2 * b + hf, h:h + 1].broadcast_to([P, P]), ident)
                        last.then_inc(vec_full, 1)
                elif kind == "back":
                    pe.wait_ge(w_ready, b + 1)
                    t = vec_bank(("Y", b))
                    for h in range(MH):
                        r, at = h % 2 * 64, h // 2 * 256
                        pe.matmul(t[r:r + 64, at:at + 256], xdt[:, 2 * b, h * 64:(h + 1) * 64], wL[:, b % 2, h, 0:256], start=True, stop=False)
                        last = pe.matmul(t[r:r + 64, at + P:at + 256], xdt[:, 2 * b + 1, h * 64:(h + 1) * 64], wL[:, b % 2, h, 256:384],
                                         start=False, stop=True)
                    last.then_inc(vec_full, 1)
                elif kind == "out":
                    pe.wait_ge(gated, b + 1)
                    t = vec_bank(("out0", b))
                    for hf in range(2):
                        for c in range(2):
                            pe.matmul(t[:, hf * P:(hf + 1) * P], yg[:, b % 2, c, hf * P:(hf + 1) * P], ow2[:, c, :], start=(c == 0), stop=(c == 1))
                    pe.wait_ge(ysq_ready, b + 1)
                    for hf in range(2):
                        for c in range(2):
                            last = pe.matmul(t[:, 256 + hf:257 + hf], ysq[:, b % 2, c, hf * P:(hf + 1) * P], K["ones"][:, 0:1],
                                             start=(c == 0), stop=(c == 1))
                    last.then_inc(vec_full, 1)

            for kind, b, h in XORDER:
                n, c, r = b * XH + h, h // 2, h % 2 * 64
                if kind == "latent":
                    pe.wait_ge(ln_rows, 4 * 2 + b + 1)
                    t = vec_bank(("uT", 2, b))
                    for hf in range(2):
                        last = pe.transpose(t[:, hf * P:(hf + 1) * P], urow[ROW[2]][:, 2 * b + hf, :], ident)
                    last.then_inc(vec_full, 1)
                elif kind == "value":
                    values(1, h)
                elif kind == "head":
                    head_rows(b)
                elif kind == "turn":
                    head_turn(b)
                elif kind == "sim":
                    act_has(("kT", NT + 4 * b + 3))
                    banks = [act_bank(("sim", n, 0)), act_bank(("sim", n, 1))]
                    assert for_act.number[("sim", n, 0)] % 2 == 0
                    for kt in range(4):
                        keys = (kcT if kt < 2 else klT)[r:r + 64, c, b * S + kt % 2 * P:b * S + (kt % 2 + 1) * P]
                        last = pe.matmul(banks[kt // 2][:, kt % 2 * 256:(kt % 2 + 1) * 256], keys, qT[r:r + 64, c, b * S:(b + 1) * S],
                                         start=True, stop=True)
                    last.then_inc(act_full, 2)
                elif kind == "pv":
                    act_has(("sim", n, 1))
                    act_has(("xv", 1, 2 * b + 1))
                    if n == 0:
                        pe.wait_ge(val_ones, 1)
                        pe.wait_ge(vac_mask, 1)
                    t = vec_bank(("pv", n))
                    at = h % 2 * 64
                    for kt in range(4):
                        last = pe.matmul(t[:, 0:256], (vac if kt < 2 else val)[:, 2 * b + kt % 2, c, at:at + P], pT[:, n % 3, kt, :],
                                         start=(kt == 0), stop=(kt == 3))
                    last.then_inc(vec_full, 1)
                elif kind == "result":
                    vec_has(("pv", b * XH + XH - 1))
                    t = vec_bank(("out1", b))
                    for qt in range(2):
                        for c in range(XC):
                            last = pe.matmul(t[:, qt * P:(qt + 1) * P], oT[:, b % 2, c, qt * P:(qt + 1) * P], X0["wo"][:, c * P:(c + 1) * P],
                                             start=(c == 0), stop=(c == XC - 1))
                    last.then_inc(vec_full, 1)

            gate_ps = {}

            def gate_x(t):
                act_has(("uT", 3, t))
                fi, g = act_bank(("fi", t)), act_bank(("g", t))
                gate_ps[t] = (fi[:, 0:256], fi[:, 256:512], g[:, 0:256])
                for n, w, first in ((0, "wf", True), (1, "wi", False), (2, "wc", True)):
                    pe.matmul(gate_ps[t][n], F[w], uT[1][:, t, :], start=first, stop=False, skip_group_check=True)

            pe.wait_ge(f_in, 16)
            for b in range(B):
                rows_turn(3, b)
            gate_x(0)
            for t in range(B):
                if t + 1 < B:
                    gate_x(t + 1)
                pe.wait_ge(cell_ready, t + 1)
                for n in range(3):
                    last = pe.matmul(gate_ps[t][n], uh[:, n, :], cell[:, t % 2, :], start=False, stop=True, skip_group_check=True)
                last.then_inc(act_full, 2)
            pe.wait_ge(cell_ready, B + 1)
            for p in range(2):
                ps_h = act_bank(("h", p))
                for t in range(2):
                    pe.matmul(ps_h[:, t * 256:(t + 1) * 256], F["wo"], uT[1][:, 2 * p + t, :], start=True, stop=False)
                    last = pe.matmul(ps_h[:, t * 256:(t + 1) * 256], uh[:, 3, :], cell[:, 0, :], start=False, stop=True)
                last.then_inc(act_full, 1)
            for b in range(B):
                act_has(("h", b // 2))
                t = vec_bank(("hrow", b))
                for hf in range(2):
                    last = pe.transpose(t[:, hf * P:(hf + 1) * P], hT[:, b, hf * P:(hf + 1) * P], ident)
                last.then_inc(vec_full, 1)

            pe.wait_ge(wa_ready, 1)
            for p in range(2):
                for b in (2 * p, 2 * p + 1):
                    rows_turn(4, b)
                act_has(("uT", 4, 2 * p + 1))
                for k in range(2):
                    for s, w in enumerate((wa32, wrot)):
                        t = vec_bank(("qk", p, k, s))
                        pe.matmul(t, w[:, k * P:(k + 1) * P], uT[0][:, 2 * p:2 * p + 2, :], start=True, stop=True).then_inc(vec_full, 1)
                for b in (2 * p, 2 * p + 1):
                    t = act_bank(("av", b))
                    for hf in range(2):
                        last = pe.matmul(t[:, hf * P:(hf + 1) * P], uT[0][:, b, hf * P:(hf + 1) * P], wa32[:, 256:384], start=True, stop=True)
                    last.then_inc(act_full, 1)
            pe.wait_ge(h_in, 16)
            pe.wait_ge(b_in, 16)
            for p in range(2):
                for k in range(2):
                    pe.wait_ge(lead_ready, 2 * p + k + 1)
                    pe.wait_ge(rest_ready, 2 * p + k + 1)
                    for j in range(4):
                        t = act_bank(("st", p, k, j)) if k == 0 else vec_bank(("st", p, k, j))
                        for s in range(2):
                            sel = KH[("selq1", "selq2", "selk1", "selk2")[2 * k + s]][:, j * P:(j + 1) * P]
                            last = pe.matmul(t, sel, qh[:, k, s, p * 512:(p + 1) * 512], start=(s == 0), stop=(s == 1))
                        last.then_inc(vec_full if k else act_full, 1)

            for kind, b, i in AORDER:
                n, r, at = 4 * b + i, 32 * i, b * S
                if kind == "row":
                    if n % 4 == 0:
                        act_has(("st", b // 2, 0, 3))
                        vec_has(("st", b // 2, 1, 3))
                    mask = KB["mask_row"].unsqueeze(1)
                    t = vec_bank(("row", b, i, 0)).rearrange("p (j k) -> p j k", j=4)
                    pe.matmul(t, KB["ident"], mask.broadcast_to([P, 4, P]), start=True, stop=False, skip_group_check=True)
                    for j in range(4):
                        last = pe.matmul(t[:, j, :], qst[r:r + 32, 0, j, at:at + P], kst[r:r + 32, j, at:at + P],
                                         start=False, stop=True, skip_group_check=True)
                    last.then_inc(vec_full, 1)
                    for jj in range(2):
                        t = vec_bank(("row", b, i, 1 + jj)).rearrange("p (j k) -> p j k", j=2)
                        pe.matmul(t[:, :, P:S], KB["ident"], mask.broadcast_to([P, 2, P]), start=True, stop=False, skip_group_check=True)
                        for j in range(2):
                            last = pe.matmul(t[:, j, :], qst[r:r + 32, 0, 2 * jj + j, at + P:at + S], kst[r:r + 32, 2 * jj + j, at:at + S],
                                             start=False, stop=True, skip_group_check=True)
                        last.then_inc(vec_full, 1)
                elif kind == "stack":
                    pe.wait_ge(mneg_ready, b + 1)
                    for jj in range(2):
                        t = act_bank(("st2", b, jj)).rearrange("p (j q) -> p j q", j=2)
                        for j in (2 * jj, 2 * jj + 1):
                            o = t[:, j % 2, :]
                            pe.matmul(o, KH["selq1"][:, j * P:(j + 1) * P], qh[:, 0, 0, at:at + S], start=True, stop=False, skip_group_check=True)
                            pe.matmul(o, KH["selq2"][:, j * P:(j + 1) * P], qh[:, 0, 1, at:at + S], start=False, stop=False, skip_group_check=True)
                            for qt in range(2):
                                last = pe.matmul(o[:, qt * P:(qt + 1) * P], mneg[:, b % 2, qt, j, :], KH["ident"], start=False, stop=True,
                                                 skip_group_check=True)
                        last.then_inc(act_full, 1)
                elif kind == "col":
                    if i == 0:
                        act_has(("st2", b, 1))
                    mask = KB["mask_col"].unsqueeze(1)
                    for jj in range(2):
                        t = act_bank(("col", b, i, jj)).rearrange("p (j q) -> p j q", j=2)
                        pe.matmul(t[:, :, 0:P], KB["ident"], mask.broadcast_to([P, 2, P]), start=True, stop=False, skip_group_check=True)
                        for j in range(2):
                            last = pe.matmul(t[:, j, :], kst[r:r + 32, 2 * jj + j, at:at + P], qst[r:r + 32, 1, 2 * jj + j, at:at + S],
                                             start=False, stop=True, skip_group_check=True)
                        last.then_inc(act_full, 1)
                    t = act_bank(("col", b, i, 2)).rearrange("p (j q) -> p j q", j=4)
                    pe.matmul(t, KB["ident"], mask.broadcast_to([P, 4, P]), start=True, stop=False, skip_group_check=True)
                    for j in range(4):
                        last = pe.matmul(t[:, j, :], kst[r:r + 32, j, at + P:at + S], qst[r:r + 32, 1, j, at + P:at + S],
                                         start=False, stop=True, skip_group_check=True)
                    last.then_inc(act_full, 1)
                elif kind == "pv":
                    act_has(("col", b, i, 2))
                    if n == 0:
                        pe.wait_ge(va1_ones, 1)
                    t = act_bank(("apv", b, i))
                    for j in range(4):
                        o, h, prob = t[32 * j:32 * j + 32, 0:S], 4 * j + i, pT1[:, n % 3, :]
                        pe.matmul(o, va1[:, 2 * b, h, :], prob[:, j * S:(j + 1) * S], start=True, stop=False)
                        last = pe.matmul(o[:, P:S], va1[:, 2 * b + 1, h, :], prob[:, 1024 + j * P:1024 + (j + 1) * P], start=False, stop=True)
                    last.then_inc(act_full, 1)
                elif kind == "back":
                    act_has(("apv", b, i))
                    t = vec_bank(("aback", b, i))
                    for qt in range(2):
                        last = pe.transpose(t[:, qt * P:(qt + 1) * P], oc1[:, n % 2, qt * P:(qt + 1) * P], ident)
                    last.then_inc(vec_full, 1)
                elif kind == "turn":
                    vec_has(("aback", b, 3))
                    t = act_bank(("oT1", b))
                    for qt in range(2):
                        last = pe.transpose(t[:, qt * P:(qt + 1) * P], or1[:, b % 2, qt, :], ident)
                    last.then_inc(act_full, 1)
                else:
                    act_has(("oT1", b))
                    t = vec_bank(("out4", b))
                    for qt in range(2):
                        last = pe.matmul(t[:, qt * P:(qt + 1) * P], oT1[:, b % 2, qt * P:(qt + 1) * P], wa32[:, 384:512], start=True, stop=True)
                    last.then_inc(vec_full, 1)

            pe.wait_ge(c1_in, 16)

            def corr_rows(k, b):
                t = act_bank(("cr", k, b))
                for hf in range(2):
                    src = (uT[1] if k == 0 else cT)[:, b, hf * P:(hf + 1) * P]
                    last = pe.matmul(t[:, hf * P:(hf + 1) * P], src, C1[("wq", "wk", "wv")[k]], start=True, stop=True)
                last.then_inc(act_full, 1)

            def spectrum(k, f):
                t = act_bank(("fk", f)) if k else vec_bank(("fq", f))
                for hf in range(2):
                    at = hf * 384 + f * P
                    last = pe.matmul(t, K["dft"][:, at:at + P], qr[:, k, hf, :, :], start=(hf == 0), stop=(hf == 1))
                last.then_inc(act_full if k else vec_full, 1)

            for k in (1, 2):
                for b in range(B):
                    corr_rows(k, b)
            act_has(("cr", 2, B - 1))
            for bp in range(2):
                t = act_bank(("vo", bp))
                for b in range(2):
                    for hf in range(2):
                        at = (2 * b + hf) * P
                        last = pe.matmul(t[:, at:at + P], qr[:, 2, hf, 2 * bp + b, :], C1["wo"], start=True, stop=True)
                last.then_inc(act_full, 1)
            for f in range(3):
                spectrum(1, f)
            for b in range(B):
                rows_turn(5, b)
            for b in range(B):
                act_has(("uT", 5, b))
                corr_rows(0, b)
            act_has(("cr", 0, B - 1))
            for f in range(2):
                spectrum(0, f)
            for bp in range(2):
                t = vec_bank(("corr", bp))
                pe.wait_ge(prod_ready, 1)
                for b in range(2):
                    at = (2 * bp + b) * P
                    pe.matmul(t[:, b * S:(b + 1) * S], prod[:, 0, at:at + P], K["idft"][:, 0:S], start=True, stop=False)
                    last = pe.matmul(t[:, b * S:(b + 1) * S], prod[:, 1, at:at + P], K["idft"][:, S:2 * S], start=False, stop=True)
                last.then_inc(vec_full, 1)
            pe.wait_ge(mbd_ready, 1)
            t = act_bank("mix")
            for b in range(B):
                last = pe.matmul(t[:, b * P:(b + 1) * P], mbd[:, b, :, :].rearrange("p h j -> p (h j)"), K["permute"], start=True, stop=True)
            last.then_inc(act_full, 1)
            act_has("mix")
            for b in range(B):
                t = vec_bank(("out5", b))
                for tile in range(2):
                    for hf in range(2):
                        last = pe.matmul(t[:, tile * P:(tile + 1) * P], place[:, b, tile, hf, :], vo[:, b, hf * P:(hf + 1) * P],
                                         start=(hf == 0), stop=(hf == 1))
                last.then_inc(vec_full, 1)

            pe.wait_ge(e_in, 16)
            for b in range(B):
                rows_turn(6, b)
            act_has(("uT", 6, B - 1))
            t = act_bank("gl")
            for tile in range(NT):
                last = pe.matmul(t[:, tile * E:(tile + 1) * E], uT[0][:, tile // 2, tile % 2 * P:(tile % 2 + 1) * P], G["gate"], start=True, stop=True)
            last.then_inc(act_full, 1)
            for kind, p, c in EORDER:
                if kind == "turn":
                    pe.wait_ge(comb_ready, 1)
                    t = vec_bank("cbT").bitcast(BF16)
                    for tile in range(NT):
                        last = pe.transpose(t[0:48, tile * P:(tile + 1) * P], comb3[:, tile, :, :].rearrange("p s e -> p (s e)"), KB["ident"])
                    last.then_inc(vec_full, 1)
                elif kind == "up":
                    w1, w3 = (G["e_win"][:, c * P:(c + 1) * P], G["e_vin"][:, c * P:(c + 1) * P]) if c < 8 else (G["ws_in"], G["vs_in"])
                    t = act_bank(("hin", p, c))
                    pe.matmul(t, w1, uT[0][:, 2 * p:2 * p + 2, :], start=True, stop=True).then_inc(act_full, 1)
                    t = vec_bank(("vin", p, c))
                    pe.matmul(t, w3, uT[0][:, 2 * p:2 * p + 2, :], start=True, stop=True).then_inc(vec_full, 1)
                    if c < 8:
                        vec_has("cbT")
                        t = vec_bank(("cw", p, c))
                        pe.matmul(t, KB["expand"][0:48, c * P:(c + 1) * P], combT[0:48, p * 512:(p + 1) * 512], start=True, stop=True)\
                          .then_inc(vec_full, 1)
                else:
                    b = c
                    vec_has(("cw", b // 2, 7))
                    t = vec_bank(("out6", b))
                    for hf in range(2):
                        at = b * S + hf * P
                        for c in range(HC):
                            last = pe.matmul(t[:, hf * P:(hf + 1) * P], hid[:, c, at:at + P], G["w_out"][:, c * P:(c + 1) * P],
                                             start=(c == 0), stop=(c == HC - 1))
                    last.then_inc(vec_full, 1)

        @block.scalar
        def _(act):
            steps = 0

            def after(ins):
                nonlocal steps
                steps += 1
                ins.then_inc(act_step, 1)
                act.wait_ge(act_step, steps)

            def full(key):
                act.wait_ge(act_full, for_act.number[key] + 1)

            def vec_bank_full(key):
                act.wait_ge(vec_full, for_vec.number[key] + 1)

            def vec_bank_read(key):
                act.wait_ge(vec_free, for_vec.number[key] + 1)

            def copy_out(key, dst, src, scale=1.0):
                full(key)
                act.activation(dst, src, ACT.Copy, scale=scale).then_inc(act_free, 1)

            def copy_uT(k, b):
                copy_out(("uT", k, b), uT[ROW[k]][:, b, :], pbank(for_act, ("uT", k, b), S))

            def values(s, tile):
                key = ("xv", s, tile)
                full(key)
                dst = (vac, val)[s][:, tile, :, :].rearrange("p c (s d) -> p c s d", s=3)[:, :, 0::2, :]
                act.activation(dst, pbank(for_act, key).rearrange("p (c s d) -> p c s d", c=XC, s=2), ACT.Copy,
                               scale=maskf[:, tile:tile + 1] if s == 0 else 1.0).then_inc(act_free, 1)

            def head_square(u):
                vec_bank_full(("kr", u))
                if u >= 2:
                    act.wait_ge(ssq_ready, u - 1)
                act.activation(sqr[:, u % 2, :], pbank(for_vec, ("kr", u)), ACT.Square).then_inc(sq_ready, 1)

            def head_scale(u):
                s, tile = UNITS[u]
                full(("kT", u))
                dst = (kcT, klT, qT)[s][:, :, tile * P:(tile + 1) * P]
                act.activation(dst, pbank(for_act, ("kT", u)).rearrange("p (c t) -> p c t", c=XC), ACT.Copy,
                               scale=X0["q_scale"] if s == 2 else X0["k_scale"]).then_inc(act_free, 1)

            for b in range(B):
                copy_uT(0, b)
            act.wait_ge(m_in, 16)
            act.activation(ea, M["a_log"], ACT.Exp).then_inc(ea_ready, 1)
            act.wait_ge(dt_abs, 1)
            after(act.activation(dte, dta, ACT.Exp, scale=-1.0))
            act.activation(dtl, dte, ACT.Ln, bias=1.0).then_inc(dt_log, 1)

            waiting = []

            def conv_silu():
                p, c = waiting.pop(0)
                vec_bank_read(("in", p, c))
                o = xc[:, c - 2, p * 512:(p + 1) * 512]
                act.activation(o, o, ACT.Silu).then_inc(conv_ready, 1)

            for kind, b, c in MORDER:
                if kind == "in" and c >= 2:
                    key, k = ("in", b, c), c - 2
                    vec_bank_full(key)
                    act.activation(xc[:, k, b * 512:(b + 1) * 512], pbank(for_vec, key), ACT.Identity, bias=M["conv_b"][:, k:k + 1],
                                   scale=M["conv_w"][:, 4 * k + 3:4 * k + 4]).then_inc(tap_ready, 1)
                    waiting.append((b, c))
                    if len(waiting) > 2:
                        conv_silu()
                elif kind == "in":
                    full(("in", b, c))
                    act.activation(zs[:, c, b * 512:(b + 1) * 512], pbank(for_act, ("in", b, c)), ACT.Silu).then_inc(act_free, 1)
                    if waiting:
                        conv_silu()
                elif kind == "context":
                    copy_out(("cT", b), cT[:, b, :], pbank(for_act, ("cT", b), S))
                    act.wait_ge(xw_in, 16)
                    full(("uT", 1, b))
                    act.activation(cnT[:, b, :], pbank(for_act, ("uT", 1, b), S), ACT.Identity, bias=X0["lnx_b"], scale=X0["lnx_w"])\
                       .then_inc(act_free, 1)
                elif kind == "value":
                    if c == 0:
                        act.wait_ge(vac_mask, 1)
                    values(0, c)
                elif kind == "head":
                    head_square(b)
                elif kind == "turn":
                    head_scale(b)
                elif kind == "front":
                    vec_bank_read(("bc", b, 1))
                    act.activation(eL[:, b % 2, :, :], eL[:, b % 2, :, :], ACT.Exp).then_inc(decay_ready, 1)
                elif kind == "back":
                    act.wait_ge(gated, b + 1)
                    if b >= 2:
                        vec_bank_full(("out0", b - 2))
                    act.activation(ysq[:, b % 2, :, :], yg[:, b % 2, :, :], ACT.Square).then_inc(ysq_ready, 1)

            for kind, b, h in XORDER:
                n = b * XH + h
                if kind == "value":
                    values(1, h)
                elif kind == "head":
                    head_square(b)
                elif kind == "turn":
                    head_scale(b)
                elif kind == "sim":
                    if n == 0:
                        act.wait_ge(shift_ready, 1)
                    act.wait_ge(act_full, for_act.number[("sim", n, 1)] + 1)
                    if n >= 3:
                        vec_bank_full(("pv", n - 3))
                    act.activation(pT[:, n % 3, :, :], pbank(for_act, ("sim", n, 0), 1024).rearrange("p (k q) -> p k q", k=4), ACT.Exp,
                                   bias=shift[:, 1:2], scale=8.0).then_inc(act_free, 2)
                elif kind == "pv":
                    vec_bank_full(("pv", n))
                    if n >= 4:
                        vec_bank_read(("pv", n - 4 | 1))
                    r = h % 2 * 64
                    act.activation(den[r:r + 64, n // 2 % 2, :], pbank(for_vec, ("pv", n), S)[64 - r:128 - r, :], ACT.Copy).then_inc(den_ready, 1)

            for b in range(B):
                copy_uT(3, b)
            act.wait_ge(halves_ready, 1)
            for t in range(B):
                full(("g", t))
                if t >= 2:
                    act.wait_ge(cell_ready, t)
                fi = pbank(for_act, ("fi", t))
                act.activation(gat[:, t % 2, 0, :], fi[:, 0:256], ACT.Tanh, bias=halfb[:, 0:1], scale=0.5)
                act.activation(gat[:, t % 2, 1, :], fi[:, 256:512], ACT.Tanh, bias=halfb[:, 1:2], scale=0.5).then_inc(act_free, 1)
                act.activation(gat[:, t % 2, 2, :], pbank(for_act, ("g", t), 256), ACT.Tanh, bias=F["bc"]).then_inc(act_free, 1)
            for p in range(2):
                full(("h", p))
                act.activation(hT[:, 2 * p:2 * p + 2, :], pbank(for_act, ("h", p)).rearrange("p (t n) -> p t n", t=2), ACT.Tanh,
                               bias=F["bo"]).then_inc(act_free, 1)

            for p in range(2):
                for b in (2 * p, 2 * p + 1):
                    copy_uT(4, b)
                for b in (2 * p, 2 * p + 1):
                    copy_out(("av", b), va1[:, 2 * b:2 * b + 2, :, 0:AD], pbank(for_act, ("av", b), 256).rearrange("p (t h d) -> p t h d", t=2, h=AH))
                for k in range(2):
                    act.wait_ge(rope_ready, 2 * p + k + 1)
                    act.activation(qh[:, k, 0, p * 512:(p + 1) * 512], rot[:, k, 0, :], ACT.Copy).then_inc(lead_ready, 1)
            for p in range(2):
                for j in range(4):
                    copy_out(("st", p, 0, j), qst[:, 0, j, p * 512:(p + 1) * 512], pbank(for_act, ("st", p, 0, j)))
            for kind, b, i in AORDER:
                n = 4 * b + i
                if kind == "stack":
                    for jj in range(2):
                        copy_out(("st2", b, jj), qst[:, 1, 2 * jj:2 * jj + 2, b * S:(b + 1) * S],
                                 pbank(for_act, ("st2", b, jj)).rearrange("p (j q) -> p j q", j=2))
                elif kind == "col":
                    for part in range(3):
                        key = ("col", b, i, part)
                        full(key)
                        act.activation(pT1[:, n % 3, part * 512:(part + 1) * 512], pbank(for_act, key), ACT.Exp, scale=1.0 / 11.3125)\
                           .then_inc(act_free, 1)
                elif kind == "pv":
                    if n >= 2:
                        vec_bank_full(("aback", (n - 2) // 4, (n - 2) % 4))
                    copy_out(("apv", b, i), oc1[:, n % 2, :], pbank(for_act, ("apv", b, i), 256))
                elif kind == "turn":
                    if b >= 2:
                        vec_bank_full(("out4", b - 2))
                    copy_out(("oT1", b), oT1[:, b % 2, :], pbank(for_act, ("oT1", b), 256))

            def corr_rows(k, b):
                copy_out(("cr", k, b), qr[:, k, :, b, :], pbank(for_act, ("cr", k, b), 256).rearrange("p (h n) -> p h n", h=2))

            for k in (1, 2):
                for b in range(B):
                    corr_rows(k, b)
            for bp in range(2):
                copy_out(("vo", bp), vo[:, 2 * bp:2 * bp + 2, :], pbank(for_act, ("vo", bp)).rearrange("p (b n) -> p b n", b=2))
            for f in range(3):
                copy_out(("fk", f), pr[:, f, :], pbank(for_act, ("fk", f)))
            for b in range(B):
                copy_uT(5, b)
            for b in range(B):
                corr_rows(0, b)
            act.wait_ge(corr_diff, 1)
            act.activation(tope[:, :, 0:TOPC], delta[:, :, 0:TOPC], ACT.Exp).then_inc(corr_exp, 1)
            full("mix")
            act.wait_ge(place_zero, 1)
            mix = pbank(for_act, "mix").rearrange("p (b t g) -> p b t g", b=B, t=2)
            for hf in range(2):
                last = act.activation(place[:, :, :, hf, hf::2], mix, ACT.Copy)
            last.then_inc(act_free, 1)

            for b in range(B):
                copy_uT(6, b)
            full("gl")
            act.activation(gex, pbank(for_act, "gl", NT * E).rearrange("p (t e) -> p t e", t=NT), ACT.Exp, scale=-1.0).then_inc(act_free, 1)
            used = []
            for kind, p, c in EORDER:
                if kind == "up":
                    key = ("hin", p, c)
                    full(key)
                    if len(used) >= 2:
                        vec_bank_read(used[-2])
                    act.activation(sil[:, len(used) % 2, :], pbank(for_act, key), ACT.Silu).then_inc(act_free, 1)
                    used.append(("cw" if c < 8 else "vin", p, c))

        @block.vector
        def _(vec):
            steps = 0

            def after(ins):
                nonlocal steps
                steps += 1
                ins.then_inc(vec_step, 1)
                vec.wait_ge(vec_step, steps)

            def full(key):
                vec.wait_ge(vec_full, for_vec.number[key] + 1)

            def own(key):
                vec.wait_ge(vec_free, for_vec.number[key] + 1)

            def act_read(key):
                vec.wait_ge(act_free, for_act.number[key] + 1)

            def var(k, b, src):
                vec.bn_stats(stats[:, k, 2 * b, :], src[:, 2 * b, :])
                after(vec.bn_stats(stats[:, k, 2 * b + 1, :], src[:, 2 * b + 1, :]))
                vec.bn_aggr(mv[:, k, 2 * b, :], stats[:, k, 2 * b, :])
                vec.bn_aggr(mv[:, k, 2 * b + 1, :], stats[:, k, 2 * b + 1, :]).then_inc(ln_var, 1)

            def rows(k, b, src):
                vec.wait_ge(ln_rstd, 4 * k + b + 1)
                for t in (2 * b, 2 * b + 1):
                    last = vec.tensor_scalar(urow[ROW[k]][:, t, :], src[:, t, :], mv[:, k, t, 0:1], rstd[:, k, t:t + 1],
                                             ALU.subtract, ALU.mult)
                last.then_inc(ln_rows, 1)

            def residual(key, b):
                full(key)
                xb = x[:, 2 * b:2 * b + 2, :]
                vec.tensor_tensor(xb, xb, pbank(for_vec, key, 256).rearrange("p (t n) -> p t n", t=2), ALU.add).then_inc(vec_free, 1)
                own(key)

            vec.wait_ge(x_in, 16)
            for b in range(B):
                var(0, b, x)
            vec.wait_ge(c_in, 16)
            for b in range(B):
                rows(0, b, x)
            for b in range(B):
                var(1, b, cx)
            vec.wait_ge(m_in, 16)
            full("dt")
            vec.tensor_tensor(dtx, pbank(for_vec, "dt", 32).rearrange("p (t h) -> p t h", h=MH),
                              M["dt_bias"].unsqueeze(1).broadcast_to([P, NT, MH]), ALU.add).then_inc(vec_free, 1)
            own("dt")
            vec.scalar_tensor_tensor(out=dta, in0=dtx, scalar=-1.0, in1=dtx, op0=ALU.mult, op1=ALU.max).then_inc(dt_abs, 1)
            for b in range(B):
                rows(1, b, cx)
            for c in range(2):
                vec.tensor_scalar(ow2[:, c, :], M["out_w"][:, c * P:(c + 1) * P], M["norm_w"][:, c:c + 1], None, ALU.mult)
            vec.wait_ge(dt_log, 1)
            after(vec.scalar_tensor_tensor(out=dt, in0=dtx, scalar=0.0, in1=dtl, op0=ALU.max, op1=ALU.add))
            vec.wait_ge(ea_ready, 1)
            vec.scalar_tensor_tensor(out=da, in0=dt, scalar=-1.0, in1=ea.unsqueeze(1).broadcast_to([P, NT, MH]),
                                     op0=ALU.mult, op1=ALU.mult).then_inc(da_ready, 1)
            def head_sum(u):
                s, tile = UNITS[u]
                vec.wait_ge(sq_ready, u + 1)
                vec.tensor_reduce(ssq[:, s, tile, :], sqr[:, u % 2, :].rearrange("p (h d) -> p h d", h=XH), AX.X, ALU.add).then_inc(ssq_ready, 1)

            def head_norm(u):
                s, tile = UNITS[u]
                vec.wait_ge(rnk_ready, u + 1)
                full(("kr", u))
                if u >= 2:
                    vec.wait_ge(act_full, for_act.number[("kT", u - 2)] + 1)
                vec.tensor_tensor(knr[:, u % 2, :].rearrange("p (h d) -> p h d", h=XH), pbank(for_vec, ("kr", u)).rearrange("p (h d) -> p h d", h=XH),
                                  rnk[:, s, tile, :].unsqueeze(2).broadcast_to([P, XH, XD]), ALU.mult).then_inc(vec_free, 1)

            taps = 0
            for kind, b, c in MORDER:
                v = b % 2
                if kind == "in" and c >= 2:
                    k, key = c - 2, ("in", b, c)
                    taps += 1
                    vec.wait_ge(tap_ready, taps)
                    full(key)
                    src = pbank(for_vec, key).rearrange("p (b t) -> p b t", b=2)
                    dst = xc[:, k, b * 512:(b + 1) * 512].rearrange("p (b t) -> p b t", b=2)
                    for j in (1, 2):
                        after(vec.scalar_tensor_tensor(out=dst[:, :, j:], in0=src[:, :, 0:S - j], scalar=M["conv_w"][:, 4 * k + 3 - j:4 * k + 4 - j],
                                                       in1=dst[:, :, j:], op0=ALU.mult, op1=ALU.add))
                    vec.scalar_tensor_tensor(out=dst[:, :, 3:], in0=src[:, :, 0:S - 3], scalar=M["conv_w"][:, 4 * k:4 * k + 1],
                                             in1=dst[:, :, 3:], op0=ALU.mult, op1=ALU.add).then_inc(vec_free, 1)
                elif kind == "cum":
                    full("cum")
                    c32 = pbank(for_vec, "cum", 32).rearrange("p (t h) -> p t h", h=MH)
                    vec.tensor_copy(cum, c32).then_inc(vec_free, 1)
                    own("cum")
                elif kind == "head":
                    head_sum(b)
                elif kind == "norm":
                    head_norm(b)
                elif kind == "front":
                    full(("xrow", b))
                    vec.tensor_tensor(xdt[:, 2 * b:2 * b + 2, :].rearrange("p t (h n) -> p t h n", h=MH),
                                      pbank(for_vec, ("xrow", b)).rearrange("p (t h n) -> p t h n", t=2, h=MH),
                                      dt[:, 2 * b:2 * b + 2, :].unsqueeze(3).broadcast_to([P, 2, MH, 64]), ALU.mult).then_inc(vec_free, 1)
                    full(("G", b))
                    vec.tensor_tensor(gm[:, v, :], pbank(for_vec, ("G", b), 384), K["gmask"], ALU.mult).then_inc(vec_free, 1)
                    for hf in range(2):
                        full(("bc", b, hf))
                        sums = pbank(for_vec, ("bc", b, hf)).rearrange("p (h l) -> p h l", h=MH)
                        if hf == 1:
                            vec.tensor_tensor(eL[:, v, :, P:256], sums, cum[:, 2 * b, :].unsqueeze(2).broadcast_to([P, MH, P]), ALU.subtract)
                        for h in range(MH):
                            last = vec.tensor_scalar(eL[:, v, h, 256 * hf:256 * hf + P], sums[:, h, :], cum[:, 2 * b + hf, h:h + 1], 0.0,
                                                     ALU.subtract, ALU.min)
                        last.then_inc(vec_free, 1)
                elif kind == "decay":
                    vec.wait_ge(decay_ready, b + 1)
                    vec.tensor_tensor(wL[:, v, :, :], eL[:, v, :, :], gm[:, v, :].unsqueeze(1).broadcast_to([P, MH, 384]), ALU.mult)\
                       .then_inc(w_ready, 1)
                elif kind == "back":
                    key = ("Y", b)
                    full(key)
                    for c in range(2):
                        last = vec.scalar_tensor_tensor(out=yg[:, v, c, :], in0=xc[:, c, b * S:(b + 1) * S], scalar=M["skip"][:, c:c + 1],
                                                        in1=pbank(for_vec, key)[:, c * S:(c + 1) * S], op0=ALU.mult, op1=ALU.add)
                    last.then_inc(vec_free, 1)
                    own(key)
                    vec.tensor_tensor(yg[:, v, :, :], yg[:, v, :, :], zs[:, :, b * S:(b + 1) * S], ALU.mult).then_inc(gated, 1)
                elif kind == "out":
                    key = ("out0", b)
                    full(key)
                    vec.tensor_scalar(msq[:, 2 * b:2 * b + 2], pbank(for_vec, key)[:, 256:258], 1.0 / 256, EPS, ALU.mult, ALU.add).then_inc(msq_ready, 1)
                    if b >= 1:
                        rows(2, b - 1, x)
                    vec.wait_ge(rms_ready, b + 1)
                    for t in range(2):
                        xb = x[:, 2 * b + t, :]
                        last = vec.scalar_tensor_tensor(out=xb, in0=pbank(for_vec, key)[:, t * P:(t + 1) * P], scalar=rms[:, 2 * b + t:2 * b + t + 1],
                                                        in1=xb, op0=ALU.mult, op1=ALU.add)
                    last.then_inc(vec_free, 1)
                    own(key)
                    var(2, b, x)

            after(vec.tensor_tensor(qks[:], X0["q_scale_row"], X0["k_scale_row"], ALU.mult))
            after(vec.tensor_reduce(shift[:, 0:1], qks[:], AX.X, ALU.max, apply_absolute_value=True))
            vec.tensor_scalar(shift[:, 1:2], shift[:, 0:1], -8.0, None, ALU.mult).then_inc(shift_ready, 1)
            rows(2, B - 1, x)
            for kind, b, h in XORDER:
                n, v = b * XH + h, (b * XH + h) // 2 % 2
                if kind == "latent":
                    key = ("uT", 2, b)
                    full(key)
                    vec.tensor_scalar(uT[0][:, b, :], pbank(for_vec, key, S), X0["lnl_w"], X0["lnl_b"], ALU.mult, ALU.add).then_inc(vec_free, 1)
                elif kind == "head":
                    head_sum(b)
                elif kind == "norm":
                    head_norm(b)
                elif kind == "pv" and h % 2:
                    vec.wait_ge(den_ready, n + 1)
                    full(("pv", n))
                    after(vec.reciprocal(rec[:, v, :], den[:, v, :]))
                    for r in (0, 64):
                        vec.tensor_tensor(oT[r:r + 64, b % 2, h // 2, :], pbank(for_vec, ("pv", n - 1 + r // 64), S)[r:r + 64, :],
                                          rec[r:r + 64, v, :], ALU.mult).then_inc(vec_free, 1)
                elif kind == "result":
                    key = ("out1", b)
                    full(key)
                    o = pbank(for_vec, key, 256).rearrange("p (q n) -> p q n", q=2)
                    vec.bn_stats(ostat[:, 2 * b, :], o[:, 0, :])
                    after(vec.bn_stats(ostat[:, 2 * b + 1, :], o[:, 1, :]))
                    vec.bn_aggr(omv[:, 2 * b, :], ostat[:, 2 * b, :])
                    vec.bn_aggr(omv[:, 2 * b + 1, :], ostat[:, 2 * b + 1, :]).then_inc(ovar_ready, 1)
                    vec.wait_ge(orstd_ready, b + 1)
                    for q in range(2):
                        last = vec.tensor_scalar(on[:, q, :], o[:, q, :], omv[:, 2 * b + q, 0:1], ort[:, 1, 2 * b + q:2 * b + q + 1],
                                                 ALU.subtract, ALU.mult)
                    last.then_inc(vec_free, 1)
                    own(key)
                    xb = x[:, 2 * b:2 * b + 2, :]
                    after(vec.tensor_tensor(on, on, X0["lno_w"].unsqueeze(1).broadcast_to([P, 2, P]), ALU.mult))
                    after(vec.tensor_tensor(on, on, X0["lno_b"].unsqueeze(1).broadcast_to([P, 2, P]), ALU.add))
                    after(vec.tensor_tensor(xb, xb, on, ALU.add))
                    var(3, b, x)

            vec.wait_ge(f_in, 16)
            for g, w in enumerate(("uf", "ui", "uc", "uo")):
                vec.tensor_scalar(uh[:, g, :], F[w], 0.5, None, ALU.mult)
            vec.tensor_scalar(halfb[:, 0:1], F["bf"], 0.5, None, ALU.mult)
            vec.tensor_scalar(halfb[:, 1:2], F["bi"], 0.5, None, ALU.mult).then_inc(halves_ready, 1)
            vec.tensor_scalar(cell[:, 0, :], F["in_c"].broadcast_to([P, 256]), 2.0, None, ALU.mult).then_inc(cell_ready, 1)
            for b in range(B):
                rows(3, b, x)
            for t in range(B):
                act_read(("g", t))
                g = gat[:, t % 2]
                vec.wait_ge(cell_ready, t + 1)
                vec.scalar_tensor_tensor(out=mixa, in0=g[:, 0, :], scalar=1.0, in1=cell[:, t % 2, :], op0=ALU.add, op1=ALU.mult)
                after(vec.scalar_tensor_tensor(out=mixb, in0=g[:, 1, :], scalar=1.0, in1=g[:, 2, :], op0=ALU.add, op1=ALU.mult))
                vec.scalar_tensor_tensor(out=cell[:, (t + 1) % 2, :], in0=mixa, scalar=0.5, in1=mixb, op0=ALU.mult, op1=ALU.add)\
                   .then_inc(cell_ready, 1)
            for b in range(B):
                residual(("hrow", b), b)
                var(4, b, x)

            vec.wait_ge(a_in, 16)
            vec.tensor_copy(wa32, w_a)
            turned, plain = wrot.rearrange("p (n s) -> p n s", s=2), w_a[:, 0:256].rearrange("p (n s) -> p n s", s=2)
            vec.tensor_scalar(turned[:, :, 0], plain[:, :, 1], -1.0, None, ALU.mult)
            vec.tensor_copy(turned[:, :, 1], plain[:, :, 0]).then_inc(wa_ready, 1)
            for b in range(B):
                rows(4, b, x)
            vec.wait_ge(r_in, 16)
            for p in range(2):
                for k in range(2):
                    if p == 1:
                        vec.wait_ge(rest_ready, k + 1)
                    for s, table in enumerate((R["cos"], R["sin"])):
                        key = ("qk", p, k, s)
                        full(key)
                        vec.tensor_tensor(rot[:, k, s, :].rearrange("p (b t) -> p b t", b=2), pbank(for_vec, key).rearrange("p (b t) -> p b t", b=2),
                                          table.unsqueeze(1).broadcast_to([P, 2, S]), ALU.mult).then_inc(vec_free, 1)
                    own(("qk", p, k, 1))
                    vec.tensor_tensor(rot[:, k, 0, :], rot[:, k, 0, :], rot[:, k, 1, :], ALU.add).then_inc(rope_ready, 1)
            for p in range(2):
                for j in range(4):
                    full(("st", p, 1, j))
                    vec.tensor_scalar(kst[:, j, p * 512:(p + 1) * 512], pbank(for_vec, ("st", p, 1, j)), K["sixteen"], None, ALU.add).then_inc(vec_free, 1)
            vec.wait_ge(mneg_zero, 1)
            for kind, b, i in AORDER:
                n = 4 * b + i
                if kind == "row":
                    for part in range(3):
                        key, heads = ("row", b, i, part), (4, 2, 2)[part]
                        full(key)
                        dst = mx[:, b, 0, i, :] if part == 0 else mx[:, b, 1, i, 2 * part - 2:2 * part]
                        vec.tensor_reduce(dst, pbank(for_vec, key).rearrange("p (j k) -> p j k", j=heads), AX.X, ALU.max).then_inc(vec_free, 1)
                    if i == 3:
                        own(key)
                        if b >= 2:
                            vec.wait_ge(act_full, for_act.number[("st2", b - 2, 1)] + 1)
                        for q in range(2):
                            last = vec.tensor_scalar(mneg[:, b % 2, q, :, 24::32], mx[:, b, q, :, :].rearrange("p i j -> p j i"),
                                                     -1.0 / 16, None, ALU.mult)
                        last.then_inc(mneg_ready, 1)
                elif kind == "back":
                    key = ("aback", b, i)
                    full(key)
                    t = pbank(for_vec, key, 256).rearrange("p (q j n) -> p q j n", q=2, j=4)
                    d = rec1[:, b, :, 4 * i:4 * i + 4].unsqueeze(3)
                    after(vec.reciprocal(d, t[:, :, :, AD:AD + 1]))
                    o = or1[:, b % 2, :, :].rearrange("p q (j i d) -> p q j i d", j=4, i=4)[:, :, :, i, :]
                    vec.tensor_tensor(o, t[:, :, :, 0:AD], d.broadcast_to([P, 2, 4, AD]), ALU.mult).then_inc(vec_free, 1)
                elif kind == "out":
                    residual(("out4", b), b)
                    var(5, b, x)

            for b in range(B):
                rows(5, b, x)
            act_read(("fk", 2))
            full(("fq", 0))
            full(("fq", 1))
            aq, bq = pbank(for_vec, ("fq", 0)), pbank(for_vec, ("fq", 1))
            vec.tensor_tensor(sab[:, 0, :], aq, pr[:, 0, :], ALU.mult)
            after(vec.scalar_tensor_tensor(out=sab[:, 1, :], in0=bq, scalar=K["keep"], in1=pr[:, 1, :], op0=ALU.mult, op1=ALU.mult))
            after(vec.tensor_tensor(prod[:, 0, :], sab[:, 0, :], sab[:, 1, :], ALU.add))
            vec.scalar_tensor_tensor(out=sab[:, 0, :], in0=aq, scalar=K["keep"], in1=pr[:, 1, :], op0=ALU.mult, op1=ALU.mult).then_inc(vec_free, 1)
            vec.tensor_tensor(sab[:, 1, :], bq, pr[:, 2, :], ALU.mult).then_inc(vec_free, 1)
            own(("fq", 1))
            vec.tensor_tensor(prod[:, 1, :], sab[:, 1, :], sab[:, 0, :], ALU.subtract).then_inc(prod_ready, 1)
            for bp in range(2):
                key = ("corr", bp)
                full(key)
                for b in (2 * bp, 2 * bp + 1):
                    c = pbank(for_vec, key)[:, b % 2 * S:(b % 2 + 1) * S]
                    after(vec.max(top[:, b, :], c))
                    last = vec.max_index(topi[:, b, :], top[:, b, :], c)
                last.then_inc(vec_free, 1)
            own(("corr", 1))
            vec.tensor_tensor(delta[:, :, 0:TOPC], top[:, :, 0:TOPC], top[:, :, 0:1].broadcast_to([P, B, TOPC]), ALU.subtract).then_inc(corr_diff, 1)
            after(vec.tensor_scalar(delm, topi, 7, None, ALU.bitwise_and))
            after(vec.tensor_copy(delf, delm))
            after(vec.tensor_tensor(hit, delf[:, :, 0:TOPC].unsqueeze(3).broadcast_to([P, B, TOPC, 8]),
                                    K["jmod"].unsqueeze(1).unsqueeze(1).broadcast_to([P, B, TOPC, 8]), ALU.is_equal))
            vec.wait_ge(corr_exp, 1)
            after(vec.tensor_reduce(tsum, tope[:, :, 0:TOPC], AX.X, ALU.add))
            vec.reciprocal(trec, tsum)
            after(vec.tensor_tensor(hitw, hit, tope[:, :, 0:TOPC].unsqueeze(3).broadcast_to([P, B, TOPC, 8]), ALU.mult))
            after(vec.tensor_reduce(roll, hitw.rearrange("p b k j -> p b j k"), AX.X, ALU.add))
            after(vec.tensor_tensor(roll, roll, trec.unsqueeze(2).broadcast_to([P, B, 8]), ALU.mult))
            for b in range(B):
                last = vec.tensor_tensor(mbd[:, b, :, :], roll[:, b, :].unsqueeze(1).broadcast_to([P, 16, 8]),
                                         K["bd"].rearrange("p (h j) -> p h j", h=16), ALU.mult)
            last.then_inc(mbd_ready, 1)
            for b in range(B):
                residual(("out5", b), b)
                var(6, b, x)

            for b in range(B):
                rows(6, b, x)
            act_read("gl")
            after(vec.tensor_scalar(gde, gex, 1.0, None, ALU.add))
            vec.wait_ge(gpad_set, 1)
            after(vec.reciprocal(gpad[:, :, 0:E], gde))
            for t in range(NT):
                last = vec.max(gtop[:, t, :], gpad[:, t, :])
            after(last)
            vec.tensor_copy(gfind[:, :, 0:TOPE], gtop[:, :, 0:TOPE])
            after(vec.tensor_reduce(gsum, gtop[:, :, 0:TOPE], AX.X, ALU.add))
            for t in range(NT):
                vec.match_replace(grep[:, t, :], gfind[:, t, :], gpad[:, t, :], 0.0)
            after(vec.reciprocal(grec, gsum))
            after(vec.tensor_tensor(comb, gpad[:, :, 0:E], grep[:, :, 0:E], ALU.subtract))
            after(vec.tensor_tensor(comb, comb, grec.unsqueeze(2).broadcast_to([P, NT, E]), ALU.mult))
            after(vec.tensor_copy(comb3[:, :, 0, :], comb))
            after(vec.tensor_tensor(comr[:, 0], comb, comb3[:, :, 0, :], ALU.subtract))
            after(vec.tensor_copy(comb3[:, :, 1, :], comr[:, 0]))
            after(vec.tensor_tensor(comr[:, 1], comr[:, 0], comb3[:, :, 1, :], ALU.subtract))
            vec.tensor_copy(comb3[:, :, 2, :], comr[:, 1]).then_inc(comb_ready, 1)
            n = 0
            for kind, p, c in EORDER:
                if kind == "turn":
                    full("cbT")
                    vec.tensor_copy(combT[0:48, :], pbank(for_vec, "cbT").bitcast(BF16)[0:48, :]).then_inc(vec_free, 1)
                elif kind == "up":
                    o = hid[:, c, p * 512:(p + 1) * 512]
                    full(("vin", p, c))
                    act_read(("hin", p, c))
                    if c == 8:
                        vec.tensor_tensor(o, sil[:, n % 2, :], pbank(for_vec, ("vin", p, c)), ALU.mult).then_inc(vec_free, 1)
                    else:
                        vec.tensor_tensor(hmul[:, n % 2, :], sil[:, n % 2, :], pbank(for_vec, ("vin", p, c)), ALU.mult).then_inc(vec_free, 1)
                        full(("cw", p, c))
                        own(("vin", p, c))
                        vec.tensor_tensor(o, hmul[:, n % 2, :], pbank(for_vec, ("cw", p, c)), ALU.mult).then_inc(vec_free, 1)
                    n += 1
                else:
                    residual(("out6", c), c)
                    vec.sem_inc(res_ready, 1)

        @block.gpsimd
        def _(pool):
            steps = 0

            def after(ins):
                nonlocal steps
                steps += 1
                ins.then_inc(pool_step, 1)
                pool.wait_ge(pool_step, steps)

            def root(dst, tmp, src, n, eps, done):
                after(pool.tensor_scalar(tmp, src, eps, None, ALU.add))
                pool.tensor_tensor(dst, tmp, half[:, 0:n], ALU.pow).then_inc(done, 1)

            def norm_root(k, b):
                pool.wait_ge(ln_var, 4 * k + b + 1)
                root(rstd[:, k, 2 * b:2 * b + 2], rtmp[:, k, 2 * b:2 * b + 2], mv[:, k, 2 * b:2 * b + 2, 1], 2, EPS, ln_rstd)

            def head_root(u):
                s, tile = UNITS[u]
                pool.wait_ge(ssq_ready, u + 1)
                after(pool.tensor_scalar(ssq[:, s, tile, :], ssq[:, s, tile, :], 1e-24, None, ALU.max))
                pool.tensor_tensor(rnk[:, s, tile, :], ssq[:, s, tile, :], half[:, 0:XH], ALU.pow).then_inc(rnk_ready, 1)

            after(pool.memset(half[:], -0.5))
            for b in range(B):
                norm_root(0, b)
            for b in range(B):
                norm_root(1, b)
            pool.wait_ge(mask_in, 16)
            after(pool.tensor_copy(maskf, mask8[:]))
            pool.tensor_copy(vac[:, :, :, 64:128], maskf[:].unsqueeze(2).unsqueeze(3).broadcast_to([P, NT, XC, 64])).then_inc(vac_mask, 1)
            for kind, b, c in MORDER:
                if kind == "head":
                    head_root(b)
                elif kind == "out":
                    pool.wait_ge(msq_ready, b + 1)
                    pool.tensor_tensor(rms[:, 2 * b:2 * b + 2], msq[:, 2 * b:2 * b + 2], half[:, 0:2], ALU.pow).then_inc(rms_ready, 1)
                    pool.wait_ge(ln_var, 4 * 2 + b + 1)
                    r, t, v = rstd[:, 2, 2 * b:2 * b + 2], rtmp[:, 2, 2 * b:2 * b + 2], mv[:, 2, 2 * b:2 * b + 2, 1]
                    after(pool.tensor_scalar(t, v, EPS, None, ALU.add))
                    after(pool.tensor_tensor(r, t, half[:, 0:2], ALU.pow))
                    after(pool.tensor_tensor(t, r, r, ALU.mult))
                    after(pool.tensor_tensor(t, t, v, ALU.mult))
                    after(pool.tensor_scalar(t, t, EPS, None, ALU.add))
                    after(pool.tensor_tensor(t, t, half[:, 0:2], ALU.pow))
                    pool.tensor_tensor(r, r, t, ALU.mult).then_inc(ln_rstd, 1)
            pool.memset(val[:, :, :, 64:128], 1.0).then_inc(val_ones, 1)
            for kind, b, h in XORDER:
                if kind == "head":
                    head_root(b)
                elif kind == "result":
                    pool.wait_ge(ovar_ready, b + 1)
                    root(ort[:, 1, 2 * b:2 * b + 2], ort[:, 0, 2 * b:2 * b + 2], omv[:, 2 * b:2 * b + 2, 1], 2, EPS, orstd_ready)
                    norm_root(3, b)
            for b in range(B):
                norm_root(4, b)
            for n in range(4):
                pool.wait_ge(lead_ready, n + 1)
                p, k = n // 2, n % 2
                pool.tensor_tensor(qh[:, k, 1, p * 512:(p + 1) * 512], rot[:, k, 0, :], qh[:, k, 0, p * 512:(p + 1) * 512], ALU.subtract)\
                    .then_inc(rest_ready, 1)
            after(pool.memset(mneg, 0.0))
            pool.sem_inc(mneg_zero, 1)
            pool.memset(va1[:, :, :, 2 * AD:32], 0.0)
            pool.memset(va1[:, :, :, AD:2 * AD], 1.0).then_inc(va1_ones, 1)
            pool.wait_ge(vec_full, for_vec.number[("out4", B - 1)] + 1)
            pool.memset(place, 0.0).then_inc(place_zero, 1)
            for k in (5, 6):
                for b in range(B):
                    norm_root(k, b)
                if k == 6:
                    pool.memset(gpad[:, :, E:PADE], -1.0)
                    pool.memset(gfind[:, :, TOPE:8], -1.0).then_inc(gpad_set, 1)

        @block.sync
        def _(sp):
            for dst, src, done in ((x, "x", x_in), (w_k, "k", k_in), (w_m, "m", m_in), (cx, "ctx", c_in), (w_x, "xw", xw_in),
                                   (mask8, "mask", mask_in), (w_f, "f", f_in), (w_a, "a", a_in), (w_r, "r", r_in), (w_h, "h", h_in), (w_b, "b", b_in),
                                   (w_c, "c", c1_in)):
                sp.dma_start(dst[:], io[src]).then_inc(done, 16)
            sp.wait_ge(vec_full, for_vec.number[("out1", B - 1)] + 1)
            sp.dma_start(w_e, io["e"]).then_inc(e_in, 16)
            for b in range(B):
                sp.wait_ge(res_ready, b + 1)
                sp.dma_start(io["out"][:, 2 * b:2 * b + 2, :], x[:, 2 * b:2 * b + 2, :]).then_inc(stored, 16)
            sp.wait_ge(stored, 16 * B)


def program(nc, arrays):
    io = {}
    for name, a in arrays.items():
        io[name] = nc.dram_tensor("in_" + name, a.shape, mybir.dt.from_np(a.dtype), kind="ExternalInput").ap()
    for name in ("x", "ctx"):
        io[name] = io[name].rearrange("b (h p) d -> p (b h) d", p=P)
    out = nc.dram_tensor("out_rows", (B, S, D), F32, kind="ExternalOutput").ap()
    io["out"] = out.rearrange("b (h p) d -> p (b h) d", p=P)
    decoder(nc, io)


def kernel(**inputs):
    import concourse.bacc as _bacc
    import ml_dtypes
    import numpy as np
    from concourse.bass_utils import run_bass_kernel_spmd

    w = {name: np.asarray(a) for name, a in inputs.items()}

    def pack(spec, parts):
        cols = []
        for name, n in spec:
            a = parts[name]
            assert a.size in (P * n, n), (name, a.shape)
            cols.append(a.reshape(P, n) if a.size == P * n else np.broadcast_to(a.reshape(1, n), (P, n)))
        return np.ascontiguousarray(np.concatenate(cols, axis=1))

    def chunks(a):
        return a.reshape(-1, P, a.shape[1]).transpose(1, 0, 2)

    def col(a):
        return a.reshape(-1, P).T

    m = "L0_attn_"
    mamba = pack(SPEC_M, {
        "in_w": w[m + "in_proj_w"], "conv_w": chunks(w[m + "conv_w"][:, 0, :]), "conv_b": col(w[m + "conv_b"]),
        "dt_bias": w[m + "dt_bias"], "a_log": w[m + "A_log"], "skip": col(np.repeat(w[m + "D"], 64)), "norm_w": col(w[m + "norm_w"]),
        "out_w": chunks(w[m + "out_proj_w"])})
    m = "L0_xattn_"
    cross = pack(SPEC_X, {
        "lnx_w": w[m + "ln_x_w"].reshape(P, 1), "lnx_b": w[m + "ln_x_b"].reshape(P, 1), "lnl_w": w[m + "ln_l_w"].reshape(P, 1),
        "lnl_b": w[m + "ln_l_b"].reshape(P, 1), "q_scale": np.tile(w[m + "q_scale"], 2).reshape(P, 1), "k_scale": np.tile(w[m + "k_scale"], 2).reshape(P, 1),
        "wq": w[m + "Wq"], "wkv": w[m + "Wkv"], "wo": chunks(w[m + "Wo"]), "lno_w": w[m + "ln_o_w"], "lno_b": w[m + "ln_o_b"],
        "q_scale_row": w[m + "q_scale"], "k_scale_row": w[m + "k_scale"]})
    m = "L0_ffn_"
    rec = pack(SPEC_F, {n: w[m + n].T if w[m + n].ndim == 2 else w[m + n].reshape(P, 1) for n, _ in SPEC_F})
    attn = pack(SPEC_A, {n: w["L1_attn_" + n] for n, _ in SPEC_A})
    corr = pack(SPEC_C, {n: w["L1_xattn_" + n] for n, _ in SPEC_C})
    m = "L1_ffn_"
    moe = pack(SPEC_E, {
        "gate": w[m + "gate_w"].T, "ws_in": w[m + "ws_in"], "vs_in": w[m + "vs_in"],
        "e_win": w[m + "e_win"].transpose(1, 0, 2), "e_vin": w[m + "e_vin"].transpose(1, 0, 2),
        "w_out": chunks(np.concatenate([w[m + "e_wout"].reshape(-1, D), w[m + "ws_out"]]))})

    eye, i, f = np.eye(P), np.arange(P), np.arange(P)
    tri = (i[:, None] <= i[None, :]).astype(np.float64)
    t, tau = np.arange(S), np.arange(S)
    cos = np.cos(2 * np.pi * np.outer(t, f) / S)
    sin = np.sin(2 * np.pi * np.outer(t, f) / S)
    mid = np.where(t % 2 == 0, 1.0, -1.0)
    cos_mid, sin_mid = cos.copy(), sin.copy()
    cos_mid[:, 0] = mid
    sin_mid[:, 0] = mid
    dft = np.stack([cos, sin_mid, cos_mid], axis=1).reshape(2, P, 3, P).transpose(1, 0, 2, 3)
    weight = np.where(f == 0, 1.0, 2.0)[:, None] / S
    icos = weight * np.cos(2 * np.pi * np.outer(f, tau) / S)
    isin = weight * np.sin(2 * np.pi * np.outer(f, tau) / S)
    isin[0] = mid / S
    freq = (np.arange(S, dtype=np.float32)[:, None] * (1.0 / np.float32(10000.0) ** (np.arange(0, AD, 2, dtype=np.float32) / np.float32(AD)))[None, :]).T
    freq = np.tile(np.repeat(freq, 2, axis=0), (AH, 1))
    rope = pack(SPEC_R, {"cos": np.cos(freq), "sin": np.sin(freq)}).astype(np.float32)
    heads = (i[:, None] // 8 == i[None, :] // 8).astype(np.float64)
    consts = pack(SPEC_K, {
        "ident": eye, "ones": np.ones((P, P)), "tri": tri, "gmask": np.concatenate([tri, np.ones((P, P)), tri], axis=1), "dft": dft,
        "idft": np.concatenate([icos, isin], axis=1), "keep": (f > 0).astype(np.float64).reshape(P, 1),
        "sixteen": np.where(i % 32 == 24, 16.0, 0.0).reshape(P, 1), "jmod": (i[:, None] - np.arange(8)[None, :]) % 8, "bd": heads, "permute": (i[:, None] == (i[None, :] % AH) * AD + i[None, :] // AH).astype(np.float64)}).astype(np.float32)
    sel = np.zeros((4, P, 4, P))
    for j in range(4):
        for g in range(4):
            for d in range(8):
                for r, (qp, kp) in enumerate(((0, 0), (0, 1), (1, 0))):
                    sel[qp, 8 * (4 * j + g) + d, j, 32 * g + 8 * r + d] = 1.0
                    sel[2 + kp, 8 * (4 * j + g) + d, j, 32 * g + 8 * r + d] = 1.0
    halves = pack(SPEC_H, {"ident": eye, "selq1": sel[0], "selq2": sel[1], "selk1": sel[2], "selk2": sel[3]}).astype(np.float16)
    far = np.float64(-1e30)
    expand = np.zeros((P, 8, P))
    for part in range(3):
        for e in range(E):
            expand[part * E + e, e // 2, e % 2 * 64:e % 2 * 64 + 64] = 1.0
    brain = pack(SPEC_B, {
        "ident": eye, "mask_row": np.where(i[None, :] > i[:, None], far, 0.0), "mask_col": np.where(i[:, None] > i[None, :], far, 0.0),
        "expand": expand}).astype(ml_dtypes.bfloat16)

    arrays = {
        "x": np.ascontiguousarray(w["x"]), "ctx": np.ascontiguousarray(w["ctx_1024"]),
        "mask": np.ascontiguousarray(w["mask_BxS2_bk0"].reshape(NT, P).T), "m": mamba, "xw": cross, "f": rec, "a": attn, "c": corr,
        "e": moe, "k": consts, "h": halves, "r": rope, "b": brain}
    nc = _bacc.Bacc("TRN2", target_bir_lowering=False, num_devices=1)
    program(nc, arrays)
    return run_bass_kernel_spmd(nc, [{"in_" + name: a for name, a in arrays.items()}], core_ids=[0]).results[0]["out_rows"]
```

```python
from contextlib import ExitStack

import concourse.bass as bass
from concourse import mybir

F32 = mybir.dt.float32
F16 = mybir.dt.float16
BF16 = mybir.dt.bfloat16
U8 = mybir.dt.uint8
U32 = mybir.dt.uint32
I32 = mybir.dt.int32
ALU = mybir.AluOpType
ACT = mybir.ActivationFunctionType
AX = mybir.AxisListType

P = 128
B = 4
S = 256
D = 128
NT = B * S // P
EPS = 1e-5

MH = 4
MC = 4
TAPS = 4
XH = 8
XD = 64
XC = 4
AH = 16
AD = 8
TOPC = 5
E = 16
TOPE = 4
HC = 9
PADE = E + 4

SPEC_M = [("in_w", 772), ("conv_w", 16), ("conv_b", 4), ("dt_bias", 4), ("a_log", 4), ("skip", 2), ("norm_w", 2), ("out_w", 256)]
SPEC_X = [("lnx_w", 1), ("lnx_b", 1), ("lnl_w", 1), ("lnl_b", 1), ("q_scale", 1), ("k_scale", 1), ("wq", 512), ("wkv", 1024), ("wo", 512),
          ("lno_w", 128), ("lno_b", 128), ("q_scale_row", 64), ("k_scale_row", 64)]
SPEC_F = [("wf", 128), ("uf", 128), ("wi", 128), ("ui", 128), ("wc", 128), ("uc", 128), ("wo", 128), ("uo", 128),
          ("bf", 1), ("bi", 1), ("bc", 1), ("bo", 1), ("in_c", 1)]
SPEC_A = [("qw", 128), ("kw", 128), ("vw", 128), ("ow", 128)]
SPEC_C = [("wq", 128), ("wk", 128), ("wv", 128), ("wo", 128)]
SPEC_E = [("gate", 16), ("ws_in", 128), ("vs_in", 128), ("e_win", 1024), ("e_vin", 1024), ("w_out", 1152)]
SPEC_K = [("ident", 128), ("ones", 128), ("tri", 128), ("gmask", 384), ("dft", 768), ("idft", 512), ("keep", 1), ("sixteen", 1),
          ("jmod", 8), ("bd", 128), ("permute", 128)]
SPEC_R = [("cos", 256), ("sin", 256)]
SPEC_H = [("ident", 128), ("selq1", 512), ("selq2", 512), ("selk1", 512), ("selk2", 512)]
SPEC_B = [("ident", 128), ("mask_row", 128), ("mask_col", 128), ("expand", 1024)]


def width(spec):
    return sum(n for _, n in spec)


def columns(tile, spec):
    at, out = 0, {}
    for name, n in spec:
        out[name] = tile[:, at:at + n]
        at += n
    return out


class Uses:

    def __init__(self, first):
        self.first = first
        self.number = {}

    def add(self, key):
        assert key not in self.number, key
        self.number[key] = len(self.number)
        return self.number[key]


def decoder(nc, io):
    ctx = ExitStack()
    with ctx:
        def sb(name, shape, dt=F32):
            return ctx.enter_context(nc.sbuf_tensor(name, shape, dt))[:]

        def sem(name):
            return ctx.enter_context(nc.semaphore(name))

        ps = ctx.enter_context(nc.psum_tensor("ps", [P, 8 * 512], F32))
        for_act, for_vec = Uses(0), Uses(4)

        def pbank(uses, key, n=512):
            b = uses.first + uses.number[key] % 4
            return ps[:, b * 512:b * 512 + n]

        w_m, w_x, w_f = sb("w_m", [P, width(SPEC_M)]), sb("w_x", [P, width(SPEC_X)]), sb("w_f", [P, width(SPEC_F)])
        w_k = sb("w_k", [P, width(SPEC_K)])
        M, X0, F, K = columns(w_m, SPEC_M), columns(w_x, SPEC_X), columns(w_f, SPEC_F), columns(w_k, SPEC_K)
        ident = K["ident"]
        mask8, maskf = sb("mask8", [P, NT], U8), sb("maskf", [P, NT])

        x = sb("x", [P, NT, D])
        urow = [sb(f"urow{i}", [P, NT, D]) for i in range(2)]
        uT = [sb(f"uT{i}", [P, B, S]) for i in range(2)]
        cx = sb("cx", [P, NT, D])
        cT = sb("cT", [P, B, S])
        cnT = sb("cnT", [P, B, S])
        stats = sb("stats", [P, 7, NT, 6])
        mv = sb("mv", [P, 7, NT, 2])
        rstd = sb("rstd", [P, 7, NT])
        rtmp = sb("rtmp", [P, 7, NT])
        half = sb("half", [P, 64])

        XTOP = 13664
        WA = 24128
        WB = 12800
        regA, regB = sb("regA", [P, WA]), sb("regB", [P, WB])

        class Carve:
            def __init__(self, region, size, at=0):
                self.region, self.size, self.at = region, size, at

            def f32(self, n):
                a = self.region[:, self.at:self.at + n]
                self.at += n
                assert self.at <= self.size, (self.at, self.size)
                return a

            def f16(self, n):
                return self.f32(n // 2).bitcast(F16)

            def bf16(self, n):
                return self.f32(n // 2).bitcast(BF16)

        a = Carve(regA, WA, XTOP)
        xc = a.f32(MC * 1024).rearrange("p (c t) -> p c t", c=MC)
        zs = a.f32(2 * 1024).rearrange("p (c t) -> p c t", c=2)
        dtx = a.f32(32).rearrange("p (t h) -> p t h", h=MH)
        dta = a.f32(32).rearrange("p (t h) -> p t h", h=MH)
        dte = a.f32(32).rearrange("p (t h) -> p t h", h=MH)
        dtl = a.f32(32).rearrange("p (t h) -> p t h", h=MH)
        dt = a.f32(32).rearrange("p (t h) -> p t h", h=MH)
        ea = a.f32(4)
        da = a.f32(32).rearrange("p (t h) -> p t h", h=MH)
        cum = a.f32(32).rearrange("p (t h) -> p t h", h=MH)
        gm = a.f32(384)
        eL = a.f32(2 * 4 * 384).rearrange("p (v h n) -> p v h n", v=2, h=MH)
        xdt = cx.rearrange("p t n -> p (t n)").rearrange("p (t n) -> p t n", t=4)
        spare = uT[1].rearrange("p b s -> p (b s)").rearrange("p (v c n) -> p v c n", v=2, c=2)
        yg, ysq = spare[:, 0, :, :], spare[:, 1, :, :]
        msq = a.f32(8)
        rms = a.f32(8)
        ow2 = a.f32(256).rearrange("p (c n) -> p c n", c=2)

        a = Carve(regA, XTOP)
        pT = a.f32(3 * 1024).rearrange("p (v k q) -> p v k q", v=3, k=4)
        q1 = a.f16(XH * 512).rearrange("p (h t) -> p h t", h=XH)
        q2 = a.f16(XC * 512).rearrange("p (c t) -> p c t", c=XC)
        kl = a.f16(XH * 512).rearrange("p (h t) -> p h t", h=XH)
        val = a.f32(4 * XC * 192).rearrange("p (t c n) -> p t c n", t=4, c=XC)
        den = a.f32(2 * 256).rearrange("p (v n) -> p v n", v=2)
        rec = a.f32(256)
        oT = a.f32(5 * 256).rearrange("p (c n) -> p c n", c=5)
        on = a.f32(256).rearrange("p (q n) -> p q n", q=2)
        ostat = a.f32(NT * 6).rearrange("p (t n) -> p t n", t=NT)
        omv = a.f32(NT * 2).rearrange("p (t n) -> p t n", t=NT)
        ort = a.f32(2 * NT).rearrange("p (v t) -> p v t", v=2)
        bb = Carve(regB, WB)
        kc = bb.f16(XH * 1024).rearrange("p (h t) -> p h t", h=XH)
        vac = bb.f32(NT * XC * 192).rearrange("p (t c n) -> p t c n", t=NT, c=XC)
        sqr = bb.f32(2 * 512).rearrange("p (v n) -> p v n", v=2)
        parts = bb.f16(2 * 1536).rearrange("p (v n) -> p v n", v=2)
        ssq = sb("ssq", [P, 3, NT, XH])
        rnk = sb("rnk", [P, 3, NT, XH])
        qks = sb("qks", [P, 64])
        ident16 = sb("ident16", [P, P], F16)
        shift = sb("shift", [P, 2])

        a = Carve(regA, WA, XTOP)
        w_a, w_c, w_r = a.f16(width(SPEC_A)), a.f32(width(SPEC_C)), a.f32(width(SPEC_R))
        w_h, w_b = a.f16(width(SPEC_H)), a.bf16(width(SPEC_B))
        A1, C1, R, KH, KB = columns(w_a, SPEC_A), columns(w_c, SPEC_C), columns(w_r, SPEC_R), columns(w_h, SPEC_H), columns(w_b, SPEC_B)
        above = a.at

        uh = a.f32(4 * 128).rearrange("p (g n) -> p g n", g=4)
        halfb = a.f32(2)
        cell = a.f32(2 * 256).rearrange("p (v n) -> p v n", v=2)
        gat = a.f32(2 * 3 * 256).rearrange("p (v g n) -> p v g n", v=2, g=3)
        mixa = a.f32(256)
        mixb = a.f32(256)
        hT = cx.rearrange("p t n -> p (t n)").rearrange("p (t n) -> p t n", t=B)

        a = Carve(regA, XTOP)
        wa32 = a.f32(512)
        wrot = a.f32(256)
        rot = a.f32(2 * 2 * 512).rearrange("p (v s t) -> p v s t", v=2, s=2)
        qh = a.f16(2 * 2 * 1024).rearrange("p (k s t) -> p k s t", k=2, s=2)
        qst = a.f16(2 * 4 * 1024).rearrange("p (v j t) -> p v j t", v=2, j=4)
        kst = a.f16(4 * 1024).rearrange("p (j t) -> p j t", j=4)
        sixteen = a.f32(1)
        mx = a.f32(B * 2 * 16).rearrange("p (b q i j) -> p b q i j", b=B, q=2, i=4)
        mneg = a.f16(2 * 2 * 4 * 128).rearrange("p (v q j c) -> p v q j c", v=2, q=2, j=4)
        oc1 = a.f32(2 * 256).rearrange("p (v n) -> p v n", v=2)
        or1 = a.f32(2 * 256).rearrange("p (v q n) -> p v q n", v=2, q=2)
        rec1 = a.f32(B * 32).rearrange("p (b q h) -> p b q h", b=B, q=2)
        a = Carve(regA, WA, above)
        oT1 = a.f32(2 * 256).rearrange("p (v n) -> p v n", v=2)
        pT1 = a.f32(3 * 1536).rearrange("p (v n) -> p v n", v=3)

        a = Carve(regA, XTOP)
        qr = a.f32(2 * 512).rearrange("p (h b n) -> p h b n", h=2, b=B)
        sab = a.f32(2 * 512).rearrange("p (f n) -> p f n", f=2)
        prod = a.f32(2 * 512).rearrange("p (f n) -> p f n", f=2)
        top = a.f32(B * 8).rearrange("p (b n) -> p b n", b=B)
        topi = a.f32(B * 8).rearrange("p (b n) -> p b n", b=B).bitcast(U32)
        topf = a.f32(B * 8).rearrange("p (b n) -> p b n", b=B)
        tope = a.f32(B * 8).rearrange("p (b n) -> p b n", b=B)
        ntop = a.f32(B)
        tsum = a.f32(B)
        trec = a.f32(B)
        delta = a.f32(B * 8).rearrange("p (b n) -> p b n", b=B)
        deli = a.f32(B * 8).rearrange("p (b n) -> p b n", b=B).bitcast(U32)
        delm = a.f32(B * 8).rearrange("p (b n) -> p b n", b=B).bitcast(U32)
        delf = a.f32(B * 8).rearrange("p (b n) -> p b n", b=B)
        hit = a.f32(B * 5 * 8).rearrange("p (b k j) -> p b k j", b=B, k=5)
        hitw = a.f32(B * 5 * 8).rearrange("p (b k j) -> p b k j", b=B, k=5)
        roll = a.f32(B * 8).rearrange("p (b j) -> p b j", b=B)
        mbd = a.f32(B * 128).rearrange("p (b h j) -> p b h j", b=B, h=16)
        place = a.f32(B * 512).rearrange("p (b t h r) -> p b t h r", b=B, t=2, h=2)

        a = Carve(regA, XTOP)
        hid = a.f32(HC * 1024).rearrange("p (c t) -> p c t", c=HC)
        sil = a.f32(2 * 512).rearrange("p (v n) -> p v n", v=2)
        hmul = a.f32(2 * 512).rearrange("p (v n) -> p v n", v=2)
        gex = a.f32(NT * E).rearrange("p (t e) -> p t e", t=NT)
        gde = a.f32(NT * E).rearrange("p (t e) -> p t e", t=NT)
        gpad = a.f32(NT * PADE).rearrange("p (t e) -> p t e", t=NT)
        grep = a.f32(NT * PADE).rearrange("p (t e) -> p t e", t=NT)
        gtop = a.f32(NT * 8).rearrange("p (t e) -> p t e", t=NT)
        gfind = a.f32(NT * 8).rearrange("p (t e) -> p t e", t=NT)
        gsum = a.f32(NT)
        grec = a.f32(NT)
        comb = a.f32(NT * E).rearrange("p (t e) -> p t e", t=NT)
        comr = a.f32(2 * NT * E).rearrange("p (v t e) -> p v t e", v=2, t=NT)
        comb3 = a.bf16(NT * 48).rearrange("p (t s e) -> p t s e", t=NT, s=3)
        combT = a.bf16(1024)
        bb = Carve(regB, WB)
        w_e = bb.f32(width(SPEC_E))
        G = columns(w_e, SPEC_E)
        va1 = bb.f32(NT * AH * 32).rearrange("p (t h n) -> p t h n", t=NT, h=AH)

        kr = bb.f32(2 * 512).rearrange("p (h b n) -> p h b n", h=2, b=B)
        vr = bb.f32(2 * 512).rearrange("p (h b n) -> p h b n", h=2, b=B)
        vo = bb.f32(1024).rearrange("p (b n) -> p b n", b=B)
        pr = bb.f32(3 * 512).rearrange("p (f n) -> p f n", f=3)

        names = ["x_in", "m_in", "k_in", "c_in", "xw_in", "f_in", "a_in", "h_in", "r_in", "b_in", "c1_in", "e_in", "mask_in", "stored"]
        x_in, m_in, k_in, c_in, xw_in, f_in, a_in, h_in, r_in, b_in, c1_in, e_in, mask_in, stored = [sem(n) for n in names]
        act_full, act_free, vec_full, vec_free = sem("act_full"), sem("act_free"), sem("vec_full"), sem("vec_free")
        ln_var, ln_rstd, ln_rows, x_ready = sem("ln_var"), sem("ln_rstd"), sem("ln_rows"), sem("x_ready")
        half_set = sem("half_set")
        pool_step = sem("pool_step")
        vec_step = sem("vec_step")
        act_step = sem("act_step")

        block = ctx.enter_context(nc.Block())
        LN = {"mamba": 0, "ctx": 1, "lat": 2, "rec": 3, "attn": 4, "corr": 5, "moe": 6}
        ROW = {0: 0, 1: 1, 2: 0, 3: 1, 4: 0, 5: 1, 6: 0}
        ORDER = []
        for n, (p, c) in enumerate([(p, c) for p in range(2) for c in (2, 3, 4, 5, 0, 1)]):
            ORDER.append(("in", p, c))
            if n == 5:
                ORDER.append(("cum", 0, 0))
            ORDER.append(("context", n, 0) if n < B else ("value", 0, n - B))

        def each(step, s, b):
            return [(step, s, 2 * b), (step, s, 2 * b + 1)]

        ORDER += [("front", 0, 0)] + each("head", 0, 0) + [("decay", 0, 0)] + each("norm", 0, 0) + [("front", 1, 0)] + each("parts", 0, 0)
        ORDER += [("back", 0, 0)] + each("turn", 0, 0) + each("head", 0, 1) + [("decay", 1, 0)] + each("norm", 0, 1) + [("out", 0, 0)]
        ORDER += each("parts", 0, 1) + [("front", 2, 0)] + each("turn", 0, 1) + [("back", 1, 0), ("rows2", 0, 0), ("latent", 0, 0)]
        ORDER += each("head", 1, 0) + [("decay", 2, 0)] + each("norm", 1, 0) + [("out", 1, 0)] + each("parts", 1, 0) + [("front", 3, 0)]
        ORDER += each("turn", 1, 0) + [("back", 2, 0)] + each("head", 2, 0) + [("decay", 3, 0)] + each("norm", 2, 0)
        ORDER += [("out", 2, 0)] + each("parts", 2, 0) + [("rows2", 1, 0)] + each("value", 1, 0) + each("turn", 2, 0)
        BESIDE = {0: [("back", 3, 0)], 1: [("out", 3, 0)], 6: [("rows2", 2, 0)], 8: [("rows2", 3, 0), ("halves", 0, 0)]}
        for n in range(B * XH + 9):
            b, h = n // XH, n % XH
            k = b + 1
            if n < B * XH:
                ORDER.append(("sim", b, h))
            ORDER += BESIDE.get(n, [])
            if 1 <= b < 3:
                ORDER += {0: each("norm", 0, k), 1: each("parts", 0, k), 2: each("turn", 0, k)}.get(h, [])
            if k < B:
                ORDER += {0: [("latent", k, 0)], 2: each("norm", 1, k), 3: each("parts", 1, k), 4: each("turn", 1, k) + each("head", 2, k),
                          5: each("norm", 2, k), 6: each("parts", 2, k), 7: each("turn", 2, k) + each("value", 1, k)}.get(h, [])
            if 0 <= n - 2 < B * XH:
                ORDER.append(("pv", (n - 2) // XH, (n - 2) % XH))
            if k < B and h == 1:
                ORDER += each("head", 1, k)
            if b >= 1:
                ORDER += {3: [("result", b - 1, 0)], 4: [("rows3", b - 1, 0)]}.get(h, [])
                ORDER += {5: [("turn3", b - 1, 0)], 6: [("gates", b - 1, 0)], 7: [("cell", b - 1, 0)]}.get(h if b == B else h - 2, [])
            if 2 <= b <= B and h < 2:
                ORDER += [("gates", b - 2, 0)] if h == 0 else [("cell", b - 2, 0)]
            if b < 2 and h == 7:
                ORDER += each("head", 0, k + 1)
            if b == B:
                ORDER += {3: [("corr_rows", "k", i) for i in range(B)], 4: [("corr_rows", "v", i) for i in range(B)],
                          5: [("corr_vo", 0, 0)], 6: [("corr_spectra", 0, 0)]}.get(h, [])
        UNIT = {}
        for step, s, tile in ORDER:
            if step == "head":
                UNIT[s, tile] = len(UNIT)
        AORDER = [("row", 0, i) for i in range(4)] + [("stack", 0, 0)]
        for n in range(4 * B + 4):
            b, i = n // 4, n % 4
            if b + 1 < B:
                AORDER.append(("row", b + 1, i))
            if b < B:
                AORDER.append(("col", b, i))
            if 0 <= n - 1 < 4 * B:
                AORDER.append(("pv", (n - 1) // 4, (n - 1) % 4))
            if 0 <= n - 2 < 4 * B:
                AORDER.append(("back", (n - 2) // 4, (n - 2) % 4))
            if b + 1 < B and i == 3:
                AORDER.append(("stack", b + 1, 0))
            if n >= 4 and i == 2:
                AORDER.append(("turn", b - 1, 0))
            if n >= 4 and i == 3:
                AORDER.append(("out", b - 1, 0))
        EORDER = [("up", 0, 8), ("turn", 0, 0)] + [("up", 0, c) for c in range(8)] + [("up", 1, c) for c in (8, 0, 1, 2)]
        EORDER += [("down", 0, 0), ("down", 0, 1)] + [("up", 1, c) for c in range(3, 8)] + [("down", 1, 2), ("down", 1, 3)]

        da_ready, conv_ready, w_ready, gated, ysq_ready = sem("da_ready"), sem("conv_ready"), sem("w_ready"), sem("gated"), sem("ysq_ready")
        tap_ready, lead_parts, parts_ready, q_scaled, ident16_set = sem("tap_ready"), sem("lead_parts"), sem("parts_ready"), sem("q_scaled"), sem("ident16_set")
        dt_abs, dt_log, ea_ready = sem("dt_abs"), sem("dt_log"), sem("ea_ready")
        den_ready, decay_ready, msq_ready, rms_ready = sem("den_ready"), sem("decay_ready"), sem("msq_ready"), sem("rms_ready")
        sq_ready, ssq_ready, rnk_ready = sem("sq_ready"), sem("ssq_ready"), sem("rnk_ready")
        val_ones, vac_mask, shift_ready = sem("val_ones"), sem("vac_mask"), sem("shift_ready")
        ovar_ready, orstd_ready = sem("ovar_ready"), sem("orstd_ready")
        cell_ready, gates_ready, halves_ready = sem("cell_ready"), sem("gates_ready"), sem("halves_ready")
        rope_ready, lead_ready, wa_ready, mneg_zero, mneg_ready, va1_ones = sem("rope_ready"), sem("lead_ready"), sem("wa_ready"), sem("mneg_zero"), sem("mneg_ready"), sem("va1_ones")
        place_zero, prod_ready, mbd_ready, corr_diff, corr_exp = sem("place_zero"), sem("prod_ready"), sem("mbd_ready"), sem("corr_diff"), sem("corr_exp")
        gpad_set, comb_ready = sem("gpad_set"), sem("comb_ready")
        res_ready, rest_ready = sem("res_ready"), sem("rest_ready")

        @block.tensor
        def _(pe):
            def act_bank(key):
                n = for_act.add(key)
                if n >= 4:
                    pe.wait_ge(act_free, n - 3)
                return pbank(for_act, key)

            def vec_bank(key):
                n = for_vec.add(key)
                if n >= 4:
                    pe.wait_ge(vec_free, n - 3)
                return pbank(for_vec, key)

            def act_has(key):
                pe.wait_ge(act_free, for_act.number[key] + 1)

            def vec_has(key):
                pe.wait_ge(vec_free, for_vec.number[key] + 1)

            def rows_turn(k, b):
                pe.wait_ge(ln_rows, 4 * k + b + 1)
                t = act_bank(("uT", k, b))
                for hf in range(2):
                    last = pe.transpose(t[:, hf * P:(hf + 1) * P], urow[ROW[k]][:, 2 * b + hf, :], ident)
                last.then_inc(act_full, 1)

            def values(s, tile):
                if s == 0:
                    act_has(("uT", 1, tile // 2))
                else:
                    vec_has(("uT", 2, tile // 2))
                t = act_bank(("xv", s, tile))
                pe.matmul(t, (cnT, uT[0])[s][:, tile // 2, tile % 2 * P:(tile % 2 + 1) * P], X0["wkv"][:, 512:1024],
                          start=True, stop=True).then_inc(act_full, 1)

            def head_rows(s, tile):
                u = UNIT[s, tile]
                if s == 0:
                    act_has(("uT", 1, tile // 2))
                else:
                    vec_has(("uT", 2, tile // 2))
                t = vec_bank(("kr", u))
                w = X0["wq"] if s == 2 else X0["wkv"][:, 0:512]
                pe.matmul(t, (uT[0] if s else cnT)[:, tile // 2, tile % 2 * P:(tile % 2 + 1) * P], w, start=True, stop=True).then_inc(vec_full, 1)

            def head_turn(s, tile):
                u = UNIT[s, tile]
                pe.wait_ge(parts_ready, u + 1)
                t = act_bank(("kT", u)).bitcast(F16)
                for h in range(XH):
                    last = pe.transpose(t[:, h * P:(h + 1) * P], parts[:, u % 2, h * P:(h + 1) * P], ident16)
                last.then_inc(act_full, 1)
                if s == 2:
                    t = act_bank(("qT", u)).bitcast(F16)
                    for c in range(XC):
                        last = pe.transpose(t[:, c * P:(c + 1) * P], parts[:, u % 2, 1024 + c * P:1024 + (c + 1) * P], ident16)
                    last.then_inc(act_full, 1)

            def corr_rows(name, b):
                t = act_bank(("cr", name, b))
                for hf in range(2):
                    src = (uT[1] if name == "q" else cT)[:, b, hf * P:(hf + 1) * P]
                    last = pe.matmul(t[:, hf * P:(hf + 1) * P], src, C1["w" + name], start=True, stop=True)
                last.then_inc(act_full, 1)

            def spectrum(name, f):
                t = act_bank(("fk", f)) if name == "k" else vec_bank(("fq", f))
                for hf in range(2):
                    at = hf * 384 + f * P
                    last = pe.matmul(t, K["dft"][:, at:at + P], (kr if name == "k" else qr)[:, hf, :, :], start=(hf == 0), stop=(hf == 1))
                last.then_inc(act_full if name == "k" else vec_full, 1)

            pe.wait_ge(k_in, 16)
            for b in range(B):
                rows_turn(0, b)
            pe.wait_ge(m_in, 16)
            act_has(("uT", 0, B - 1))
            t = vec_bank("dt")
            for tile in range(NT):
                last = pe.matmul(t[:, tile * MH:(tile + 1) * MH], uT[0][:, tile // 2, tile % 2 * P:(tile % 2 + 1) * P],
                                 M["in_w"][:, 768:772], start=True, stop=True)
            last.then_inc(vec_full, 1)
            for kind, b, c in ORDER:
                h = c
                if kind == "in":
                    t = vec_bank(("in", b, c)) if c >= 2 else act_bank(("in", b, c))
                    pe.matmul(t, M["in_w"][:, c * P:(c + 1) * P], uT[0][:, 2 * b:2 * b + 2, :], start=True, stop=True)\
                      .then_inc(vec_full if c >= 2 else act_full, 1)
                elif kind == "cum":
                    pe.wait_ge(da_ready, 1)
                    t = vec_bank("cum")[:, 0:NT * MH].rearrange("p (b s h) -> p b s h", b=B, s=2)
                    pe.matmul(t[:, :, 0, :], K["tri"], da[:, 0::2, :], start=True, stop=True)
                    pe.matmul(t[:, :, 1, :], K["tri"], da[:, 1::2, :], start=True, stop=False)
                    pe.matmul(t[:, :, 1, :], K["ones"], da[:, 0::2, :], start=False, stop=True).then_inc(vec_full, 1)
                elif kind == "context":
                    pe.wait_ge(c_in, 16)
                    t = act_bank(("cT", b))
                    for hf in range(2):
                        last = pe.transpose(t[:, hf * P:(hf + 1) * P], cx[:, 2 * b + hf, :], ident)
                    last.then_inc(act_full, 1)
                    rows_turn(1, b)
                elif kind == "value":
                    if b == 0 and c == 0:
                        pe.wait_ge(xw_in, 16)
                    values(b, c)
                elif kind == "head":
                    head_rows(b, c)
                elif kind == "turn":
                    if (b, c) == (0, 0):
                        pe.wait_ge(ident16_set, 1)
                    head_turn(b, c)
                elif kind == "front":
                    pe.wait_ge(conv_ready, 4 * (b // 2) + 2)
                    t = vec_bank(("xrow", b))
                    for hf in range(2):
                        for c in range(2):
                            at = b * S + hf * P
                            last = pe.transpose(t[:, hf * 256 + c * P:hf * 256 + (c + 1) * P], xc[:, c, at:at + P], ident)
                    last.then_inc(vec_full, 1)
                    pe.wait_ge(conv_ready, 4 * (b // 2) + 4)
                    t = vec_bank(("G", b))
                    pe.matmul(t[:, 0:256], xc[:, 2, b * S:b * S + P], xc[:, 3, b * S:(b + 1) * S], start=True, stop=True)
                    pe.matmul(t[:, 256:384], xc[:, 2, b * S + P:(b + 1) * S], xc[:, 3, b * S + P:(b + 1) * S],
                              start=True, stop=True).then_inc(vec_full, 1)
                    vec_has("cum")
                    for hf in range(2):
                        t = vec_bank(("bc", b, hf))
                        for h in range(MH):
                            last = pe.transpose(t[:, h * P:(h + 1) * P], cum[:, 2 * b + hf, h:h + 1].broadcast_to([P, P]), ident)
                        last.then_inc(vec_full, 1)
                elif kind == "back":
                    pe.wait_ge(w_ready, b + 1)
                    t = vec_bank(("Y", b))
                    for h in range(MH):
                        r, at = h % 2 * 64, h // 2 * 256
                        pe.matmul(t[r:r + 64, at:at + 256], xdt[:, b % 2 * 2, h * 64:(h + 1) * 64], eL[:, b % 2, h, 0:256], start=True, stop=False)
                        last = pe.matmul(t[r:r + 64, at + P:at + 256], xdt[:, b % 2 * 2 + 1, h * 64:(h + 1) * 64], eL[:, b % 2, h, 256:384],
                                         start=False, stop=True)
                    last.then_inc(vec_full, 1)
                elif kind == "out":
                    pe.wait_ge(gated, b + 1)
                    t = vec_bank(("out0", b))
                    for hf in range(2):
                        for c in range(2):
                            pe.matmul(t[:, hf * P:(hf + 1) * P], yg[:, c, hf * P:(hf + 1) * P], ow2[:, c, :], start=(c == 0), stop=(c == 1))
                    pe.wait_ge(ysq_ready, b + 1)
                    for hf in range(2):
                        for c in range(2):
                            last = pe.matmul(t[:, 256 + hf:257 + hf], ysq[:, c, hf * P:(hf + 1) * P], K["ones"][:, 0:1],
                                             start=(c == 0), stop=(c == 1))
                    last.then_inc(vec_full, 1)
                elif kind == "latent":
                    pe.wait_ge(ln_rows, 4 * 2 + b + 1)
                    t = vec_bank(("uT", 2, b))
                    for hf in range(2):
                        last = pe.transpose(t[:, hf * P:(hf + 1) * P], urow[ROW[2]][:, 2 * b + hf, :], ident)
                    last.then_inc(vec_full, 1)
                elif kind == "sim":
                    n, c, r = b * XH + h, h // 2, h % 2 * 64
                    act_has(("qT", UNIT[2, 2 * b + 1]))
                    banks = [act_bank(("sim", n, 0)), act_bank(("sim", n, 1))]
                    assert for_act.number[("sim", n, 0)] % 2 == 0
                    at = b % 2 * S
                    for kt in range(4):
                        keys = kc[:, h, b * S + kt * P:b * S + (kt + 1) * P] if kt < 2 else kl[:, h, at + (kt - 2) * P:at + (kt - 1) * P]
                        o = banks[kt // 2][:, kt % 2 * 256:(kt % 2 + 1) * 256]
                        pe.matmul(o, keys, q1[:, h, at:at + S], start=True, stop=False)
                        last = pe.matmul(o, keys[r:r + 64, :], q2[r:r + 64, c, at:at + S], start=False, stop=True)
                    last.then_inc(act_full, 2)
                elif kind == "pv":
                    n, c = b * XH + h, h // 2
                    act_has(("sim", n, 1))
                    act_has(("xv", 1, 2 * b + 1))
                    if n == 0:
                        pe.wait_ge(val_ones, 1)
                        pe.wait_ge(vac_mask, 1)
                    t = vec_bank(("pv", n))
                    at = h % 2 * 64
                    for kt in range(4):
                        values_of = vac[:, 2 * b + kt, c, at:at + P] if kt < 2 else val[:, b % 2 * 2 + kt - 2, c, at:at + P]
                        last = pe.matmul(t[:, 0:256], values_of, pT[:, n % 3, kt, :],
                                         start=(kt == 0), stop=(kt == 3))
                    last.then_inc(vec_full, 1)
                elif kind == "result":
                    vec_has(("pv", b * XH + XH - 1))
                    t = vec_bank(("out1", b))
                    for qt in range(2):
                        for c in range(XC):
                            last = pe.matmul(t[:, qt * P:(qt + 1) * P], oT[:, (XC * b + c) % 5, qt * P:(qt + 1) * P], X0["wo"][:, c * P:(c + 1) * P],
                                             start=(c == 0), stop=(c == XC - 1))
                    last.then_inc(vec_full, 1)
                elif kind == "corr_rows":
                    if b == "k" and h == 0:
                        pe.wait_ge(c1_in, 16)
                    corr_rows(b, h)
                elif kind == "corr_vo":
                    act_has(("cr", "v", B - 1))
                    for bp in range(2):
                        t = act_bank(("vo", bp))
                        for i in range(2):
                            for hf in range(2):
                                at = (2 * i + hf) * P
                                last = pe.matmul(t[:, at:at + P], vr[:, hf, 2 * bp + i, :], C1["wo"], start=True, stop=True)
                        last.then_inc(act_full, 1)
                elif kind == "corr_spectra":
                    for f in range(3):
                        spectrum("k", f)
                elif kind == "turn3":
                    pe.wait_ge(ln_rows, 4 * 3 + b + 1)
                    t = vec_bank(("uT", 3, b))
                    for hf in range(2):
                        last = pe.transpose(t[:, hf * P:(hf + 1) * P], urow[ROW[3]][:, 2 * b + hf, :], ident)
                    last.then_inc(vec_full, 1)
                elif kind == "gates":
                    if b == 0:
                        pe.wait_ge(f_in, 16)
                    vec_has(("uT", 3, b))
                    fi, g = act_bank(("fi", b)), act_bank(("g", b))
                    gates = ((fi[:, 0:256], "wf"), (fi[:, 256:512], "wi"), (g[:, 0:256], "wc"))
                    for o, w in gates:
                        pe.matmul(o, F[w], uT[1][:, b, :], start=(w != "wi"), stop=False, skip_group_check=True)
                    pe.wait_ge(cell_ready, b + 1)
                    for k, (o, w) in enumerate(gates):
                        last = pe.matmul(o, uh[:, k, :], cell[:, b % 2, :], start=False, stop=True, skip_group_check=True)
                    last.then_inc(act_full, 2)

            pe.wait_ge(cell_ready, B + 1)
            for p in range(2):
                ps_h = act_bank(("h", p))
                for t in range(2):
                    pe.matmul(ps_h[:, t * 256:(t + 1) * 256], F["wo"], uT[1][:, 2 * p + t, :], start=True, stop=False)
                    last = pe.matmul(ps_h[:, t * 256:(t + 1) * 256], uh[:, 3, :], cell[:, 0, :], start=False, stop=True)
                last.then_inc(act_full, 1)
            for b in range(B):
                act_has(("h", b // 2))
                t = vec_bank(("hrow", b))
                for hf in range(2):
                    last = pe.transpose(t[:, hf * P:(hf + 1) * P], hT[:, b, hf * P:(hf + 1) * P], ident)
                last.then_inc(vec_full, 1)

            pe.wait_ge(wa_ready, 1)
            for p in range(2):
                for b in (2 * p, 2 * p + 1):
                    rows_turn(4, b)
                act_has(("uT", 4, 2 * p + 1))
                for k in range(2):
                    for s, w in enumerate((wa32, wrot)):
                        t = vec_bank(("qk", p, k, s))
                        pe.matmul(t, w[:, k * P:(k + 1) * P], uT[0][:, 2 * p:2 * p + 2, :], start=True, stop=True).then_inc(vec_full, 1)
                for b in (2 * p, 2 * p + 1):
                    t = act_bank(("av", b))
                    for hf in range(2):
                        last = pe.matmul(t[:, hf * P:(hf + 1) * P], uT[0][:, b, hf * P:(hf + 1) * P], wa32[:, 256:384], start=True, stop=True)
                    last.then_inc(act_full, 1)
            pe.wait_ge(h_in, 16)
            pe.wait_ge(b_in, 16)
            for p in range(2):
                for k in range(2):
                    pe.wait_ge(lead_ready, 2 * p + k + 1)
                    pe.wait_ge(rest_ready, 2 * p + k + 1)
                    for j in range(4):
                        t = act_bank(("st", p, k, j)) if k == 0 else vec_bank(("st", p, k, j))
                        for s in range(2):
                            sel = KH[("selq1", "selq2", "selk1", "selk2")[2 * k + s]][:, j * P:(j + 1) * P]
                            last = pe.matmul(t, sel, qh[:, k, s, p * 512:(p + 1) * 512], start=(s == 0), stop=(s == 1))
                        last.then_inc(vec_full if k else act_full, 1)

            for kind, b, i in AORDER:
                n, r, at = 4 * b + i, 32 * i, b * S
                if kind == "row":
                    if n % 4 == 0:
                        act_has(("st", b // 2, 0, 3))
                        vec_has(("st", b // 2, 1, 3))
                    mask = KB["mask_row"].unsqueeze(1)
                    t = vec_bank(("row", b, i, 0)).rearrange("p (j k) -> p j k", j=4)
                    pe.matmul(t, KB["ident"], mask.broadcast_to([P, 4, P]), start=True, stop=False, skip_group_check=True)
                    for j in range(4):
                        last = pe.matmul(t[:, j, :], qst[r:r + 32, 0, j, at:at + P], kst[r:r + 32, j, at:at + P],
                                         start=False, stop=True, skip_group_check=True)
                    last.then_inc(vec_full, 1)
                    for jj in range(2):
                        t = vec_bank(("row", b, i, 1 + jj)).rearrange("p (j k) -> p j k", j=2)
                        pe.matmul(t[:, :, P:S], KB["ident"], mask.broadcast_to([P, 2, P]), start=True, stop=False, skip_group_check=True)
                        for j in range(2):
                            last = pe.matmul(t[:, j, :], qst[r:r + 32, 0, 2 * jj + j, at + P:at + S], kst[r:r + 32, 2 * jj + j, at:at + S],
                                             start=False, stop=True, skip_group_check=True)
                        last.then_inc(vec_full, 1)
                elif kind == "stack":
                    pe.wait_ge(mneg_ready, b + 1)
                    for jj in range(2):
                        t = act_bank(("st2", b, jj)).rearrange("p (j q) -> p j q", j=2)
                        for j in (2 * jj, 2 * jj + 1):
                            o = t[:, j % 2, :]
                            pe.matmul(o, KH["selq1"][:, j * P:(j + 1) * P], qh[:, 0, 0, at:at + S], start=True, stop=False, skip_group_check=True)
                            pe.matmul(o, KH["selq2"][:, j * P:(j + 1) * P], qh[:, 0, 1, at:at + S], start=False, stop=False, skip_group_check=True)
                            for qt in range(2):
                                last = pe.matmul(o[:, qt * P:(qt + 1) * P], mneg[:, b % 2, qt, j, :], KH["ident"], start=False, stop=True,
                                                 skip_group_check=True)
                        last.then_inc(act_full, 1)
                elif kind == "col":
                    if i == 0:
                        act_has(("st2", b, 1))
                    mask = KB["mask_col"].unsqueeze(1)
                    for jj in range(2):
                        t = act_bank(("col", b, i, jj)).rearrange("p (j q) -> p j q", j=2)
                        pe.matmul(t[:, :, 0:P], KB["ident"], mask.broadcast_to([P, 2, P]), start=True, stop=False, skip_group_check=True)
                        for j in range(2):
                            last = pe.matmul(t[:, j, :], kst[r:r + 32, 2 * jj + j, at:at + P], qst[r:r + 32, 1, 2 * jj + j, at:at + S],
                                             start=False, stop=True, skip_group_check=True)
                        last.then_inc(act_full, 1)
                    t = act_bank(("col", b, i, 2)).rearrange("p (j q) -> p j q", j=4)
                    pe.matmul(t, KB["ident"], mask.broadcast_to([P, 4, P]), start=True, stop=False, skip_group_check=True)
                    for j in range(4):
                        last = pe.matmul(t[:, j, :], kst[r:r + 32, j, at + P:at + S], qst[r:r + 32, 1, j, at + P:at + S],
                                         start=False, stop=True, skip_group_check=True)
                    last.then_inc(act_full, 1)
                elif kind == "pv":
                    act_has(("col", b, i, 2))
                    if n == 0:
                        pe.wait_ge(va1_ones, 1)
                    t = act_bank(("apv", b, i))
                    for j in range(4):
                        o, h, prob = t[32 * j:32 * j + 32, 0:S], 4 * j + i, pT1[:, n % 3, :]
                        pe.matmul(o, va1[:, 2 * b, h, :], prob[:, j * S:(j + 1) * S], start=True, stop=False)
                        last = pe.matmul(o[:, P:S], va1[:, 2 * b + 1, h, :], prob[:, 1024 + j * P:1024 + (j + 1) * P], start=False, stop=True)
                    last.then_inc(act_full, 1)
                elif kind == "back":
                    act_has(("apv", b, i))
                    t = vec_bank(("aback", b, i))
                    for qt in range(2):
                        last = pe.transpose(t[:, qt * P:(qt + 1) * P], oc1[:, n % 2, qt * P:(qt + 1) * P], ident)
                    last.then_inc(vec_full, 1)
                elif kind == "turn":
                    vec_has(("aback", b, 3))
                    t = act_bank(("oT1", b))
                    for qt in range(2):
                        last = pe.transpose(t[:, qt * P:(qt + 1) * P], or1[:, b % 2, qt, :], ident)
                    last.then_inc(act_full, 1)
                else:
                    act_has(("oT1", b))
                    t = vec_bank(("out4", b))
                    for qt in range(2):
                        last = pe.matmul(t[:, qt * P:(qt + 1) * P], oT1[:, b % 2, qt * P:(qt + 1) * P], wa32[:, 384:512], start=True, stop=True)
                    last.then_inc(vec_full, 1)

            for b in range(B):
                rows_turn(5, b)
            for b in range(B):
                act_has(("uT", 5, b))
                corr_rows("q", b)
            act_has(("cr", "q", B - 1))
            for f in range(2):
                spectrum("q", f)
            for bp in range(2):
                t = vec_bank(("corr", bp))
                pe.wait_ge(prod_ready, 1)
                for b in range(2):
                    at = (2 * bp + b) * P
                    pe.matmul(t[:, b * S:(b + 1) * S], prod[:, 0, at:at + P], K["idft"][:, 0:S], start=True, stop=False)
                    last = pe.matmul(t[:, b * S:(b + 1) * S], prod[:, 1, at:at + P], K["idft"][:, S:2 * S], start=False, stop=True)
                last.then_inc(vec_full, 1)
            pe.wait_ge(mbd_ready, 1)
            t = act_bank("mix")
            for b in range(B):
                last = pe.matmul(t[:, b * P:(b + 1) * P], mbd[:, b, :, :].rearrange("p h j -> p (h j)"), K["permute"], start=True, stop=True)
            last.then_inc(act_full, 1)
            act_has("mix")
            for b in range(B):
                t = vec_bank(("out5", b))
                for tile in range(2):
                    for hf in range(2):
                        last = pe.matmul(t[:, tile * P:(tile + 1) * P], place[:, b, tile, hf, :], vo[:, b, hf * P:(hf + 1) * P],
                                         start=(hf == 0), stop=(hf == 1))
                last.then_inc(vec_full, 1)

            pe.wait_ge(e_in, 16)
            for b in range(B):
                rows_turn(6, b)
            act_has(("uT", 6, B - 1))
            t = act_bank("gl")
            for tile in range(NT):
                last = pe.matmul(t[:, tile * E:(tile + 1) * E], uT[0][:, tile // 2, tile % 2 * P:(tile % 2 + 1) * P], G["gate"], start=True, stop=True)
            last.then_inc(act_full, 1)
            for kind, p, c in EORDER:
                if kind == "turn":
                    pe.wait_ge(comb_ready, 1)
                    t = vec_bank("cbT").bitcast(BF16)
                    for tile in range(NT):
                        last = pe.transpose(t[0:48, tile * P:(tile + 1) * P], comb3[:, tile, :, :].rearrange("p s e -> p (s e)"), KB["ident"])
                    last.then_inc(vec_full, 1)
                elif kind == "up":
                    w1, w3 = (G["e_win"][:, c * P:(c + 1) * P], G["e_vin"][:, c * P:(c + 1) * P]) if c < 8 else (G["ws_in"], G["vs_in"])
                    t = act_bank(("hin", p, c))
                    pe.matmul(t, w1, uT[0][:, 2 * p:2 * p + 2, :], start=True, stop=True).then_inc(act_full, 1)
                    t = vec_bank(("vin", p, c))
                    pe.matmul(t, w3, uT[0][:, 2 * p:2 * p + 2, :], start=True, stop=True).then_inc(vec_full, 1)
                    if c < 8:
                        vec_has("cbT")
                        t = vec_bank(("cw", p, c))
                        pe.matmul(t, KB["expand"][0:48, c * P:(c + 1) * P], combT[0:48, p * 512:(p + 1) * 512], start=True, stop=True)\
                          .then_inc(vec_full, 1)
                else:
                    b = c
                    vec_has(("cw", b // 2, 7))
                    t = vec_bank(("out6", b))
                    for hf in range(2):
                        at = b * S + hf * P
                        for c in range(HC):
                            last = pe.matmul(t[:, hf * P:(hf + 1) * P], hid[:, c, at:at + P], G["w_out"][:, c * P:(c + 1) * P],
                                             start=(c == 0), stop=(c == HC - 1))
                    last.then_inc(vec_full, 1)

        @block.scalar
        def _(act):
            steps = 0

            def after(ins):
                nonlocal steps
                steps += 1
                ins.then_inc(act_step, 1)
                act.wait_ge(act_step, steps)

            def full(key):
                act.wait_ge(act_full, for_act.number[key] + 1)

            def vec_bank_full(key):
                act.wait_ge(vec_full, for_vec.number[key] + 1)

            def vec_bank_read(key):
                act.wait_ge(vec_free, for_vec.number[key] + 1)

            def copy_out(key, dst, src, scale=1.0):
                full(key)
                act.activation(dst, src, ACT.Copy, scale=scale).then_inc(act_free, 1)

            def copy_uT(k, b):
                copy_out(("uT", k, b), uT[ROW[k]][:, b, :], pbank(for_act, ("uT", k, b), S))

            def values(s, tile):
                key = ("xv", s, tile)
                full(key)
                dst = (val[:, tile % 4, :, :] if s else vac[:, tile, :, :]).rearrange("p c (s d) -> p c s d", s=3)[:, :, 0::2, :]
                act.activation(dst, pbank(for_act, key).rearrange("p (c s d) -> p c s d", c=XC, s=2), ACT.Copy,
                               scale=maskf[:, tile:tile + 1] if s == 0 else 1.0).then_inc(act_free, 1)

            def head_square(s, tile):
                u = UNIT[s, tile]
                vec_bank_full(("kr", u))
                if u >= 2:
                    act.wait_ge(parts_ready, u - 1)
                act.activation(sqr[:, u % 2, :], pbank(for_vec, ("kr", u)), ACT.Square).then_inc(sq_ready, 1)

            def head_lead(s, tile):
                u = UNIT[s, tile]
                if s == 2:
                    act.wait_ge(q_scaled, tile + 1)
                else:
                    vec_bank_read(("kr", u))
                if u >= 2:
                    act.wait_ge(act_full, for_act.number[("qT", u - 2)] + 1 if ("qT", u - 2) in for_act.number else for_act.number[("kT", u - 2)] + 1)
                if s == 2:
                    rows = sqr[:, u % 2, :].rearrange("p (h d) -> p h d", h=XH).unsqueeze(2).broadcast_to([P, XH, 2, XD])
                    dst = parts[:, u % 2, 0:1024].rearrange("p (h s d) -> p h s d", h=XH, s=2)
                else:
                    rows = sqr[:, u % 2, :].rearrange("p (c s d) -> p c s d", c=XC, s=2)
                    dst = parts[:, u % 2, 0:1024].rearrange("p (c s d) -> p c s d", c=XC, s=4)[:, :, 0::3, :]
                act.activation(dst, rows, ACT.Copy).then_inc(lead_parts, 1)

            def head_turned(s, tile):
                u = UNIT[s, tile]
                at = (tile % 4 if s else tile) * P
                copy_out(("kT", u), (kc, kl, q1)[s][:, :, at:at + P], pbank(for_act, ("kT", u)).bitcast(F16).rearrange("p (h t) -> p h t", h=XH))
                if s == 2:
                    copy_out(("qT", u), q2[:, :, at:at + P], pbank(for_act, ("qT", u), 256).bitcast(F16).rearrange("p (c t) -> p c t", c=XC))

            def corr_rows(name, b):
                copy_out(("cr", name, b), {"q": qr, "k": kr, "v": vr}[name][:, :, b, :],
                         pbank(for_act, ("cr", name, b), 256).rearrange("p (h n) -> p h n", h=2))

            for b in range(B):
                copy_uT(0, b)
            act.wait_ge(m_in, 16)
            act.activation(ea, M["a_log"], ACT.Exp).then_inc(ea_ready, 1)
            act.wait_ge(dt_abs, 1)
            after(act.activation(dte, dta, ACT.Exp, scale=-1.0))
            act.activation(dtl, dte, ACT.Ln, bias=1.0).then_inc(dt_log, 1)

            waiting = []

            def conv_silu():
                p, c = waiting.pop(0)
                vec_bank_read(("in", p, c))
                o = xc[:, c - 2, p * 512:(p + 1) * 512]
                act.activation(o, o, ACT.Silu).then_inc(conv_ready, 1)

            for kind, b, c in ORDER:
                h = c
                if kind == "in" and c >= 2:
                    key, k = ("in", b, c), c - 2
                    vec_bank_full(key)
                    act.activation(xc[:, k, b * 512:(b + 1) * 512], pbank(for_vec, key), ACT.Identity, bias=M["conv_b"][:, k:k + 1],
                                   scale=M["conv_w"][:, 4 * k + 3:4 * k + 4]).then_inc(tap_ready, 1)
                    waiting.append((b, c))
                    if len(waiting) > 2:
                        conv_silu()
                elif kind == "in":
                    full(("in", b, c))
                    act.activation(zs[:, c, b * 512:(b + 1) * 512], pbank(for_act, ("in", b, c)), ACT.Silu).then_inc(act_free, 1)
                    if waiting:
                        conv_silu()
                elif kind == "context":
                    copy_out(("cT", b), cT[:, b, :], pbank(for_act, ("cT", b), S))
                    act.wait_ge(xw_in, 16)
                    full(("uT", 1, b))
                    act.activation(cnT[:, b, :], pbank(for_act, ("uT", 1, b), S), ACT.Identity, bias=X0["lnx_b"], scale=X0["lnx_w"])\
                       .then_inc(act_free, 1)
                elif kind == "value":
                    if b == 0 and c == 0:
                        act.wait_ge(vac_mask, 1)
                    values(b, c)
                elif kind == "head":
                    head_square(b, c)
                elif kind == "parts":
                    head_lead(b, c)
                elif kind == "turn":
                    head_turned(b, c)
                elif kind == "front":
                    vec_bank_read(("bc", b, 1))
                    act.activation(eL[:, b % 2, :, :], eL[:, b % 2, :, :], ACT.Exp).then_inc(decay_ready, 1)
                elif kind == "back":
                    act.wait_ge(gated, b + 1)
                    if b >= 1:
                        vec_bank_full(("out0", b - 1))
                    act.activation(ysq, yg, ACT.Square).then_inc(ysq_ready, 1)
                elif kind == "sim":
                    n = b * XH + h
                    if n == 0:
                        act.wait_ge(shift_ready, 1)
                    act.wait_ge(act_full, for_act.number[("sim", n, 1)] + 1)
                    if n >= 3:
                        vec_bank_full(("pv", n - 3))
                    act.activation(pT[:, n % 3, :, :], pbank(for_act, ("sim", n, 0), 1024).rearrange("p (k q) -> p k q", k=4), ACT.Exp,
                                   bias=shift[:, 1:2], scale=8.0 / 1024).then_inc(act_free, 2)
                elif kind == "pv":
                    n = b * XH + h
                    vec_bank_full(("pv", n))
                    if n >= 4:
                        vec_bank_read(("pv", n - 4 | 1))
                    r = h % 2 * 64
                    act.activation(den[r:r + 64, n // 2 % 2, :], pbank(for_vec, ("pv", n), S)[64 - r:128 - r, :], ACT.Copy).then_inc(den_ready, 1)
                elif kind == "corr_rows":
                    corr_rows(b, h)
                elif kind == "corr_vo":
                    for bp in range(2):
                        copy_out(("vo", bp), vo[:, 2 * bp:2 * bp + 2, :], pbank(for_act, ("vo", bp)).rearrange("p (b n) -> p b n", b=2))
                elif kind == "corr_spectra":
                    for f in range(3):
                        copy_out(("fk", f), pr[:, f, :], pbank(for_act, ("fk", f)))
                elif kind == "gates":
                    if b == 0:
                        act.wait_ge(halves_ready, 1)
                    full(("g", b))
                    if b >= 2:
                        act.wait_ge(cell_ready, b)
                    fi = pbank(for_act, ("fi", b))
                    act.activation(gat[:, b % 2, 0, :], fi[:, 0:256], ACT.Tanh, bias=halfb[:, 0:1], scale=0.5)
                    act.activation(gat[:, b % 2, 1, :], fi[:, 256:512], ACT.Tanh, bias=halfb[:, 1:2], scale=0.5).then_inc(act_free, 1)
                    act.activation(gat[:, b % 2, 2, :], pbank(for_act, ("g", b), 256), ACT.Tanh, bias=F["bc"]).then_inc(act_free, 1)

            for p in range(2):
                full(("h", p))
                act.activation(hT[:, 2 * p:2 * p + 2, :], pbank(for_act, ("h", p)).rearrange("p (t n) -> p t n", t=2), ACT.Tanh,
                               bias=F["bo"]).then_inc(act_free, 1)

            for p in range(2):
                for b in (2 * p, 2 * p + 1):
                    copy_uT(4, b)
                for b in (2 * p, 2 * p + 1):
                    copy_out(("av", b), va1[:, 2 * b:2 * b + 2, :, 0:AD], pbank(for_act, ("av", b), 256).rearrange("p (t h d) -> p t h d", t=2, h=AH))
                for k in range(2):
                    act.wait_ge(rope_ready, 2 * p + k + 1)
                    act.activation(qh[:, k, 0, p * 512:(p + 1) * 512], rot[:, k, 0, :], ACT.Copy).then_inc(lead_ready, 1)
            for p in range(2):
                for j in range(4):
                    copy_out(("st", p, 0, j), qst[:, 0, j, p * 512:(p + 1) * 512], pbank(for_act, ("st", p, 0, j)))
            for kind, b, i in AORDER:
                n = 4 * b + i
                if kind == "stack":
                    for jj in range(2):
                        copy_out(("st2", b, jj), qst[:, 1, 2 * jj:2 * jj + 2, b * S:(b + 1) * S],
                                 pbank(for_act, ("st2", b, jj)).rearrange("p (j q) -> p j q", j=2))
                elif kind == "col":
                    for part in range(3):
                        key = ("col", b, i, part)
                        full(key)
                        act.activation(pT1[:, n % 3, part * 512:(part + 1) * 512], pbank(for_act, key), ACT.Exp, scale=1.0 / 11.3125)\
                           .then_inc(act_free, 1)
                elif kind == "pv":
                    if n >= 2:
                        vec_bank_full(("aback", (n - 2) // 4, (n - 2) % 4))
                    copy_out(("apv", b, i), oc1[:, n % 2, :], pbank(for_act, ("apv", b, i), 256))
                elif kind == "turn":
                    if b >= 2:
                        vec_bank_full(("out4", b - 2))
                    copy_out(("oT1", b), oT1[:, b % 2, :], pbank(for_act, ("oT1", b), 256))

            for b in range(B):
                copy_uT(5, b)
            for b in range(B):
                corr_rows("q", b)
            act.wait_ge(corr_diff, 1)
            act.activation(tope[:, :, 0:TOPC], delta[:, :, 0:TOPC], ACT.Exp).then_inc(corr_exp, 1)
            full("mix")
            act.wait_ge(place_zero, 1)
            mix = pbank(for_act, "mix").rearrange("p (b t g) -> p b t g", b=B, t=2)
            for hf in range(2):
                last = act.activation(place[:, :, :, hf, hf::2], mix, ACT.Copy)
            last.then_inc(act_free, 1)

            for b in range(B):
                copy_uT(6, b)
            full("gl")
            act.activation(gex, pbank(for_act, "gl", NT * E).rearrange("p (t e) -> p t e", t=NT), ACT.Exp, scale=-1.0).then_inc(act_free, 1)
            used = []
            for kind, p, c in EORDER:
                if kind == "up":
                    key = ("hin", p, c)
                    full(key)
                    if len(used) >= 2:
                        vec_bank_read(used[-2])
                    act.activation(sil[:, len(used) % 2, :], pbank(for_act, key), ACT.Silu).then_inc(act_free, 1)
                    used.append(("cw" if c < 8 else "vin", p, c))

        @block.vector
        def _(vec):
            steps = 0

            def after(ins):
                nonlocal steps
                steps += 1
                ins.then_inc(vec_step, 1)
                vec.wait_ge(vec_step, steps)

            def full(key):
                vec.wait_ge(vec_full, for_vec.number[key] + 1)

            def own(key):
                vec.wait_ge(vec_free, for_vec.number[key] + 1)

            def act_read(key):
                vec.wait_ge(act_free, for_act.number[key] + 1)

            def var(k, b, src):
                vec.bn_stats(stats[:, k, 2 * b, :], src[:, 2 * b, :])
                after(vec.bn_stats(stats[:, k, 2 * b + 1, :], src[:, 2 * b + 1, :]))
                vec.bn_aggr(mv[:, k, 2 * b, :], stats[:, k, 2 * b, :])
                vec.bn_aggr(mv[:, k, 2 * b + 1, :], stats[:, k, 2 * b + 1, :]).then_inc(ln_var, 1)

            def rows(k, b, src):
                vec.wait_ge(ln_rstd, 4 * k + b + 1)
                for t in (2 * b, 2 * b + 1):
                    last = vec.tensor_scalar(urow[ROW[k]][:, t, :], src[:, t, :], mv[:, k, t, 0:1], rstd[:, k, t:t + 1],
                                             ALU.subtract, ALU.mult)
                last.then_inc(ln_rows, 1)

            def residual(key, b):
                full(key)
                xb = x[:, 2 * b:2 * b + 2, :]
                vec.tensor_tensor(xb, xb, pbank(for_vec, key, 256).rearrange("p (t n) -> p t n", t=2), ALU.add).then_inc(vec_free, 1)
                own(key)

            vec.wait_ge(x_in, 16)
            for b in range(B):
                var(0, b, x)
            vec.wait_ge(c_in, 16)
            for b in range(B):
                rows(0, b, x)
            for b in range(B):
                var(1, b, cx)
            vec.wait_ge(m_in, 16)
            full("dt")
            vec.tensor_tensor(dtx, pbank(for_vec, "dt", 32).rearrange("p (t h) -> p t h", h=MH),
                              M["dt_bias"].unsqueeze(1).broadcast_to([P, NT, MH]), ALU.add).then_inc(vec_free, 1)
            own("dt")
            vec.scalar_tensor_tensor(out=dta, in0=dtx, scalar=-1.0, in1=dtx, op0=ALU.mult, op1=ALU.max).then_inc(dt_abs, 1)
            for b in range(B):
                rows(1, b, cx)
            for c in range(2):
                vec.tensor_scalar(ow2[:, c, :], M["out_w"][:, c * P:(c + 1) * P], M["norm_w"][:, c:c + 1], None, ALU.mult)
            vec.wait_ge(dt_log, 1)
            after(vec.scalar_tensor_tensor(out=dt, in0=dtx, scalar=0.0, in1=dtl, op0=ALU.max, op1=ALU.add))
            vec.wait_ge(ea_ready, 1)
            vec.scalar_tensor_tensor(out=da, in0=dt, scalar=-1.0, in1=ea.unsqueeze(1).broadcast_to([P, NT, MH]),
                                     op0=ALU.mult, op1=ALU.mult).then_inc(da_ready, 1)
            def head_sum(s, tile):
                u = UNIT[s, tile]
                vec.wait_ge(sq_ready, u + 1)
                vec.tensor_reduce(ssq[:, s, tile, :], sqr[:, u % 2, :].rearrange("p (h d) -> p h d", h=XH), AX.X, ALU.add).then_inc(ssq_ready, 1)

            def head_norm(s, tile):
                u = UNIT[s, tile]
                vec.wait_ge(rnk_ready, u + 1)
                full(("kr", u))
                row = sqr[:, u % 2, :].rearrange("p (h d) -> p h d", h=XH)
                vec.tensor_tensor(row, pbank(for_vec, ("kr", u)).rearrange("p (h d) -> p h d", h=XH),
                                  rnk[:, s, tile, :].unsqueeze(2).broadcast_to([P, XH, XD]), ALU.mult).then_inc(vec_free, 1)
                if s == 2:
                    own(("kr", u))
                    vec.tensor_tensor(row, row, qks[:].unsqueeze(1).broadcast_to([P, XH, XD]), ALU.mult).then_inc(q_scaled, 1)

            def head_rest(s, tile):
                u = UNIT[s, tile]
                vec.wait_ge(lead_parts, u + 1)
                if s == 2:
                    lead = parts[:, u % 2, 0:1024].rearrange("p (h s d) -> p h s d", h=XH, s=2)[:, :, 0, :]
                    vec.tensor_tensor(parts[:, u % 2, 1024:1536].rearrange("p (h d) -> p h d", h=XH),
                                      sqr[:, u % 2, :].rearrange("p (h d) -> p h d", h=XH), lead, ALU.subtract).then_inc(parts_ready, 1)
                else:
                    four = parts[:, u % 2, 0:1024].rearrange("p (c s d) -> p c s d", c=XC, s=4)
                    vec.tensor_tensor(four[:, :, 1:3, :], sqr[:, u % 2, :].rearrange("p (c s d) -> p c s d", c=XC, s=2), four[:, :, 0::3, :],
                                      ALU.subtract).then_inc(parts_ready, 1)

            vec.wait_ge(xw_in, 16)
            after(vec.tensor_tensor(qks[:], X0["q_scale_row"], X0["k_scale_row"], ALU.mult))
            after(vec.tensor_reduce(shift[:, 0:1], qks[:], AX.X, ALU.max, apply_absolute_value=True))
            vec.tensor_scalar(shift[:, 1:2], shift[:, 0:1], -8.0, None, ALU.mult).then_inc(shift_ready, 1)
            vec.wait_ge(k_in, 16)
            vec.tensor_copy(ident16, ident).then_inc(ident16_set, 1)
            taps = 0
            for kind, b, c in ORDER:
                h = c
                if kind == "in" and c >= 2:
                    k, key = c - 2, ("in", b, c)
                    taps += 1
                    vec.wait_ge(tap_ready, taps)
                    full(key)
                    src = pbank(for_vec, key).rearrange("p (b t) -> p b t", b=2)
                    dst = xc[:, k, b * 512:(b + 1) * 512].rearrange("p (b t) -> p b t", b=2)
                    for j in (1, 2):
                        after(vec.scalar_tensor_tensor(out=dst[:, :, j:], in0=src[:, :, 0:S - j], scalar=M["conv_w"][:, 4 * k + 3 - j:4 * k + 4 - j],
                                                       in1=dst[:, :, j:], op0=ALU.mult, op1=ALU.add))
                    vec.scalar_tensor_tensor(out=dst[:, :, 3:], in0=src[:, :, 0:S - 3], scalar=M["conv_w"][:, 4 * k:4 * k + 1],
                                             in1=dst[:, :, 3:], op0=ALU.mult, op1=ALU.add).then_inc(vec_free, 1)
                elif kind == "cum":
                    full("cum")
                    c32 = pbank(for_vec, "cum", 32).rearrange("p (t h) -> p t h", h=MH)
                    vec.tensor_copy(cum, c32).then_inc(vec_free, 1)
                    own("cum")
                elif kind == "head":
                    head_sum(b, c)
                elif kind == "norm":
                    head_norm(b, c)
                elif kind == "parts":
                    head_rest(b, c)
                elif kind == "front":
                    v = b % 2
                    full(("xrow", b))
                    vec.tensor_tensor(xdt[:, 2 * v:2 * v + 2, :].rearrange("p t (h n) -> p t h n", h=MH),
                                      pbank(for_vec, ("xrow", b)).rearrange("p (t h n) -> p t h n", t=2, h=MH),
                                      dt[:, 2 * b:2 * b + 2, :].unsqueeze(3).broadcast_to([P, 2, MH, 64]), ALU.mult).then_inc(vec_free, 1)
                    full(("G", b))
                    if b >= 1:
                        vec.wait_ge(w_ready, b)
                    vec.tensor_tensor(gm, pbank(for_vec, ("G", b), 384), K["gmask"], ALU.mult).then_inc(vec_free, 1)
                    for hf in range(2):
                        full(("bc", b, hf))
                        sums = pbank(for_vec, ("bc", b, hf)).rearrange("p (h l) -> p h l", h=MH)
                        if hf == 1:
                            vec.tensor_tensor(eL[:, v, :, P:256], sums, cum[:, 2 * b, :].unsqueeze(2).broadcast_to([P, MH, P]), ALU.subtract)
                        for h in range(MH):
                            last = vec.tensor_scalar(eL[:, v, h, 256 * hf:256 * hf + P], sums[:, h, :], cum[:, 2 * b + hf, h:h + 1], 0.0,
                                                     ALU.subtract, ALU.min)
                        last.then_inc(vec_free, 1)
                elif kind == "decay":
                    vec.wait_ge(decay_ready, b + 1)
                    v = b % 2
                    vec.tensor_tensor(eL[:, v, :, :], eL[:, v, :, :], gm.unsqueeze(1).broadcast_to([P, MH, 384]), ALU.mult)\
                       .then_inc(w_ready, 1)
                elif kind == "back":
                    key = ("Y", b)
                    full(key)
                    for c in range(2):
                        last = vec.scalar_tensor_tensor(out=yg[:, c, :], in0=xc[:, c, b * S:(b + 1) * S], scalar=M["skip"][:, c:c + 1],
                                                        in1=pbank(for_vec, key)[:, c * S:(c + 1) * S], op0=ALU.mult, op1=ALU.add)
                    last.then_inc(vec_free, 1)
                    own(key)
                    vec.tensor_tensor(yg, yg, zs[:, :, b * S:(b + 1) * S], ALU.mult).then_inc(gated, 1)
                elif kind == "out":
                    key = ("out0", b)
                    full(key)
                    vec.tensor_scalar(msq[:, 2 * b:2 * b + 2], pbank(for_vec, key)[:, 256:258], 1.0 / 256, EPS, ALU.mult, ALU.add).then_inc(msq_ready, 1)
                    vec.wait_ge(rms_ready, b + 1)
                    for t in range(2):
                        xb = x[:, 2 * b + t, :]
                        last = vec.scalar_tensor_tensor(out=xb, in0=pbank(for_vec, key)[:, t * P:(t + 1) * P], scalar=rms[:, 2 * b + t:2 * b + t + 1],
                                                        in1=xb, op0=ALU.mult, op1=ALU.add)
                    last.then_inc(vec_free, 1)
                    own(key)
                    var(2, b, x)
                elif kind == "rows2":
                    rows(2, b, x)
                elif kind == "halves":
                    vec.wait_ge(f_in, 16)
                    for g, w in enumerate(("uf", "ui", "uc", "uo")):
                        vec.tensor_scalar(uh[:, g, :], F[w], 0.5, None, ALU.mult)
                    vec.tensor_scalar(halfb[:, 0:1], F["bf"], 0.5, None, ALU.mult)
                    vec.tensor_scalar(halfb[:, 1:2], F["bi"], 0.5, None, ALU.mult).then_inc(halves_ready, 1)
                    vec.tensor_scalar(cell[:, 0, :], F["in_c"].broadcast_to([P, 256]), 2.0, None, ALU.mult).then_inc(cell_ready, 1)
                    vec.wait_ge(cell_ready, 1)
                elif kind == "latent":
                    key = ("uT", 2, b)
                    full(key)
                    vec.tensor_scalar(uT[0][:, b, :], pbank(for_vec, key, S), X0["lnl_w"], X0["lnl_b"], ALU.mult, ALU.add).then_inc(vec_free, 1)
                elif kind == "pv" and h % 2:
                    n, v = b * XH + h, h // 2 % 2
                    vec.wait_ge(den_ready, n + 1)
                    full(("pv", n))
                    if n > 1:
                        own(("pv", n - 2))
                    after(vec.reciprocal(rec, den[:, v, :]))
                    for r in (0, 64):
                        vec.tensor_tensor(oT[r:r + 64, (XC * b + h // 2) % 5, :], pbank(for_vec, ("pv", n - 1 + r // 64), S)[r:r + 64, :],
                                          rec[r:r + 64, :], ALU.mult).then_inc(vec_free, 1)
                elif kind == "result":
                    key = ("out1", b)
                    full(key)
                    o = pbank(for_vec, key, 256).rearrange("p (q n) -> p q n", q=2)
                    vec.bn_stats(ostat[:, 2 * b, :], o[:, 0, :])
                    after(vec.bn_stats(ostat[:, 2 * b + 1, :], o[:, 1, :]))
                    vec.bn_aggr(omv[:, 2 * b, :], ostat[:, 2 * b, :])
                    vec.bn_aggr(omv[:, 2 * b + 1, :], ostat[:, 2 * b + 1, :]).then_inc(ovar_ready, 1)
                    vec.wait_ge(orstd_ready, b + 1)
                    for q in range(2):
                        last = vec.tensor_scalar(on[:, q, :], o[:, q, :], omv[:, 2 * b + q, 0:1], ort[:, 1, 2 * b + q:2 * b + q + 1],
                                                 ALU.subtract, ALU.mult)
                    last.then_inc(vec_free, 1)
                    own(key)
                    xb = x[:, 2 * b:2 * b + 2, :]
                    after(vec.tensor_tensor(on, on, X0["lno_w"].unsqueeze(1).broadcast_to([P, 2, P]), ALU.mult))
                    after(vec.tensor_tensor(on, on, X0["lno_b"].unsqueeze(1).broadcast_to([P, 2, P]), ALU.add))
                    after(vec.tensor_tensor(xb, xb, on, ALU.add))
                    var(3, b, x)
                elif kind == "rows3":
                    rows(3, b, x)
                elif kind == "turn3":
                    key = ("uT", 3, b)
                    full(key)
                    vec.tensor_copy(uT[1][:, b, :], pbank(for_vec, key, S)).then_inc(vec_free, 1)
                elif kind == "cell":
                    act_read(("g", b))
                    g = gat[:, b % 2]
                    vec.scalar_tensor_tensor(out=mixa, in0=g[:, 0, :], scalar=1.0, in1=cell[:, b % 2, :], op0=ALU.add, op1=ALU.mult)
                    after(vec.scalar_tensor_tensor(out=mixb, in0=g[:, 1, :], scalar=1.0, in1=g[:, 2, :], op0=ALU.add, op1=ALU.mult))
                    vec.scalar_tensor_tensor(out=cell[:, (b + 1) % 2, :], in0=mixa, scalar=0.5, in1=mixb, op0=ALU.mult, op1=ALU.add)\
                       .then_inc(cell_ready, 1)
                    vec.wait_ge(cell_ready, b + 2)

            for b in range(B):
                residual(("hrow", b), b)
                var(4, b, x)

            vec.wait_ge(a_in, 16)
            vec.tensor_copy(wa32, w_a)
            turned, plain = wrot.rearrange("p (n s) -> p n s", s=2), w_a[:, 0:256].rearrange("p (n s) -> p n s", s=2)
            vec.tensor_scalar(turned[:, :, 0], plain[:, :, 1], -1.0, None, ALU.mult)
            vec.tensor_copy(turned[:, :, 1], plain[:, :, 0]).then_inc(wa_ready, 1)
            for b in range(B):
                rows(4, b, x)
            vec.wait_ge(r_in, 16)
            for p in range(2):
                for k in range(2):
                    if p == 1:
                        vec.wait_ge(rest_ready, k + 1)
                    for s, table in enumerate((R["cos"], R["sin"])):
                        key = ("qk", p, k, s)
                        full(key)
                        vec.tensor_tensor(rot[:, k, s, :].rearrange("p (b t) -> p b t", b=2), pbank(for_vec, key).rearrange("p (b t) -> p b t", b=2),
                                          table.unsqueeze(1).broadcast_to([P, 2, S]), ALU.mult).then_inc(vec_free, 1)
                    own(("qk", p, k, 1))
                    vec.tensor_tensor(rot[:, k, 0, :], rot[:, k, 0, :], rot[:, k, 1, :], ALU.add).then_inc(rope_ready, 1)
            for p in range(2):
                for j in range(4):
                    full(("st", p, 1, j))
                    vec.tensor_scalar(kst[:, j, p * 512:(p + 1) * 512], pbank(for_vec, ("st", p, 1, j)), K["sixteen"], None, ALU.add).then_inc(vec_free, 1)
            vec.wait_ge(mneg_zero, 1)
            for kind, b, i in AORDER:
                n = 4 * b + i
                if kind == "row":
                    for part in range(3):
                        key, heads = ("row", b, i, part), (4, 2, 2)[part]
                        full(key)
                        dst = mx[:, b, 0, i, :] if part == 0 else mx[:, b, 1, i, 2 * part - 2:2 * part]
                        vec.tensor_reduce(dst, pbank(for_vec, key).rearrange("p (j k) -> p j k", j=heads), AX.X, ALU.max).then_inc(vec_free, 1)
                    if i == 3:
                        own(key)
                        if b >= 2:
                            vec.wait_ge(act_full, for_act.number[("st2", b - 2, 1)] + 1)
                        for q in range(2):
                            last = vec.tensor_scalar(mneg[:, b % 2, q, :, 24::32], mx[:, b, q, :, :].rearrange("p i j -> p j i"),
                                                     -1.0 / 16, None, ALU.mult)
                        last.then_inc(mneg_ready, 1)
                elif kind == "back":
                    key = ("aback", b, i)
                    full(key)
                    t = pbank(for_vec, key, 256).rearrange("p (q j n) -> p q j n", q=2, j=4)
                    d = rec1[:, b, :, 4 * i:4 * i + 4].unsqueeze(3)
                    after(vec.reciprocal(d, t[:, :, :, AD:AD + 1]))
                    o = or1[:, b % 2, :, :].rearrange("p q (j i d) -> p q j i d", j=4, i=4)[:, :, :, i, :]
                    vec.tensor_tensor(o, t[:, :, :, 0:AD], d.broadcast_to([P, 2, 4, AD]), ALU.mult).then_inc(vec_free, 1)
                elif kind == "out":
                    residual(("out4", b), b)
                    var(5, b, x)

            for b in range(B):
                rows(5, b, x)
            act_read(("fk", 2))
            full(("fq", 0))
            full(("fq", 1))
            aq, bq = pbank(for_vec, ("fq", 0)), pbank(for_vec, ("fq", 1))
            vec.tensor_tensor(sab[:, 0, :], aq, pr[:, 0, :], ALU.mult)
            after(vec.scalar_tensor_tensor(out=sab[:, 1, :], in0=bq, scalar=K["keep"], in1=pr[:, 1, :], op0=ALU.mult, op1=ALU.mult))
            after(vec.tensor_tensor(prod[:, 0, :], sab[:, 0, :], sab[:, 1, :], ALU.add))
            vec.scalar_tensor_tensor(out=sab[:, 0, :], in0=aq, scalar=K["keep"], in1=pr[:, 1, :], op0=ALU.mult, op1=ALU.mult).then_inc(vec_free, 1)
            vec.tensor_tensor(sab[:, 1, :], bq, pr[:, 2, :], ALU.mult).then_inc(vec_free, 1)
            own(("fq", 1))
            vec.tensor_tensor(prod[:, 1, :], sab[:, 1, :], sab[:, 0, :], ALU.subtract).then_inc(prod_ready, 1)
            for bp in range(2):
                key = ("corr", bp)
                full(key)
                for b in (2 * bp, 2 * bp + 1):
                    c = pbank(for_vec, key)[:, b % 2 * S:(b % 2 + 1) * S]
                    after(vec.max(top[:, b, :], c))
                    last = vec.max_index(topi[:, b, :], top[:, b, :], c)
                last.then_inc(vec_free, 1)
            own(("corr", 1))
            vec.tensor_tensor(delta[:, :, 0:TOPC], top[:, :, 0:TOPC], top[:, :, 0:1].broadcast_to([P, B, TOPC]), ALU.subtract).then_inc(corr_diff, 1)
            after(vec.tensor_scalar(delm, topi, 7, None, ALU.bitwise_and))
            after(vec.tensor_copy(delf, delm))
            after(vec.tensor_tensor(hit, delf[:, :, 0:TOPC].unsqueeze(3).broadcast_to([P, B, TOPC, 8]),
                                    K["jmod"].unsqueeze(1).unsqueeze(1).broadcast_to([P, B, TOPC, 8]), ALU.is_equal))
            vec.wait_ge(corr_exp, 1)
            after(vec.tensor_reduce(tsum, tope[:, :, 0:TOPC], AX.X, ALU.add))
            vec.reciprocal(trec, tsum)
            after(vec.tensor_tensor(hitw, hit, tope[:, :, 0:TOPC].unsqueeze(3).broadcast_to([P, B, TOPC, 8]), ALU.mult))
            after(vec.tensor_reduce(roll, hitw.rearrange("p b k j -> p b j k"), AX.X, ALU.add))
            after(vec.tensor_tensor(roll, roll, trec.unsqueeze(2).broadcast_to([P, B, 8]), ALU.mult))
            for b in range(B):
                last = vec.tensor_tensor(mbd[:, b, :, :], roll[:, b, :].unsqueeze(1).broadcast_to([P, 16, 8]),
                                         K["bd"].rearrange("p (h j) -> p h j", h=16), ALU.mult)
            last.then_inc(mbd_ready, 1)
            for b in range(B):
                residual(("out5", b), b)
                var(6, b, x)

            for b in range(B):
                rows(6, b, x)
            act_read("gl")
            after(vec.tensor_scalar(gde, gex, 1.0, None, ALU.add))
            vec.wait_ge(gpad_set, 1)
            after(vec.reciprocal(gpad[:, :, 0:E], gde))
            for t in range(NT):
                last = vec.max(gtop[:, t, :], gpad[:, t, :])
            after(last)
            vec.tensor_copy(gfind[:, :, 0:TOPE], gtop[:, :, 0:TOPE])
            after(vec.tensor_reduce(gsum, gtop[:, :, 0:TOPE], AX.X, ALU.add))
            for t in range(NT):
                vec.match_replace(grep[:, t, :], gfind[:, t, :], gpad[:, t, :], 0.0)
            after(vec.reciprocal(grec, gsum))
            after(vec.tensor_tensor(comb, gpad[:, :, 0:E], grep[:, :, 0:E], ALU.subtract))
            after(vec.tensor_tensor(comb, comb, grec.unsqueeze(2).broadcast_to([P, NT, E]), ALU.mult))
            after(vec.tensor_copy(comb3[:, :, 0, :], comb))
            after(vec.tensor_tensor(comr[:, 0], comb, comb3[:, :, 0, :], ALU.subtract))
            after(vec.tensor_copy(comb3[:, :, 1, :], comr[:, 0]))
            after(vec.tensor_tensor(comr[:, 1], comr[:, 0], comb3[:, :, 1, :], ALU.subtract))
            vec.tensor_copy(comb3[:, :, 2, :], comr[:, 1]).then_inc(comb_ready, 1)
            n = 0
            for kind, p, c in EORDER:
                if kind == "turn":
                    full("cbT")
                    vec.tensor_copy(combT[0:48, :], pbank(for_vec, "cbT").bitcast(BF16)[0:48, :]).then_inc(vec_free, 1)
                elif kind == "up":
                    o = hid[:, c, p * 512:(p + 1) * 512]
                    full(("vin", p, c))
                    act_read(("hin", p, c))
                    if c == 8:
                        vec.tensor_tensor(o, sil[:, n % 2, :], pbank(for_vec, ("vin", p, c)), ALU.mult).then_inc(vec_free, 1)
                    else:
                        vec.tensor_tensor(hmul[:, n % 2, :], sil[:, n % 2, :], pbank(for_vec, ("vin", p, c)), ALU.mult).then_inc(vec_free, 1)
                        full(("cw", p, c))
                        own(("vin", p, c))
                        vec.tensor_tensor(o, hmul[:, n % 2, :], pbank(for_vec, ("cw", p, c)), ALU.mult).then_inc(vec_free, 1)
                    n += 1
                else:
                    residual(("out6", c), c)
                    vec.sem_inc(res_ready, 1)

        @block.gpsimd
        def _(pool):
            steps = 0

            def after(ins):
                nonlocal steps
                steps += 1
                ins.then_inc(pool_step, 1)
                pool.wait_ge(pool_step, steps)

            def root(dst, tmp, src, n, eps, done):
                after(pool.tensor_scalar(tmp, src, eps, None, ALU.add))
                pool.tensor_tensor(dst, tmp, half[:, 0:n], ALU.pow).then_inc(done, 1)

            def norm_root(k, b):
                pool.wait_ge(ln_var, 4 * k + b + 1)
                root(rstd[:, k, 2 * b:2 * b + 2], rtmp[:, k, 2 * b:2 * b + 2], mv[:, k, 2 * b:2 * b + 2, 1], 2, EPS, ln_rstd)

            def head_root(s, tile):
                u = UNIT[s, tile]
                pool.wait_ge(ssq_ready, u + 1)
                after(pool.tensor_scalar(ssq[:, s, tile, :], ssq[:, s, tile, :], 1e-24, 1.0 / 1024, ALU.max, ALU.mult))
                pool.tensor_tensor(rnk[:, s, tile, :], ssq[:, s, tile, :], half[:, 0:XH], ALU.pow).then_inc(rnk_ready, 1)

            after(pool.memset(half[:], -0.5))
            for b in range(B):
                norm_root(0, b)
            for b in range(B):
                norm_root(1, b)
            pool.wait_ge(mask_in, 16)
            after(pool.tensor_copy(maskf, mask8[:]))
            pool.tensor_copy(vac[:, :, :, 64:128], maskf[:].unsqueeze(2).unsqueeze(3).broadcast_to([P, NT, XC, 64])).then_inc(vac_mask, 1)
            pool.memset(val[:, :, :, 64:128], 1.0).then_inc(val_ones, 1)
            for kind, b, c in ORDER:
                if kind == "head":
                    head_root(b, c)
                elif kind == "out":
                    pool.wait_ge(msq_ready, b + 1)
                    pool.tensor_tensor(rms[:, 2 * b:2 * b + 2], msq[:, 2 * b:2 * b + 2], half[:, 0:2], ALU.pow).then_inc(rms_ready, 1)
                    pool.wait_ge(ln_var, 4 * 2 + b + 1)
                    r, t, v = rstd[:, 2, 2 * b:2 * b + 2], rtmp[:, 2, 2 * b:2 * b + 2], mv[:, 2, 2 * b:2 * b + 2, 1]
                    after(pool.tensor_scalar(t, v, EPS, None, ALU.add))
                    after(pool.tensor_tensor(r, t, half[:, 0:2], ALU.pow))
                    after(pool.tensor_tensor(t, r, r, ALU.mult))
                    after(pool.tensor_tensor(t, t, v, ALU.mult))
                    after(pool.tensor_scalar(t, t, EPS, None, ALU.add))
                    after(pool.tensor_tensor(t, t, half[:, 0:2], ALU.pow))
                    pool.tensor_tensor(r, r, t, ALU.mult).then_inc(ln_rstd, 1)
                elif kind == "result":
                    pool.wait_ge(ovar_ready, b + 1)
                    root(ort[:, 1, 2 * b:2 * b + 2], ort[:, 0, 2 * b:2 * b + 2], omv[:, 2 * b:2 * b + 2, 1], 2, EPS, orstd_ready)
                    norm_root(3, b)
            for b in range(B):
                norm_root(4, b)
            for n in range(4):
                pool.wait_ge(lead_ready, n + 1)
                p, k = n // 2, n % 2
                pool.tensor_tensor(qh[:, k, 1, p * 512:(p + 1) * 512], rot[:, k, 0, :], qh[:, k, 0, p * 512:(p + 1) * 512], ALU.subtract)\
                    .then_inc(rest_ready, 1)
            after(pool.memset(mneg, 0.0))
            pool.sem_inc(mneg_zero, 1)
            pool.memset(va1[:, :, :, 2 * AD:32], 0.0)
            pool.memset(va1[:, :, :, AD:2 * AD], 1.0).then_inc(va1_ones, 1)
            pool.wait_ge(vec_full, for_vec.number[("out4", B - 1)] + 1)
            pool.memset(place, 0.0).then_inc(place_zero, 1)
            for k in (5, 6):
                for b in range(B):
                    norm_root(k, b)
                if k == 6:
                    pool.memset(gpad[:, :, E:PADE], -1.0)
                    pool.memset(gfind[:, :, TOPE:8], -1.0).then_inc(gpad_set, 1)

        @block.sync
        def _(sp):
            for dst, src, done in ((x, "x", x_in), (w_k, "k", k_in), (w_m, "m", m_in), (cx, "ctx", c_in), (w_x, "xw", xw_in),
                                   (mask8, "mask", mask_in), (w_f, "f", f_in)):
                sp.dma_start(dst[:], io[src]).then_inc(done, 16)
            sp.wait_ge(ln_var, 4 * 2 + B)
            for dst, src, done in ((w_c, "c", c1_in), (w_a, "a", a_in), (w_r, "r", r_in), (w_h, "h", h_in), (w_b, "b", b_in)):
                sp.dma_start(dst, io[src]).then_inc(done, 16)
            sp.wait_ge(vec_full, for_vec.number[("out1", B - 1)] + 1)
            sp.dma_start(w_e, io["e"]).then_inc(e_in, 16)
            for b in range(B):
                sp.wait_ge(res_ready, b + 1)
                sp.dma_start(io["out"][:, 2 * b:2 * b + 2, :], x[:, 2 * b:2 * b + 2, :]).then_inc(stored, 16)
            sp.wait_ge(stored, 16 * B)


def program(nc, arrays):
    io = {}
    for name, a in arrays.items():
        io[name] = nc.dram_tensor("in_" + name, a.shape, mybir.dt.from_np(a.dtype), kind="ExternalInput").ap()
    for name in ("x", "ctx"):
        io[name] = io[name].rearrange("b (h p) d -> p (b h) d", p=P)
    out = nc.dram_tensor("out_rows", (B, S, D), F32, kind="ExternalOutput").ap()
    io["out"] = out.rearrange("b (h p) d -> p (b h) d", p=P)
    decoder(nc, io)


def kernel(**inputs):
    import concourse.bacc as _bacc
    import ml_dtypes
    import numpy as np
    from concourse.bass_utils import run_bass_kernel_spmd

    w = {name: np.asarray(a) for name, a in inputs.items()}

    def pack(spec, parts):
        cols = []
        for name, n in spec:
            a = parts[name]
            assert a.size in (P * n, n), (name, a.shape)
            cols.append(a.reshape(P, n) if a.size == P * n else np.broadcast_to(a.reshape(1, n), (P, n)))
        return np.ascontiguousarray(np.concatenate(cols, axis=1))

    def chunks(a):
        return a.reshape(-1, P, a.shape[1]).transpose(1, 0, 2)

    def col(a):
        return a.reshape(-1, P).T

    m = "L0_attn_"
    mamba = pack(SPEC_M, {
        "in_w": w[m + "in_proj_w"], "conv_w": chunks(w[m + "conv_w"][:, 0, :]), "conv_b": col(w[m + "conv_b"]),
        "dt_bias": w[m + "dt_bias"], "a_log": w[m + "A_log"], "skip": col(np.repeat(w[m + "D"], 64)), "norm_w": col(w[m + "norm_w"]),
        "out_w": chunks(w[m + "out_proj_w"])})
    m = "L0_xattn_"
    cross = pack(SPEC_X, {
        "lnx_w": w[m + "ln_x_w"].reshape(P, 1), "lnx_b": w[m + "ln_x_b"].reshape(P, 1), "lnl_w": w[m + "ln_l_w"].reshape(P, 1),
        "lnl_b": w[m + "ln_l_b"].reshape(P, 1), "q_scale": np.tile(w[m + "q_scale"], 2).reshape(P, 1), "k_scale": np.tile(w[m + "k_scale"], 2).reshape(P, 1),
        "wq": w[m + "Wq"], "wkv": w[m + "Wkv"], "wo": chunks(w[m + "Wo"]), "lno_w": w[m + "ln_o_w"], "lno_b": w[m + "ln_o_b"],
        "q_scale_row": w[m + "q_scale"], "k_scale_row": w[m + "k_scale"]})
    m = "L0_ffn_"
    rec = pack(SPEC_F, {n: w[m + n].T if w[m + n].ndim == 2 else w[m + n].reshape(P, 1) for n, _ in SPEC_F})
    attn = pack(SPEC_A, {n: w["L1_attn_" + n] for n, _ in SPEC_A})
    corr = pack(SPEC_C, {n: w["L1_xattn_" + n] for n, _ in SPEC_C})
    m = "L1_ffn_"
    moe = pack(SPEC_E, {
        "gate": w[m + "gate_w"].T, "ws_in": w[m + "ws_in"], "vs_in": w[m + "vs_in"],
        "e_win": w[m + "e_win"].transpose(1, 0, 2), "e_vin": w[m + "e_vin"].transpose(1, 0, 2),
        "w_out": chunks(np.concatenate([w[m + "e_wout"].reshape(-1, D), w[m + "ws_out"]]))})

    eye, i, f = np.eye(P), np.arange(P), np.arange(P)
    tri = (i[:, None] <= i[None, :]).astype(np.float64)
    t, tau = np.arange(S), np.arange(S)
    cos = np.cos(2 * np.pi * np.outer(t, f) / S)
    sin = np.sin(2 * np.pi * np.outer(t, f) / S)
    mid = np.where(t % 2 == 0, 1.0, -1.0)
    cos_mid, sin_mid = cos.copy(), sin.copy()
    cos_mid[:, 0] = mid
    sin_mid[:, 0] = mid
    dft = np.stack([cos, sin_mid, cos_mid], axis=1).reshape(2, P, 3, P).transpose(1, 0, 2, 3)
    weight = np.where(f == 0, 1.0, 2.0)[:, None] / S
    icos = weight * np.cos(2 * np.pi * np.outer(f, tau) / S)
    isin = weight * np.sin(2 * np.pi * np.outer(f, tau) / S)
    isin[0] = mid / S
    freq = (np.arange(S, dtype=np.float32)[:, None] * (1.0 / np.float32(10000.0) ** (np.arange(0, AD, 2, dtype=np.float32) / np.float32(AD)))[None, :]).T
    freq = np.tile(np.repeat(freq, 2, axis=0), (AH, 1))
    rope = pack(SPEC_R, {"cos": np.cos(freq), "sin": np.sin(freq)}).astype(np.float32)
    heads = (i[:, None] // 8 == i[None, :] // 8).astype(np.float64)
    consts = pack(SPEC_K, {
        "ident": eye, "ones": np.ones((P, P)), "tri": tri, "gmask": np.concatenate([tri, np.ones((P, P)), tri], axis=1), "dft": dft,
        "idft": np.concatenate([icos, isin], axis=1), "keep": (f > 0).astype(np.float64).reshape(P, 1),
        "sixteen": np.where(i % 32 == 24, 16.0, 0.0).reshape(P, 1), "jmod": (i[:, None] - np.arange(8)[None, :]) % 8, "bd": heads, "permute": (i[:, None] == (i[None, :] % AH) * AD + i[None, :] // AH).astype(np.float64)}).astype(np.float32)
    sel = np.zeros((4, P, 4, P))
    for j in range(4):
        for g in range(4):
            for d in range(8):
                for r, (qp, kp) in enumerate(((0, 0), (0, 1), (1, 0))):
                    sel[qp, 8 * (4 * j + g) + d, j, 32 * g + 8 * r + d] = 1.0
                    sel[2 + kp, 8 * (4 * j + g) + d, j, 32 * g + 8 * r + d] = 1.0
    halves = pack(SPEC_H, {"ident": eye, "selq1": sel[0], "selq2": sel[1], "selk1": sel[2], "selk2": sel[3]}).astype(np.float16)
    far = np.float64(-1e30)
    expand = np.zeros((P, 8, P))
    for part in range(3):
        for e in range(E):
            expand[part * E + e, e // 2, e % 2 * 64:e % 2 * 64 + 64] = 1.0
    brain = pack(SPEC_B, {
        "ident": eye, "mask_row": np.where(i[None, :] > i[:, None], far, 0.0), "mask_col": np.where(i[:, None] > i[None, :], far, 0.0),
        "expand": expand}).astype(ml_dtypes.bfloat16)

    arrays = {
        "x": np.ascontiguousarray(w["x"]), "ctx": np.ascontiguousarray(w["ctx_1024"]),
        "mask": np.ascontiguousarray(w["mask_BxS2_bk0"].reshape(NT, P).T), "m": mamba, "xw": cross, "f": rec, "a": attn, "c": corr,
        "e": moe, "k": consts, "h": halves, "r": rope, "b": brain}
    nc = _bacc.Bacc("TRN2", target_bir_lowering=False, num_devices=1)
    program(nc, arrays)
    return run_bass_kernel_spmd(nc, [{"in_" + name: a for name, a in arrays.items()}], core_ids=[0]).results[0]["out_rows"]
```

```python
from contextlib import ExitStack

import concourse.bass as bass
from concourse import mybir

F32 = mybir.dt.float32
F16 = mybir.dt.float16
BF16 = mybir.dt.bfloat16
U8 = mybir.dt.uint8
U32 = mybir.dt.uint32
I32 = mybir.dt.int32
ALU = mybir.AluOpType
ACT = mybir.ActivationFunctionType
AX = mybir.AxisListType

P = 128
B = 4
S = 256
D = 128
NT = B * S // P
EPS = 1e-5

MH = 4
MC = 4
TAPS = 4
XH = 8
XD = 64
XC = 4
AH = 16
AD = 8
TOPC = 5
E = 16
TOPE = 4
HC = 9
PADE = E + 4

SPEC_M = [("in_w", 772), ("conv_w", 16), ("conv_b", 4), ("dt_bias", 4), ("a_log", 4), ("skip", 2), ("norm_w", 2), ("out_w", 256)]
SPEC_X = [("lnx_w", 1), ("lnx_b", 1), ("lnl_w", 1), ("lnl_b", 1), ("q_scale", 1), ("k_scale", 1), ("wq", 512), ("wkv", 1024), ("wo", 512),
          ("lno_w", 128), ("lno_b", 128), ("q_scale_row", 64), ("k_scale_row", 64)]
SPEC_F = [("wf", 128), ("uf", 128), ("wi", 128), ("ui", 128), ("wc", 128), ("uc", 128), ("wo", 128), ("uo", 128),
          ("bf", 1), ("bi", 1), ("bc", 1), ("bo", 1), ("in_c", 1)]
SPEC_A = [("qw", 128), ("kw", 128), ("vw", 128), ("ow", 128)]
SPEC_C = [("wq", 128), ("wk", 128), ("wv", 128), ("wo", 128)]
SPEC_E = [("gate", 16), ("ws_in", 128), ("vs_in", 128), ("e_win", 1024), ("e_vin", 1024), ("w_out", 1152)]
SPEC_K = [("ident", 128), ("ones", 128), ("tri", 128), ("gmask", 384), ("dft", 768), ("idft", 512), ("keep", 1), ("sixteen", 1),
          ("jmod", 8), ("bd", 128), ("permute", 128)]
SPEC_R = [("cos", 256), ("sin", 256)]
SPEC_H = [("ident", 128), ("selq1", 512), ("selq2", 512), ("selk1", 512), ("selk2", 512)]
SPEC_B = [("ident", 128), ("mask_row", 128), ("mask_col", 128), ("expand", 1024)]


def width(spec):
    return sum(n for _, n in spec)


def columns(tile, spec):
    at, out = 0, {}
    for name, n in spec:
        out[name] = tile[:, at:at + n]
        at += n
    return out


class Uses:

    def __init__(self, first):
        self.first = first
        self.number = {}

    def add(self, key):
        assert key not in self.number, key
        self.number[key] = len(self.number)
        return self.number[key]


def decoder(nc, io):
    ctx = ExitStack()
    with ctx:
        def sb(name, shape, dt=F32):
            return ctx.enter_context(nc.sbuf_tensor(name, shape, dt))[:]

        def sem(name):
            return ctx.enter_context(nc.semaphore(name))

        ps = ctx.enter_context(nc.psum_tensor("ps", [P, 8 * 512], F32))
        for_act, for_vec = Uses(0), Uses(4)

        def pbank(uses, key, n=512):
            b = uses.first + uses.number[key] % 4
            return ps[:, b * 512:b * 512 + n]

        w_m, w_x, w_f = sb("w_m", [P, width(SPEC_M)]), sb("w_x", [P, width(SPEC_X)]), sb("w_f", [P, width(SPEC_F)])
        w_k = sb("w_k", [P, width(SPEC_K)])
        M, X0, F, K = columns(w_m, SPEC_M), columns(w_x, SPEC_X), columns(w_f, SPEC_F), columns(w_k, SPEC_K)
        ident = K["ident"]
        mask8, maskf = sb("mask8", [P, NT], U8), sb("maskf", [P, NT])

        x = sb("x", [P, NT, D])
        urow = [sb(f"urow{i}", [P, NT, D]) for i in range(2)]
        uT = [sb(f"uT{i}", [P, B, S]) for i in range(2)]
        cx = sb("cx", [P, NT, D])
        cT = sb("cT", [P, B, S])
        cnT = sb("cnT", [P, B, S])
        stats = sb("stats", [P, 7, NT, 6])
        mv = sb("mv", [P, 7, NT, 2])
        rstd = sb("rstd", [P, 7, NT])
        rtmp = sb("rtmp", [P, 7, NT])
        half = sb("half", [P, 64])

        XTOP = 13664
        WA = 24128
        WB = 12800
        regA, regB = sb("regA", [P, WA]), sb("regB", [P, WB])

        class Carve:
            def __init__(self, region, size, at=0):
                self.region, self.size, self.at = region, size, at

            def f32(self, n):
                a = self.region[:, self.at:self.at + n]
                self.at += n
                assert self.at <= self.size, (self.at, self.size)
                return a

            def f16(self, n):
                return self.f32(n // 2).bitcast(F16)

            def bf16(self, n):
                return self.f32(n // 2).bitcast(BF16)

        a = Carve(regA, WA, XTOP)
        xc = a.f32(MC * 1024).rearrange("p (c t) -> p c t", c=MC)
        zs = a.f32(2 * 1024).rearrange("p (c t) -> p c t", c=2)
        dtx = a.f32(32).rearrange("p (t h) -> p t h", h=MH)
        dta = a.f32(32).rearrange("p (t h) -> p t h", h=MH)
        dte = a.f32(32).rearrange("p (t h) -> p t h", h=MH)
        dtl = a.f32(32).rearrange("p (t h) -> p t h", h=MH)
        dt = a.f32(32).rearrange("p (t h) -> p t h", h=MH)
        ea = a.f32(4)
        da = a.f32(32).rearrange("p (t h) -> p t h", h=MH)
        cum = a.f32(32).rearrange("p (t h) -> p t h", h=MH)
        gm = a.f32(384)
        eL = a.f32(2 * 4 * 384).rearrange("p (v h n) -> p v h n", v=2, h=MH)
        xdt = cx.rearrange("p t n -> p (t n)").rearrange("p (t n) -> p t n", t=4)
        spare = uT[1].rearrange("p b s -> p (b s)").rearrange("p (v c n) -> p v c n", v=2, c=2)
        yg, ysq = spare[:, 0, :, :], spare[:, 1, :, :]
        msq = a.f32(8)
        rms = a.f32(8)
        ow2 = a.f32(256).rearrange("p (c n) -> p c n", c=2)

        a = Carve(regA, XTOP)
        pT = a.f32(3 * 1024).rearrange("p (v k q) -> p v k q", v=3, k=4)
        q1 = a.f16(XH * 512).rearrange("p (h t) -> p h t", h=XH)
        q2 = a.f16(XC * 512).rearrange("p (c t) -> p c t", c=XC)
        kl = a.f16(XH * 512).rearrange("p (h t) -> p h t", h=XH)
        val = a.f32(4 * XC * 192).rearrange("p (t c n) -> p t c n", t=4, c=XC)
        den = a.f32(2 * 256).rearrange("p (v n) -> p v n", v=2)
        rec = a.f32(256)
        oT = a.f32(5 * 256).rearrange("p (c n) -> p c n", c=5)
        on = a.f32(256).rearrange("p (q n) -> p q n", q=2)
        ostat = a.f32(NT * 6).rearrange("p (t n) -> p t n", t=NT)
        omv = a.f32(NT * 2).rearrange("p (t n) -> p t n", t=NT)
        ort = a.f32(2 * NT).rearrange("p (v t) -> p v t", v=2)
        bb = Carve(regB, WB)
        kc = bb.f16(XH * 1024).rearrange("p (h t) -> p h t", h=XH)
        vac = bb.f32(NT * XC * 192).rearrange("p (t c n) -> p t c n", t=NT, c=XC)
        sqr = bb.f32(2 * 512).rearrange("p (v n) -> p v n", v=2)
        parts = bb.f16(2 * 1536).rearrange("p (v n) -> p v n", v=2)
        ssq = sb("ssq", [P, 3, NT, XH])
        rnk = sb("rnk", [P, 3, NT, XH])
        qks = sb("qks", [P, 64])
        ident16 = sb("ident16", [P, P], F16)
        shift = sb("shift", [P, 2])

        a = Carve(regA, WA, XTOP)
        w_a, w_c, w_r = a.f16(width(SPEC_A)), a.f32(width(SPEC_C)), a.f32(width(SPEC_R))
        w_h, w_b = a.f16(width(SPEC_H)), a.bf16(width(SPEC_B))
        A1, C1, R, KH, KB = columns(w_a, SPEC_A), columns(w_c, SPEC_C), columns(w_r, SPEC_R), columns(w_h, SPEC_H), columns(w_b, SPEC_B)
        above = a.at

        uh = a.f32(4 * 128).rearrange("p (g n) -> p g n", g=4)
        halfb = a.f32(2)
        cell = a.f32(2 * 256).rearrange("p (v n) -> p v n", v=2)
        gat = a.f32(2 * 3 * 256).rearrange("p (v g n) -> p v g n", v=2, g=3)
        mixa = a.f32(256)
        mixb = a.f32(256)
        hT = cx.rearrange("p t n -> p (t n)").rearrange("p (t n) -> p t n", t=B)

        a = Carve(regA, XTOP)
        wa32 = a.f32(512)
        wrot = a.f32(256)
        rot = a.f32(2 * 2 * 512).rearrange("p (v s t) -> p v s t", v=2, s=2)
        qh = a.f16(2 * 2 * 1024).rearrange("p (k s t) -> p k s t", k=2, s=2)
        qst = a.f16(2 * 4 * 1024).rearrange("p (v j t) -> p v j t", v=2, j=4)
        kst = a.f16(4 * 1024).rearrange("p (j t) -> p j t", j=4)
        sixteen = a.f32(1)
        mx = a.f32(B * 2 * 16).rearrange("p (b q i j) -> p b q i j", b=B, q=2, i=4)
        mneg = a.f16(2 * 2 * 4 * 128).rearrange("p (v q j c) -> p v q j c", v=2, q=2, j=4)
        oc1 = a.f32(2 * 256).rearrange("p (v n) -> p v n", v=2)
        or1 = a.f32(2 * 256).rearrange("p (v q n) -> p v q n", v=2, q=2)
        rec1 = a.f32(B * 32).rearrange("p (b q h) -> p b q h", b=B, q=2)
        a = Carve(regA, WA, above)
        oT1 = a.f32(2 * 256).rearrange("p (v n) -> p v n", v=2)
        pT1 = a.f32(3 * 1536).rearrange("p (v n) -> p v n", v=3)

        prod = w_m[:, 0:1024].rearrange("p (f n) -> p f n", f=2)
        qr = cx.rearrange("p t n -> p (t n)").rearrange("p (h b n) -> p h b n", h=2, b=B)
        sab = cnT.rearrange("p b s -> p (b s)").rearrange("p (f n) -> p f n", f=2)
        mbd = w_f[:, 0:512].rearrange("p (b h j) -> p b h j", b=B, h=16)
        a = Carve(w_x, width(SPEC_X))
        place = a.f32(B * 512).rearrange("p (b t h r) -> p b t h r", b=B, t=2, h=2)
        hit = a.f32(B * 5 * 8).rearrange("p (b k j) -> p b k j", b=B, k=5)
        hitw = a.f32(B * 5 * 8).rearrange("p (b k j) -> p b k j", b=B, k=5)
        trec = a.f32(B)
        tsum = a.f32(B)
        a = Carve(w_f, width(SPEC_F), 512)
        top, tope, delta, delf, roll = [a.f32(B * 8).rearrange("p (b n) -> p b n", b=B) for _ in range(5)]
        topi, delm = [a.f32(B * 8).rearrange("p (b n) -> p b n", b=B).bitcast(U32) for _ in range(2)]

        a = Carve(regA, XTOP)
        hid = a.f32(HC * 1024).rearrange("p (c t) -> p c t", c=HC)
        sil = a.f32(2 * 512).rearrange("p (v n) -> p v n", v=2)
        hmul = a.f32(2 * 512).rearrange("p (v n) -> p v n", v=2)
        a = Carve(regA, WA, above + 5120)
        gex = a.f32(NT * E).rearrange("p (t e) -> p t e", t=NT)
        gde = a.f32(NT * E).rearrange("p (t e) -> p t e", t=NT)
        gpad = a.f32(NT * PADE).rearrange("p (t e) -> p t e", t=NT)
        grep = a.f32(NT * PADE).rearrange("p (t e) -> p t e", t=NT)
        gtop = a.f32(NT * 8).rearrange("p (t e) -> p t e", t=NT)
        gfind = a.f32(NT * 8).rearrange("p (t e) -> p t e", t=NT)
        gsum = a.f32(NT)
        grec = a.f32(NT)
        comb = a.f32(NT * E).rearrange("p (t e) -> p t e", t=NT)
        comr = a.f32(2 * NT * E).rearrange("p (v t e) -> p v t e", v=2, t=NT)
        comb3 = a.bf16(NT * 48).rearrange("p (t s e) -> p t s e", t=NT, s=3)
        combT = a.bf16(1024)
        bb = Carve(regB, WB)
        w_e = bb.f32(width(SPEC_E))
        G = columns(w_e, SPEC_E)
        va1 = bb.f32(NT * AH * 32).rearrange("p (t h n) -> p t h n", t=NT, h=AH)

        kr = bb.f32(2 * 512).rearrange("p (h b n) -> p h b n", h=2, b=B)
        vr = bb.f32(2 * 512).rearrange("p (h b n) -> p h b n", h=2, b=B)
        vo = bb.f32(1024).rearrange("p (b n) -> p b n", b=B)
        pr = bb.f32(3 * 512).rearrange("p (f n) -> p f n", f=3)

        names = ["x_in", "m_in", "k_in", "c_in", "xw_in", "f_in", "a_in", "h_in", "r_in", "b_in", "c1_in", "e_in", "mask_in", "stored"]
        x_in, m_in, k_in, c_in, xw_in, f_in, a_in, h_in, r_in, b_in, c1_in, e_in, mask_in, stored = [sem(n) for n in names]
        act_full, act_free, vec_full, vec_free = sem("act_full"), sem("act_free"), sem("vec_full"), sem("vec_free")
        ln_var, ln_rstd, ln_rows, x_ready = sem("ln_var"), sem("ln_rstd"), sem("ln_rows"), sem("x_ready")
        ln6_var, ln6_rstd, ln6_rows = sem("ln6_var"), sem("ln6_rstd"), sem("ln6_rows")

        def norm_count(k, b):
            return b + 1 if k == 6 else 4 * k + b + 1

        pool_step = sem("pool_step")
        vec_step = sem("vec_step")
        act_step = sem("act_step")

        block = ctx.enter_context(nc.Block())
        LN = {"mamba": 0, "ctx": 1, "lat": 2, "rec": 3, "attn": 4, "corr": 5, "moe": 6}
        ROW = {0: 0, 1: 1, 2: 0, 3: 1, 4: 0, 5: 1, 6: 0}
        ORDER = []
        for n, (p, c) in enumerate([(p, c) for p in range(2) for c in (2, 3, 4, 5, 0, 1)]):
            ORDER.append(("in", p, c))
            if n == 5:
                ORDER.append(("cum", 0, 0))
            ORDER.append(("context", n, 0) if n < B else ("value", 0, n - B))

        def each(step, s, b):
            return [(step, s, 2 * b), (step, s, 2 * b + 1)]

        ORDER += [("front", 0, 0)] + each("head", 0, 0) + [("decay", 0, 0)] + each("norm", 0, 0) + [("front", 1, 0)] + each("parts", 0, 0)
        ORDER += [("back", 0, 0)] + each("turn", 0, 0) + each("head", 0, 1) + [("decay", 1, 0)] + each("norm", 0, 1) + [("out", 0, 0)]
        ORDER += each("parts", 0, 1) + [("front", 2, 0)] + each("turn", 0, 1) + [("back", 1, 0), ("rows2", 0, 0), ("latent", 0, 0)]
        ORDER += each("head", 1, 0) + [("decay", 2, 0)] + each("norm", 1, 0) + [("out", 1, 0)] + each("parts", 1, 0) + [("front", 3, 0)]
        ORDER += each("turn", 1, 0) + [("back", 2, 0)] + each("head", 2, 0) + [("decay", 3, 0)] + each("norm", 2, 0)
        ORDER += [("out", 2, 0)] + each("parts", 2, 0) + [("rows2", 1, 0)] + each("value", 1, 0) + each("turn", 2, 0)
        BESIDE = {0: [("back", 3, 0)], 1: [("out", 3, 0)], 6: [("rows2", 2, 0)], 8: [("rows2", 3, 0), ("halves", 0, 0)]}
        for n in range(B * XH + 9):
            b, h = n // XH, n % XH
            k = b + 1
            if n < B * XH:
                ORDER.append(("sim", b, h))
            ORDER += BESIDE.get(n, [])
            if 1 <= b < 3:
                ORDER += {0: each("norm", 0, k), 1: each("parts", 0, k), 2: each("turn", 0, k)}.get(h, [])
            if k < B:
                ORDER += {0: [("latent", k, 0)], 2: each("norm", 1, k), 3: each("parts", 1, k), 4: each("turn", 1, k) + each("head", 2, k),
                          5: each("norm", 2, k), 6: each("parts", 2, k), 7: each("turn", 2, k) + each("value", 1, k)}.get(h, [])
            if 0 <= n - 2 < B * XH:
                ORDER.append(("pv", (n - 2) // XH, (n - 2) % XH))
            if k < B and h == 1:
                ORDER += each("head", 1, k)
            if b >= 1:
                ORDER += {3: [("result", b - 1, 0)], 4: [("rows3", b - 1, 0)]}.get(h, [])
                ORDER += {5: [("turn3", b - 1, 0)], 6: [("gates", b - 1, 0)], 7: [("cell", b - 1, 0)]}.get(h if b == B else h - 2, [])
            if 2 <= b <= B and h < 2:
                ORDER += [("gates", b - 2, 0)] if h == 0 else [("cell", b - 2, 0)]
            if b < 2 and h == 7:
                ORDER += each("head", 0, k + 1)
            if b == B:
                ORDER += {3: [("corr_rows", "k", i) for i in range(B)], 4: [("corr_rows", "v", i) for i in range(B)],
                          5: [("corr_vo", 0, 0)], 6: [("corr_spectra", 0, 0)]}.get(h, [])
        UNIT = {}
        for step, s, tile in ORDER:
            if step == "head":
                UNIT[s, tile] = len(UNIT)
        AORDER = [("row", 0, i) for i in range(4)] + [("stack", 0, 0)]
        for n in range(4 * B + 4):
            b, i = n // 4, n % 4
            if b + 1 < B:
                AORDER.append(("row", b + 1, i))
            if b < B:
                AORDER.append(("col", b, i))
            if 0 <= n - 1 < 4 * B:
                AORDER.append(("pv", (n - 1) // 4, (n - 1) % 4))
            if 0 <= n - 2 < 4 * B:
                AORDER.append(("back", (n - 2) // 4, (n - 2) % 4))
            if b + 1 < B and i == 3:
                AORDER.append(("stack", b + 1, 0))
            if n >= 4 and i == 2:
                AORDER.append(("turn", b - 1, 0))
            if n >= 4 and i == 3:
                AORDER.append(("out", b - 1, 0))
            AORDER += [(step, 0, 0) for step in {
                12: ["rows5", "turn5", "queries"], 13: ["spectra"], 14: ["delays", "weights"], 15: ["mix", "out5"], 16: ["rows6", "turn6"],
                17: ["logits"], 18: ["choice"]}.get(n, [])]
        EORDER = [("rows5", 1, 0), ("up", 0, 8), ("turn5", 1, 0), ("queries", 1, 0), ("up", 0, 0), ("spectra", 1, 0), ("up", 0, 1), ("delays", 1, 0)]
        EORDER += [("weights", 1, 0), ("up", 0, 2), ("mix", 1, 0), ("up", 0, 3), ("out5", 1, 0), ("up", 0, 4), ("rows6", 1, 0), ("up", 0, 5)]
        EORDER += [("turn6", 1, 0), ("up", 0, 6), ("logits", 1, 0), ("up", 0, 7), ("down", 0, 0), ("choice", 1, 0), ("down", 0, 1)]
        EORDER += [("up", 1, c) for c in (8, *range(8))] + [("down", 1, 2), ("down", 1, 3)]
        LORDER = AORDER + EORDER

        da_ready, conv_ready, w_ready, gated, ysq_ready = sem("da_ready"), sem("conv_ready"), sem("w_ready"), sem("gated"), sem("ysq_ready")
        tap_ready, lead_parts, parts_ready, q_scaled, ident16_set = sem("tap_ready"), sem("lead_parts"), sem("parts_ready"), sem("q_scaled"), sem("ident16_set")
        dt_abs, dt_log, ea_ready = sem("dt_abs"), sem("dt_log"), sem("ea_ready")
        den_ready, decay_ready, msq_ready, rms_ready = sem("den_ready"), sem("decay_ready"), sem("msq_ready"), sem("rms_ready")
        sq_ready, ssq_ready, rnk_ready = sem("sq_ready"), sem("ssq_ready"), sem("rnk_ready")
        val_ones, vac_mask, shift_ready = sem("val_ones"), sem("vac_mask"), sem("shift_ready")
        ovar_ready, orstd_ready = sem("ovar_ready"), sem("orstd_ready")
        cell_ready, gates_ready, halves_ready = sem("cell_ready"), sem("gates_ready"), sem("halves_ready")
        rope_ready, lead_ready, wa_ready, mneg_zero, mneg_ready, va1_ones = sem("rope_ready"), sem("lead_ready"), sem("wa_ready"), sem("mneg_zero"), sem("mneg_ready"), sem("va1_ones")
        place_zero, prod_ready, mbd_ready, corr_diff, corr_exp = sem("place_zero"), sem("prod_ready"), sem("mbd_ready"), sem("corr_diff"), sem("corr_exp")
        gpad_set, comb_ready = sem("gpad_set"), sem("comb_ready")
        res_ready, rest_ready = sem("res_ready"), sem("rest_ready")

        @block.tensor
        def _(pe):
            def act_bank(key):
                n = for_act.add(key)
                if n >= 4:
                    pe.wait_ge(act_free, n - 3)
                return pbank(for_act, key)

            def vec_bank(key):
                n = for_vec.add(key)
                if n >= 4:
                    pe.wait_ge(vec_free, n - 3)
                return pbank(for_vec, key)

            def act_has(key):
                pe.wait_ge(act_free, for_act.number[key] + 1)

            def vec_has(key):
                pe.wait_ge(vec_free, for_vec.number[key] + 1)

            def rows_turn(k, b):
                pe.wait_ge(ln6_rows if k == 6 else ln_rows, norm_count(k, b))
                t = act_bank(("uT", k, b))
                for hf in range(2):
                    last = pe.transpose(t[:, hf * P:(hf + 1) * P], urow[ROW[k]][:, 2 * b + hf, :], ident)
                last.then_inc(act_full, 1)

            def values(s, tile):
                if s == 0:
                    act_has(("uT", 1, tile // 2))
                else:
                    vec_has(("uT", 2, tile // 2))
                t = act_bank(("xv", s, tile))
                pe.matmul(t, (cnT, uT[0])[s][:, tile // 2, tile % 2 * P:(tile % 2 + 1) * P], X0["wkv"][:, 512:1024],
                          start=True, stop=True).then_inc(act_full, 1)

            def head_rows(s, tile):
                u = UNIT[s, tile]
                if s == 0:
                    act_has(("uT", 1, tile // 2))
                else:
                    vec_has(("uT", 2, tile // 2))
                t = vec_bank(("kr", u))
                w = X0["wq"] if s == 2 else X0["wkv"][:, 0:512]
                pe.matmul(t, (uT[0] if s else cnT)[:, tile // 2, tile % 2 * P:(tile % 2 + 1) * P], w, start=True, stop=True).then_inc(vec_full, 1)

            def head_turn(s, tile):
                u = UNIT[s, tile]
                pe.wait_ge(parts_ready, u + 1)
                t = act_bank(("kT", u)).bitcast(F16)
                for h in range(XH):
                    last = pe.transpose(t[:, h * P:(h + 1) * P], parts[:, u % 2, h * P:(h + 1) * P], ident16)
                last.then_inc(act_full, 1)
                if s == 2:
                    t = act_bank(("qT", u)).bitcast(F16)
                    for c in range(XC):
                        last = pe.transpose(t[:, c * P:(c + 1) * P], parts[:, u % 2, 1024 + c * P:1024 + (c + 1) * P], ident16)
                    last.then_inc(act_full, 1)

            def corr_rows(name, b):
                t = act_bank(("cr", name, b))
                for hf in range(2):
                    src = (uT[1] if name == "q" else cT)[:, b, hf * P:(hf + 1) * P]
                    last = pe.matmul(t[:, hf * P:(hf + 1) * P], src, C1["w" + name], start=True, stop=True)
                last.then_inc(act_full, 1)

            def spectrum(f):
                t = act_bank(("fk", f))
                for hf in range(2):
                    at = hf * 384 + f * P
                    last = pe.matmul(t, K["dft"][:, at:at + P], kr[:, hf, :, :], start=(hf == 0), stop=(hf == 1))
                last.then_inc(act_full, 1)

            pe.wait_ge(k_in, 16)
            for b in range(B):
                rows_turn(0, b)
            pe.wait_ge(m_in, 16)
            act_has(("uT", 0, B - 1))
            t = vec_bank("dt")
            for tile in range(NT):
                last = pe.matmul(t[:, tile * MH:(tile + 1) * MH], uT[0][:, tile // 2, tile % 2 * P:(tile % 2 + 1) * P],
                                 M["in_w"][:, 768:772], start=True, stop=True)
            last.then_inc(vec_full, 1)
            for kind, b, c in ORDER:
                h = c
                if kind == "in":
                    t = vec_bank(("in", b, c)) if c >= 2 else act_bank(("in", b, c))
                    pe.matmul(t, M["in_w"][:, c * P:(c + 1) * P], uT[0][:, 2 * b:2 * b + 2, :], start=True, stop=True)\
                      .then_inc(vec_full if c >= 2 else act_full, 1)
                elif kind == "cum":
                    pe.wait_ge(da_ready, 1)
                    t = vec_bank("cum")[:, 0:NT * MH].rearrange("p (b s h) -> p b s h", b=B, s=2)
                    pe.matmul(t[:, :, 0, :], K["tri"], da[:, 0::2, :], start=True, stop=True)
                    pe.matmul(t[:, :, 1, :], K["tri"], da[:, 1::2, :], start=True, stop=False)
                    pe.matmul(t[:, :, 1, :], K["ones"], da[:, 0::2, :], start=False, stop=True).then_inc(vec_full, 1)
                elif kind == "context":
                    pe.wait_ge(c_in, 16)
                    t = act_bank(("cT", b))
                    for hf in range(2):
                        last = pe.transpose(t[:, hf * P:(hf + 1) * P], cx[:, 2 * b + hf, :], ident)
                    last.then_inc(act_full, 1)
                    rows_turn(1, b)
                elif kind == "value":
                    if b == 0 and c == 0:
                        pe.wait_ge(xw_in, 16)
                    values(b, c)
                elif kind == "head":
                    head_rows(b, c)
                elif kind == "turn":
                    if (b, c) == (0, 0):
                        pe.wait_ge(ident16_set, 1)
                    head_turn(b, c)
                elif kind == "front":
                    pe.wait_ge(conv_ready, 4 * (b // 2) + 2)
                    t = vec_bank(("xrow", b))
                    for hf in range(2):
                        for c in range(2):
                            at = b * S + hf * P
                            last = pe.transpose(t[:, hf * 256 + c * P:hf * 256 + (c + 1) * P], xc[:, c, at:at + P], ident)
                    last.then_inc(vec_full, 1)
                    pe.wait_ge(conv_ready, 4 * (b // 2) + 4)
                    t = vec_bank(("G", b))
                    pe.matmul(t[:, 0:256], xc[:, 2, b * S:b * S + P], xc[:, 3, b * S:(b + 1) * S], start=True, stop=True)
                    pe.matmul(t[:, 256:384], xc[:, 2, b * S + P:(b + 1) * S], xc[:, 3, b * S + P:(b + 1) * S],
                              start=True, stop=True).then_inc(vec_full, 1)
                    vec_has("cum")
                    for hf in range(2):
                        t = vec_bank(("bc", b, hf))
                        for h in range(MH):
                            last = pe.transpose(t[:, h * P:(h + 1) * P], cum[:, 2 * b + hf, h:h + 1].broadcast_to([P, P]), ident)
                        last.then_inc(vec_full, 1)
                elif kind == "back":
                    pe.wait_ge(w_ready, b + 1)
                    t = vec_bank(("Y", b))
                    for h in range(MH):
                        r, at = h % 2 * 64, h // 2 * 256
                        pe.matmul(t[r:r + 64, at:at + 256], xdt[:, b % 2 * 2, h * 64:(h + 1) * 64], eL[:, b % 2, h, 0:256], start=True, stop=False)
                        last = pe.matmul(t[r:r + 64, at + P:at + 256], xdt[:, b % 2 * 2 + 1, h * 64:(h + 1) * 64], eL[:, b % 2, h, 256:384],
                                         start=False, stop=True)
                    last.then_inc(vec_full, 1)
                elif kind == "out":
                    pe.wait_ge(gated, b + 1)
                    t = vec_bank(("out0", b))
                    for hf in range(2):
                        for c in range(2):
                            pe.matmul(t[:, hf * P:(hf + 1) * P], yg[:, c, hf * P:(hf + 1) * P], ow2[:, c, :], start=(c == 0), stop=(c == 1))
                    pe.wait_ge(ysq_ready, b + 1)
                    for hf in range(2):
                        for c in range(2):
                            last = pe.matmul(t[:, 256 + hf:257 + hf], ysq[:, c, hf * P:(hf + 1) * P], K["ones"][:, 0:1],
                                             start=(c == 0), stop=(c == 1))
                    last.then_inc(vec_full, 1)
                elif kind == "latent":
                    pe.wait_ge(ln_rows, 4 * 2 + b + 1)
                    t = vec_bank(("uT", 2, b))
                    for hf in range(2):
                        last = pe.transpose(t[:, hf * P:(hf + 1) * P], urow[ROW[2]][:, 2 * b + hf, :], ident)
                    last.then_inc(vec_full, 1)
                elif kind == "sim":
                    n, c, r = b * XH + h, h // 2, h % 2 * 64
                    act_has(("qT", UNIT[2, 2 * b + 1]))
                    banks = [act_bank(("sim", n, 0)), act_bank(("sim", n, 1))]
                    assert for_act.number[("sim", n, 0)] % 2 == 0
                    at = b % 2 * S
                    for kt in range(4):
                        keys = kc[:, h, b * S + kt * P:b * S + (kt + 1) * P] if kt < 2 else kl[:, h, at + (kt - 2) * P:at + (kt - 1) * P]
                        o = banks[kt // 2][:, kt % 2 * 256:(kt % 2 + 1) * 256]
                        pe.matmul(o, keys, q1[:, h, at:at + S], start=True, stop=False)
                        last = pe.matmul(o, keys[r:r + 64, :], q2[r:r + 64, c, at:at + S], start=False, stop=True)
                    last.then_inc(act_full, 2)
                elif kind == "pv":
                    n, c = b * XH + h, h // 2
                    act_has(("sim", n, 1))
                    act_has(("xv", 1, 2 * b + 1))
                    if n == 0:
                        pe.wait_ge(val_ones, 1)
                        pe.wait_ge(vac_mask, 1)
                    t = vec_bank(("pv", n))
                    at = h % 2 * 64
                    for kt in range(4):
                        values_of = vac[:, 2 * b + kt, c, at:at + P] if kt < 2 else val[:, b % 2 * 2 + kt - 2, c, at:at + P]
                        last = pe.matmul(t[:, 0:256], values_of, pT[:, n % 3, kt, :],
                                         start=(kt == 0), stop=(kt == 3))
                    last.then_inc(vec_full, 1)
                elif kind == "result":
                    vec_has(("pv", b * XH + XH - 1))
                    t = vec_bank(("out1", b))
                    for qt in range(2):
                        for c in range(XC):
                            last = pe.matmul(t[:, qt * P:(qt + 1) * P], oT[:, (XC * b + c) % 5, qt * P:(qt + 1) * P], X0["wo"][:, c * P:(c + 1) * P],
                                             start=(c == 0), stop=(c == XC - 1))
                    last.then_inc(vec_full, 1)
                elif kind == "corr_rows":
                    if b == "k" and h == 0:
                        pe.wait_ge(c1_in, 16)
                    corr_rows(b, h)
                elif kind == "corr_vo":
                    act_has(("cr", "v", B - 1))
                    for bp in range(2):
                        t = act_bank(("vo", bp))
                        for i in range(2):
                            for hf in range(2):
                                at = (2 * i + hf) * P
                                last = pe.matmul(t[:, at:at + P], vr[:, hf, 2 * bp + i, :], C1["wo"], start=True, stop=True)
                        last.then_inc(act_full, 1)
                elif kind == "corr_spectra":
                    for f in range(3):
                        spectrum(f)
                elif kind == "turn3":
                    pe.wait_ge(ln_rows, 4 * 3 + b + 1)
                    t = vec_bank(("uT", 3, b))
                    for hf in range(2):
                        last = pe.transpose(t[:, hf * P:(hf + 1) * P], urow[ROW[3]][:, 2 * b + hf, :], ident)
                    last.then_inc(vec_full, 1)
                elif kind == "gates":
                    if b == 0:
                        pe.wait_ge(f_in, 16)
                    vec_has(("uT", 3, b))
                    fi, g = act_bank(("fi", b)), act_bank(("g", b))
                    gates = ((fi[:, 0:256], "wf"), (fi[:, 256:512], "wi"), (g[:, 0:256], "wc"))
                    for o, w in gates:
                        pe.matmul(o, F[w], uT[1][:, b, :], start=(w != "wi"), stop=False, skip_group_check=True)
                    pe.wait_ge(cell_ready, b + 1)
                    for k, (o, w) in enumerate(gates):
                        last = pe.matmul(o, uh[:, k, :], cell[:, b % 2, :], start=False, stop=True, skip_group_check=True)
                    last.then_inc(act_full, 2)

            pe.wait_ge(cell_ready, B + 1)
            for p in range(2):
                ps_h = act_bank(("h", p))
                for t in range(2):
                    pe.matmul(ps_h[:, t * 256:(t + 1) * 256], F["wo"], uT[1][:, 2 * p + t, :], start=True, stop=False)
                    last = pe.matmul(ps_h[:, t * 256:(t + 1) * 256], uh[:, 3, :], cell[:, 0, :], start=False, stop=True)
                last.then_inc(act_full, 1)
            for b in range(B):
                act_has(("h", b // 2))
                t = vec_bank(("hrow", b))
                for hf in range(2):
                    last = pe.transpose(t[:, hf * P:(hf + 1) * P], hT[:, b, hf * P:(hf + 1) * P], ident)
                last.then_inc(vec_full, 1)

            pe.wait_ge(wa_ready, 1)
            for p in range(2):
                for b in (2 * p, 2 * p + 1):
                    rows_turn(4, b)
                act_has(("uT", 4, 2 * p + 1))
                for k in range(2):
                    for s, w in enumerate((wa32, wrot)):
                        t = vec_bank(("qk", p, k, s))
                        pe.matmul(t, w[:, k * P:(k + 1) * P], uT[0][:, 2 * p:2 * p + 2, :], start=True, stop=True).then_inc(vec_full, 1)
                for b in (2 * p, 2 * p + 1):
                    t = act_bank(("av", b))
                    for hf in range(2):
                        last = pe.matmul(t[:, hf * P:(hf + 1) * P], uT[0][:, b, hf * P:(hf + 1) * P], wa32[:, 256:384], start=True, stop=True)
                    last.then_inc(act_full, 1)
            pe.wait_ge(h_in, 16)
            pe.wait_ge(b_in, 16)
            for p in range(2):
                for k in range(2):
                    pe.wait_ge(lead_ready, 2 * p + k + 1)
                    pe.wait_ge(rest_ready, 2 * p + k + 1)
                    for j in range(4):
                        t = act_bank(("st", p, k, j)) if k == 0 else vec_bank(("st", p, k, j))
                        for s in range(2):
                            sel = KH[("selq1", "selq2", "selk1", "selk2")[2 * k + s]][:, j * P:(j + 1) * P]
                            last = pe.matmul(t, sel, qh[:, k, s, p * 512:(p + 1) * 512], start=(s == 0), stop=(s == 1))
                        last.then_inc(vec_full if k else act_full, 1)

            for kind, b, i in LORDER:
                p, c, pair = b, i, (2 * b, 2 * b + 1)
                n, r, at = 4 * b + i, 32 * i, b * S
                if kind == "row":
                    if n % 4 == 0:
                        act_has(("st", b // 2, 0, 3))
                        vec_has(("st", b // 2, 1, 3))
                    mask = KB["mask_row"].unsqueeze(1)
                    t = vec_bank(("row", b, i, 0)).rearrange("p (j k) -> p j k", j=4)
                    pe.matmul(t, KB["ident"], mask.broadcast_to([P, 4, P]), start=True, stop=False, skip_group_check=True)
                    for j in range(4):
                        last = pe.matmul(t[:, j, :], qst[r:r + 32, 0, j, at:at + P], kst[r:r + 32, j, at:at + P],
                                         start=False, stop=True, skip_group_check=True)
                    last.then_inc(vec_full, 1)
                    for jj in range(2):
                        t = vec_bank(("row", b, i, 1 + jj)).rearrange("p (j k) -> p j k", j=2)
                        pe.matmul(t[:, :, P:S], KB["ident"], mask.broadcast_to([P, 2, P]), start=True, stop=False, skip_group_check=True)
                        for j in range(2):
                            last = pe.matmul(t[:, j, :], qst[r:r + 32, 0, 2 * jj + j, at + P:at + S], kst[r:r + 32, 2 * jj + j, at:at + S],
                                             start=False, stop=True, skip_group_check=True)
                        last.then_inc(vec_full, 1)
                elif kind == "stack":
                    pe.wait_ge(mneg_ready, b + 1)
                    for jj in range(2):
                        t = act_bank(("st2", b, jj)).rearrange("p (j q) -> p j q", j=2)
                        for j in (2 * jj, 2 * jj + 1):
                            o = t[:, j % 2, :]
                            pe.matmul(o, KH["selq1"][:, j * P:(j + 1) * P], qh[:, 0, 0, at:at + S], start=True, stop=False, skip_group_check=True)
                            pe.matmul(o, KH["selq2"][:, j * P:(j + 1) * P], qh[:, 0, 1, at:at + S], start=False, stop=False, skip_group_check=True)
                            for qt in range(2):
                                last = pe.matmul(o[:, qt * P:(qt + 1) * P], mneg[:, b % 2, qt, j, :], KH["ident"], start=False, stop=True,
                                                 skip_group_check=True)
                        last.then_inc(act_full, 1)
                elif kind == "col":
                    if i == 0:
                        act_has(("st2", b, 1))
                    mask = KB["mask_col"].unsqueeze(1)
                    for jj in range(2):
                        t = act_bank(("col", b, i, jj)).rearrange("p (j q) -> p j q", j=2)
                        pe.matmul(t[:, :, 0:P], KB["ident"], mask.broadcast_to([P, 2, P]), start=True, stop=False, skip_group_check=True)
                        for j in range(2):
                            last = pe.matmul(t[:, j, :], kst[r:r + 32, 2 * jj + j, at:at + P], qst[r:r + 32, 1, 2 * jj + j, at:at + S],
                                             start=False, stop=True, skip_group_check=True)
                        last.then_inc(act_full, 1)
                    t = act_bank(("col", b, i, 2)).rearrange("p (j q) -> p j q", j=4)
                    pe.matmul(t, KB["ident"], mask.broadcast_to([P, 4, P]), start=True, stop=False, skip_group_check=True)
                    for j in range(4):
                        last = pe.matmul(t[:, j, :], kst[r:r + 32, j, at + P:at + S], qst[r:r + 32, 1, j, at + P:at + S],
                                         start=False, stop=True, skip_group_check=True)
                    last.then_inc(act_full, 1)
                elif kind == "pv":
                    act_has(("col", b, i, 2))
                    if n == 0:
                        pe.wait_ge(va1_ones, 1)
                    t = act_bank(("apv", b, i))
                    for j in range(4):
                        o, h, prob = t[32 * j:32 * j + 32, 0:S], 4 * j + i, pT1[:, n % 3, :]
                        pe.matmul(o, va1[:, 2 * b, h, :], prob[:, j * S:(j + 1) * S], start=True, stop=False)
                        last = pe.matmul(o[:, P:S], va1[:, 2 * b + 1, h, :], prob[:, 1024 + j * P:1024 + (j + 1) * P], start=False, stop=True)
                    last.then_inc(act_full, 1)
                elif kind == "back":
                    act_has(("apv", b, i))
                    t = vec_bank(("aback", b, i))
                    for qt in range(2):
                        last = pe.transpose(t[:, qt * P:(qt + 1) * P], oc1[:, n % 2, qt * P:(qt + 1) * P], ident)
                    last.then_inc(vec_full, 1)
                elif kind == "turn":
                    vec_has(("aback", b, 3))
                    t = act_bank(("oT1", b))
                    for qt in range(2):
                        last = pe.transpose(t[:, qt * P:(qt + 1) * P], or1[:, b % 2, qt, :], ident)
                    last.then_inc(act_full, 1)
                elif kind == "out":
                    act_has(("oT1", b))
                    t = vec_bank(("out4", b))
                    for qt in range(2):
                        last = pe.matmul(t[:, qt * P:(qt + 1) * P], oT1[:, b % 2, qt * P:(qt + 1) * P], wa32[:, 384:512], start=True, stop=True)
                    last.then_inc(vec_full, 1)
                elif kind in ("turn5", "turn6"):
                    for b in pair:
                        rows_turn(int(kind[-1]), b)
                elif kind == "queries":
                    for b in pair:
                        act_has(("uT", 5, b))
                        corr_rows("q", b)
                elif kind == "spectra":
                    act_has(("cr", "q", pair[1]))
                    t = vec_bank(("fq", p))
                    for f in range(2):
                        for hf in range(2):
                            at = hf * 384 + f * P
                            last = pe.matmul(t[:, f * S:(f + 1) * S], K["dft"][:, at:at + P], qr[:, hf, 2 * p:2 * p + 2, :],
                                             start=(hf == 0), stop=(hf == 1))
                    last.then_inc(vec_full, 1)
                elif kind == "delays":
                    t = vec_bank(("corr", p))
                    pe.wait_ge(prod_ready, p + 1)
                    for b in range(2):
                        at = (2 * p + b) * P
                        pe.matmul(t[:, b * S:(b + 1) * S], prod[:, 0, at:at + P], K["idft"][:, 0:S], start=True, stop=False)
                        last = pe.matmul(t[:, b * S:(b + 1) * S], prod[:, 1, at:at + P], K["idft"][:, S:2 * S], start=False, stop=True)
                    last.then_inc(vec_full, 1)
                elif kind == "mix":
                    pe.wait_ge(mbd_ready, p + 1)
                    t = act_bank(("mix", p))
                    for b in pair:
                        last = pe.matmul(t[:, b % 2 * P:(b % 2 + 1) * P], mbd[:, b, :, :].rearrange("p h j -> p (h j)"), K["permute"],
                                         start=True, stop=True)
                    last.then_inc(act_full, 1)
                elif kind == "out5":
                    act_has(("mix", p))
                    for b in pair:
                        t = vec_bank(("out5", b))
                        for tile in range(2):
                            for hf in range(2):
                                last = pe.matmul(t[:, tile * P:(tile + 1) * P], place[:, b, tile, hf, :], vo[:, b, hf * P:(hf + 1) * P],
                                                 start=(hf == 0), stop=(hf == 1))
                        last.then_inc(vec_full, 1)
                elif kind == "logits":
                    if p == 0:
                        pe.wait_ge(e_in, 16)
                    act_has(("uT", 6, pair[1]))
                    t = act_bank(("gl", p))
                    for tile in range(4):
                        last = pe.matmul(t[:, tile * E:(tile + 1) * E], uT[0][:, 2 * p + tile // 2, tile % 2 * P:(tile % 2 + 1) * P],
                                         G["gate"], start=True, stop=True)
                    last.then_inc(act_full, 1)
                elif kind == "up":
                    w1, w3 = (G["e_win"][:, c * P:(c + 1) * P], G["e_vin"][:, c * P:(c + 1) * P]) if c < 8 else (G["ws_in"], G["vs_in"])
                    t = act_bank(("hin", p, c))
                    pe.matmul(t, w1, uT[0][:, 2 * p:2 * p + 2, :], start=True, stop=True).then_inc(act_full, 1)
                    t = vec_bank(("vin", p, c))
                    pe.matmul(t, w3, uT[0][:, 2 * p:2 * p + 2, :], start=True, stop=True).then_inc(vec_full, 1)
                    if c < 8:
                        vec_has(("cbT", p))
                        t = vec_bank(("cw", p, c))
                        pe.matmul(t, KB["expand"][0:48, c * P:(c + 1) * P], combT[0:48, p * 512:(p + 1) * 512], start=True, stop=True)\
                          .then_inc(vec_full, 1)
                elif kind == "choice":
                    pe.wait_ge(comb_ready, p + 1)
                    t = vec_bank(("cbT", p)).bitcast(BF16)
                    for tile in range(4):
                        last = pe.transpose(t[0:48, tile * P:(tile + 1) * P], comb3[:, 4 * p + tile, :, :].rearrange("p s e -> p (s e)"), KB["ident"])
                    last.then_inc(vec_full, 1)
                elif kind == "down":
                    vec_has(("cw", p, 7))
                    t = vec_bank(("out6", c))
                    for hf in range(2):
                        at = c * S + hf * P
                        for k in range(HC):
                            last = pe.matmul(t[:, hf * P:(hf + 1) * P], hid[:, k, at:at + P], G["w_out"][:, k * P:(k + 1) * P],
                                             start=(k == 0), stop=(k == HC - 1))
                    last.then_inc(vec_full, 1)

        @block.scalar
        def _(act):
            steps = 0

            def after(ins):
                nonlocal steps
                steps += 1
                ins.then_inc(act_step, 1)
                act.wait_ge(act_step, steps)

            def full(key):
                act.wait_ge(act_full, for_act.number[key] + 1)

            def vec_bank_full(key):
                act.wait_ge(vec_full, for_vec.number[key] + 1)

            def vec_bank_read(key):
                act.wait_ge(vec_free, for_vec.number[key] + 1)

            def copy_out(key, dst, src, scale=1.0):
                full(key)
                act.activation(dst, src, ACT.Copy, scale=scale).then_inc(act_free, 1)

            def copy_uT(k, b):
                copy_out(("uT", k, b), uT[ROW[k]][:, b, :], pbank(for_act, ("uT", k, b), S))

            def values(s, tile):
                key = ("xv", s, tile)
                full(key)
                dst = (val[:, tile % 4, :, :] if s else vac[:, tile, :, :]).rearrange("p c (s d) -> p c s d", s=3)[:, :, 0::2, :]
                act.activation(dst, pbank(for_act, key).rearrange("p (c s d) -> p c s d", c=XC, s=2), ACT.Copy,
                               scale=maskf[:, tile:tile + 1] if s == 0 else 1.0).then_inc(act_free, 1)

            def head_square(s, tile):
                u = UNIT[s, tile]
                vec_bank_full(("kr", u))
                if u >= 2:
                    act.wait_ge(parts_ready, u - 1)
                act.activation(sqr[:, u % 2, :], pbank(for_vec, ("kr", u)), ACT.Square).then_inc(sq_ready, 1)

            def head_lead(s, tile):
                u = UNIT[s, tile]
                if s == 2:
                    act.wait_ge(q_scaled, tile + 1)
                else:
                    vec_bank_read(("kr", u))
                if u >= 2:
                    act.wait_ge(act_full, for_act.number[("qT", u - 2)] + 1 if ("qT", u - 2) in for_act.number else for_act.number[("kT", u - 2)] + 1)
                if s == 2:
                    rows = sqr[:, u % 2, :].rearrange("p (h d) -> p h d", h=XH).unsqueeze(2).broadcast_to([P, XH, 2, XD])
                    dst = parts[:, u % 2, 0:1024].rearrange("p (h s d) -> p h s d", h=XH, s=2)
                else:
                    rows = sqr[:, u % 2, :].rearrange("p (c s d) -> p c s d", c=XC, s=2)
                    dst = parts[:, u % 2, 0:1024].rearrange("p (c s d) -> p c s d", c=XC, s=4)[:, :, 0::3, :]
                act.activation(dst, rows, ACT.Copy).then_inc(lead_parts, 1)

            def head_turned(s, tile):
                u = UNIT[s, tile]
                at = (tile % 4 if s else tile) * P
                copy_out(("kT", u), (kc, kl, q1)[s][:, :, at:at + P], pbank(for_act, ("kT", u)).bitcast(F16).rearrange("p (h t) -> p h t", h=XH))
                if s == 2:
                    copy_out(("qT", u), q2[:, :, at:at + P], pbank(for_act, ("qT", u), 256).bitcast(F16).rearrange("p (c t) -> p c t", c=XC))

            def corr_rows(name, b):
                copy_out(("cr", name, b), {"q": qr, "k": kr, "v": vr}[name][:, :, b, :],
                         pbank(for_act, ("cr", name, b), 256).rearrange("p (h n) -> p h n", h=2))

            for b in range(B):
                copy_uT(0, b)
            act.wait_ge(m_in, 16)
            act.activation(ea, M["a_log"], ACT.Exp).then_inc(ea_ready, 1)
            act.wait_ge(dt_abs, 1)
            after(act.activation(dte, dta, ACT.Exp, scale=-1.0))
            act.activation(dtl, dte, ACT.Ln, bias=1.0).then_inc(dt_log, 1)

            waiting = []

            def conv_silu():
                p, c = waiting.pop(0)
                vec_bank_read(("in", p, c))
                o = xc[:, c - 2, p * 512:(p + 1) * 512]
                act.activation(o, o, ACT.Silu).then_inc(conv_ready, 1)

            for kind, b, c in ORDER:
                h = c
                if kind == "in" and c >= 2:
                    key, k = ("in", b, c), c - 2
                    vec_bank_full(key)
                    act.activation(xc[:, k, b * 512:(b + 1) * 512], pbank(for_vec, key), ACT.Identity, bias=M["conv_b"][:, k:k + 1],
                                   scale=M["conv_w"][:, 4 * k + 3:4 * k + 4]).then_inc(tap_ready, 1)
                    waiting.append((b, c))
                    if len(waiting) > 2:
                        conv_silu()
                elif kind == "in":
                    full(("in", b, c))
                    act.activation(zs[:, c, b * 512:(b + 1) * 512], pbank(for_act, ("in", b, c)), ACT.Silu).then_inc(act_free, 1)
                    if waiting:
                        conv_silu()
                elif kind == "context":
                    copy_out(("cT", b), cT[:, b, :], pbank(for_act, ("cT", b), S))
                    act.wait_ge(xw_in, 16)
                    full(("uT", 1, b))
                    act.activation(cnT[:, b, :], pbank(for_act, ("uT", 1, b), S), ACT.Identity, bias=X0["lnx_b"], scale=X0["lnx_w"])\
                       .then_inc(act_free, 1)
                elif kind == "value":
                    if b == 0 and c == 0:
                        act.wait_ge(vac_mask, 1)
                    values(b, c)
                elif kind == "head":
                    head_square(b, c)
                elif kind == "parts":
                    head_lead(b, c)
                elif kind == "turn":
                    head_turned(b, c)
                elif kind == "front":
                    vec_bank_read(("bc", b, 1))
                    act.activation(eL[:, b % 2, :, :], eL[:, b % 2, :, :], ACT.Exp).then_inc(decay_ready, 1)
                elif kind == "back":
                    act.wait_ge(gated, b + 1)
                    if b >= 1:
                        vec_bank_full(("out0", b - 1))
                    act.activation(ysq, yg, ACT.Square).then_inc(ysq_ready, 1)
                elif kind == "sim":
                    n = b * XH + h
                    if n == 0:
                        act.wait_ge(shift_ready, 1)
                    act.wait_ge(act_full, for_act.number[("sim", n, 1)] + 1)
                    if n >= 3:
                        vec_bank_full(("pv", n - 3))
                    act.activation(pT[:, n % 3, :, :], pbank(for_act, ("sim", n, 0), 1024).rearrange("p (k q) -> p k q", k=4), ACT.Exp,
                                   bias=shift[:, 1:2], scale=8.0 / 1024).then_inc(act_free, 2)
                elif kind == "pv":
                    n = b * XH + h
                    vec_bank_full(("pv", n))
                    if n >= 4:
                        vec_bank_read(("pv", n - 4 | 1))
                    r = h % 2 * 64
                    act.activation(den[r:r + 64, n // 2 % 2, :], pbank(for_vec, ("pv", n), S)[64 - r:128 - r, :], ACT.Copy).then_inc(den_ready, 1)
                elif kind == "corr_rows":
                    corr_rows(b, h)
                elif kind == "corr_vo":
                    for bp in range(2):
                        copy_out(("vo", bp), vo[:, 2 * bp:2 * bp + 2, :], pbank(for_act, ("vo", bp)).rearrange("p (b n) -> p b n", b=2))
                elif kind == "corr_spectra":
                    for f in range(3):
                        copy_out(("fk", f), pr[:, f, :], pbank(for_act, ("fk", f)))
                elif kind == "gates":
                    if b == 0:
                        act.wait_ge(halves_ready, 1)
                    full(("g", b))
                    if b >= 2:
                        act.wait_ge(cell_ready, b)
                    fi = pbank(for_act, ("fi", b))
                    act.activation(gat[:, b % 2, 0, :], fi[:, 0:256], ACT.Tanh, bias=halfb[:, 0:1], scale=0.5)
                    act.activation(gat[:, b % 2, 1, :], fi[:, 256:512], ACT.Tanh, bias=halfb[:, 1:2], scale=0.5).then_inc(act_free, 1)
                    act.activation(gat[:, b % 2, 2, :], pbank(for_act, ("g", b), 256), ACT.Tanh, bias=F["bc"]).then_inc(act_free, 1)

            for p in range(2):
                full(("h", p))
                act.activation(hT[:, 2 * p:2 * p + 2, :], pbank(for_act, ("h", p)).rearrange("p (t n) -> p t n", t=2), ACT.Tanh,
                               bias=F["bo"]).then_inc(act_free, 1)

            for p in range(2):
                for b in (2 * p, 2 * p + 1):
                    copy_uT(4, b)
                for b in (2 * p, 2 * p + 1):
                    copy_out(("av", b), va1[:, 2 * b:2 * b + 2, :, 0:AD], pbank(for_act, ("av", b), 256).rearrange("p (t h d) -> p t h d", t=2, h=AH))
                for k in range(2):
                    act.wait_ge(rope_ready, 2 * p + k + 1)
                    act.activation(qh[:, k, 0, p * 512:(p + 1) * 512], rot[:, k, 0, :], ACT.Copy).then_inc(lead_ready, 1)
            for p in range(2):
                for j in range(4):
                    copy_out(("st", p, 0, j), qst[:, 0, j, p * 512:(p + 1) * 512], pbank(for_act, ("st", p, 0, j)))
            used = []
            for kind, b, i in LORDER:
                p, c, pair = b, i, (2 * b, 2 * b + 1)
                n = 4 * b + i
                if kind == "stack":
                    for jj in range(2):
                        copy_out(("st2", b, jj), qst[:, 1, 2 * jj:2 * jj + 2, b * S:(b + 1) * S],
                                 pbank(for_act, ("st2", b, jj)).rearrange("p (j q) -> p j q", j=2))
                elif kind == "col":
                    for part in range(3):
                        key = ("col", b, i, part)
                        full(key)
                        act.activation(pT1[:, n % 3, part * 512:(part + 1) * 512], pbank(for_act, key), ACT.Exp, scale=1.0 / 11.3125)\
                           .then_inc(act_free, 1)
                elif kind == "pv":
                    if n >= 2:
                        vec_bank_full(("aback", (n - 2) // 4, (n - 2) % 4))
                    copy_out(("apv", b, i), oc1[:, n % 2, :], pbank(for_act, ("apv", b, i), 256))
                elif kind == "turn":
                    if b >= 2:
                        vec_bank_full(("out4", b - 2))
                    copy_out(("oT1", b), oT1[:, b % 2, :], pbank(for_act, ("oT1", b), 256))
                elif kind in ("turn5", "turn6"):
                    for b in pair:
                        copy_uT(int(kind[-1]), b)
                elif kind == "queries":
                    for b in pair:
                        corr_rows("q", b)
                elif kind == "weights":
                    act.wait_ge(corr_diff, p + 1)
                    act.activation(tope[:, 2 * p:2 * p + 2, 0:TOPC], delta[:, 2 * p:2 * p + 2, 0:TOPC], ACT.Exp).then_inc(corr_exp, 1)
                elif kind == "mix":
                    full(("mix", p))
                    if p == 0:
                        act.wait_ge(place_zero, 1)
                    mix = pbank(for_act, ("mix", p), 256).rearrange("p (b t g) -> p b t g", b=2, t=2)
                    for hf in range(2):
                        last = act.activation(place[:, 2 * p:2 * p + 2, :, hf, hf::2], mix, ACT.Copy)
                    last.then_inc(act_free, 1)
                elif kind == "logits":
                    full(("gl", p))
                    act.activation(gex[:, 4 * p:4 * p + 4, :], pbank(for_act, ("gl", p), 4 * E).rearrange("p (t e) -> p t e", t=4), ACT.Exp,
                                   scale=-1.0).then_inc(act_free, 1)
                elif kind == "up":
                    key = ("hin", p, c)
                    full(key)
                    if len(used) >= 2:
                        vec_bank_read(used[-2])
                    act.activation(sil[:, len(used) % 2, :], pbank(for_act, key), ACT.Silu).then_inc(act_free, 1)
                    used.append(("cw" if c < 8 else "vin", p, c))

        @block.vector
        def _(vec):
            steps = 0

            def after(ins):
                nonlocal steps
                steps += 1
                ins.then_inc(vec_step, 1)
                vec.wait_ge(vec_step, steps)

            def full(key):
                vec.wait_ge(vec_full, for_vec.number[key] + 1)

            def own(key):
                vec.wait_ge(vec_free, for_vec.number[key] + 1)

            def act_read(key):
                vec.wait_ge(act_free, for_act.number[key] + 1)

            def var(k, b, src):
                vec.bn_stats(stats[:, k, 2 * b, :], src[:, 2 * b, :])
                after(vec.bn_stats(stats[:, k, 2 * b + 1, :], src[:, 2 * b + 1, :]))
                vec.bn_aggr(mv[:, k, 2 * b, :], stats[:, k, 2 * b, :])
                vec.bn_aggr(mv[:, k, 2 * b + 1, :], stats[:, k, 2 * b + 1, :]).then_inc(ln6_var if k == 6 else ln_var, 1)

            def rows(k, b, src):
                vec.wait_ge(ln6_rstd if k == 6 else ln_rstd, norm_count(k, b))
                for t in (2 * b, 2 * b + 1):
                    last = vec.tensor_scalar(urow[ROW[k]][:, t, :], src[:, t, :], mv[:, k, t, 0:1], rstd[:, k, t:t + 1],
                                             ALU.subtract, ALU.mult)
                last.then_inc(ln6_rows if k == 6 else ln_rows, 1)

            def residual(key, b):
                full(key)
                xb = x[:, 2 * b:2 * b + 2, :]
                vec.tensor_tensor(xb, xb, pbank(for_vec, key, 256).rearrange("p (t n) -> p t n", t=2), ALU.add).then_inc(vec_free, 1)
                own(key)

            vec.wait_ge(x_in, 16)
            for b in range(B):
                var(0, b, x)
            vec.wait_ge(c_in, 16)
            for b in range(B):
                rows(0, b, x)
            for b in range(B):
                var(1, b, cx)
            vec.wait_ge(m_in, 16)
            full("dt")
            vec.tensor_tensor(dtx, pbank(for_vec, "dt", 32).rearrange("p (t h) -> p t h", h=MH),
                              M["dt_bias"].unsqueeze(1).broadcast_to([P, NT, MH]), ALU.add).then_inc(vec_free, 1)
            own("dt")
            vec.scalar_tensor_tensor(out=dta, in0=dtx, scalar=-1.0, in1=dtx, op0=ALU.mult, op1=ALU.max).then_inc(dt_abs, 1)
            for b in range(B):
                rows(1, b, cx)
            for c in range(2):
                vec.tensor_scalar(ow2[:, c, :], M["out_w"][:, c * P:(c + 1) * P], M["norm_w"][:, c:c + 1], None, ALU.mult)
            vec.wait_ge(dt_log, 1)
            after(vec.scalar_tensor_tensor(out=dt, in0=dtx, scalar=0.0, in1=dtl, op0=ALU.max, op1=ALU.add))
            vec.wait_ge(ea_ready, 1)
            vec.scalar_tensor_tensor(out=da, in0=dt, scalar=-1.0, in1=ea.unsqueeze(1).broadcast_to([P, NT, MH]),
                                     op0=ALU.mult, op1=ALU.mult).then_inc(da_ready, 1)
            def head_sum(s, tile):
                u = UNIT[s, tile]
                vec.wait_ge(sq_ready, u + 1)
                vec.tensor_reduce(ssq[:, s, tile, :], sqr[:, u % 2, :].rearrange("p (h d) -> p h d", h=XH), AX.X, ALU.add).then_inc(ssq_ready, 1)

            def head_norm(s, tile):
                u = UNIT[s, tile]
                vec.wait_ge(rnk_ready, u + 1)
                full(("kr", u))
                row = sqr[:, u % 2, :].rearrange("p (h d) -> p h d", h=XH)
                vec.tensor_tensor(row, pbank(for_vec, ("kr", u)).rearrange("p (h d) -> p h d", h=XH),
                                  rnk[:, s, tile, :].unsqueeze(2).broadcast_to([P, XH, XD]), ALU.mult).then_inc(vec_free, 1)
                if s == 2:
                    own(("kr", u))
                    vec.tensor_tensor(row, row, qks[:].unsqueeze(1).broadcast_to([P, XH, XD]), ALU.mult).then_inc(q_scaled, 1)

            def head_rest(s, tile):
                u = UNIT[s, tile]
                vec.wait_ge(lead_parts, u + 1)
                if s == 2:
                    lead = parts[:, u % 2, 0:1024].rearrange("p (h s d) -> p h s d", h=XH, s=2)[:, :, 0, :]
                    vec.tensor_tensor(parts[:, u % 2, 1024:1536].rearrange("p (h d) -> p h d", h=XH),
                                      sqr[:, u % 2, :].rearrange("p (h d) -> p h d", h=XH), lead, ALU.subtract).then_inc(parts_ready, 1)
                else:
                    four = parts[:, u % 2, 0:1024].rearrange("p (c s d) -> p c s d", c=XC, s=4)
                    vec.tensor_tensor(four[:, :, 1:3, :], sqr[:, u % 2, :].rearrange("p (c s d) -> p c s d", c=XC, s=2), four[:, :, 0::3, :],
                                      ALU.subtract).then_inc(parts_ready, 1)

            vec.wait_ge(xw_in, 16)
            after(vec.tensor_tensor(qks[:], X0["q_scale_row"], X0["k_scale_row"], ALU.mult))
            after(vec.tensor_reduce(shift[:, 0:1], qks[:], AX.X, ALU.max, apply_absolute_value=True))
            vec.tensor_scalar(shift[:, 1:2], shift[:, 0:1], -8.0, None, ALU.mult).then_inc(shift_ready, 1)
            vec.wait_ge(k_in, 16)
            vec.tensor_copy(ident16, ident).then_inc(ident16_set, 1)
            taps = 0
            for kind, b, c in ORDER:
                h = c
                if kind == "in" and c >= 2:
                    k, key = c - 2, ("in", b, c)
                    taps += 1
                    vec.wait_ge(tap_ready, taps)
                    full(key)
                    src = pbank(for_vec, key).rearrange("p (b t) -> p b t", b=2)
                    dst = xc[:, k, b * 512:(b + 1) * 512].rearrange("p (b t) -> p b t", b=2)
                    for j in (1, 2):
                        after(vec.scalar_tensor_tensor(out=dst[:, :, j:], in0=src[:, :, 0:S - j], scalar=M["conv_w"][:, 4 * k + 3 - j:4 * k + 4 - j],
                                                       in1=dst[:, :, j:], op0=ALU.mult, op1=ALU.add))
                    vec.scalar_tensor_tensor(out=dst[:, :, 3:], in0=src[:, :, 0:S - 3], scalar=M["conv_w"][:, 4 * k:4 * k + 1],
                                             in1=dst[:, :, 3:], op0=ALU.mult, op1=ALU.add).then_inc(vec_free, 1)
                elif kind == "cum":
                    full("cum")
                    c32 = pbank(for_vec, "cum", 32).rearrange("p (t h) -> p t h", h=MH)
                    vec.tensor_copy(cum, c32).then_inc(vec_free, 1)
                    own("cum")
                elif kind == "head":
                    head_sum(b, c)
                elif kind == "norm":
                    head_norm(b, c)
                elif kind == "parts":
                    head_rest(b, c)
                elif kind == "front":
                    v = b % 2
                    full(("xrow", b))
                    vec.tensor_tensor(xdt[:, 2 * v:2 * v + 2, :].rearrange("p t (h n) -> p t h n", h=MH),
                                      pbank(for_vec, ("xrow", b)).rearrange("p (t h n) -> p t h n", t=2, h=MH),
                                      dt[:, 2 * b:2 * b + 2, :].unsqueeze(3).broadcast_to([P, 2, MH, 64]), ALU.mult).then_inc(vec_free, 1)
                    full(("G", b))
                    if b >= 1:
                        vec.wait_ge(w_ready, b)
                    vec.tensor_tensor(gm, pbank(for_vec, ("G", b), 384), K["gmask"], ALU.mult).then_inc(vec_free, 1)
                    for hf in range(2):
                        full(("bc", b, hf))
                        sums = pbank(for_vec, ("bc", b, hf)).rearrange("p (h l) -> p h l", h=MH)
                        if hf == 1:
                            vec.tensor_tensor(eL[:, v, :, P:256], sums, cum[:, 2 * b, :].unsqueeze(2).broadcast_to([P, MH, P]), ALU.subtract)
                        for h in range(MH):
                            last = vec.tensor_scalar(eL[:, v, h, 256 * hf:256 * hf + P], sums[:, h, :], cum[:, 2 * b + hf, h:h + 1], 0.0,
                                                     ALU.subtract, ALU.min)
                        last.then_inc(vec_free, 1)
                elif kind == "decay":
                    vec.wait_ge(decay_ready, b + 1)
                    v = b % 2
                    vec.tensor_tensor(eL[:, v, :, :], eL[:, v, :, :], gm.unsqueeze(1).broadcast_to([P, MH, 384]), ALU.mult)\
                       .then_inc(w_ready, 1)
                elif kind == "back":
                    key = ("Y", b)
                    full(key)
                    for c in range(2):
                        last = vec.scalar_tensor_tensor(out=yg[:, c, :], in0=xc[:, c, b * S:(b + 1) * S], scalar=M["skip"][:, c:c + 1],
                                                        in1=pbank(for_vec, key)[:, c * S:(c + 1) * S], op0=ALU.mult, op1=ALU.add)
                    last.then_inc(vec_free, 1)
                    own(key)
                    vec.tensor_tensor(yg, yg, zs[:, :, b * S:(b + 1) * S], ALU.mult).then_inc(gated, 1)
                elif kind == "out":
                    key = ("out0", b)
                    full(key)
                    vec.tensor_scalar(msq[:, 2 * b:2 * b + 2], pbank(for_vec, key)[:, 256:258], 1.0 / 256, EPS, ALU.mult, ALU.add).then_inc(msq_ready, 1)
                    vec.wait_ge(rms_ready, b + 1)
                    for t in range(2):
                        xb = x[:, 2 * b + t, :]
                        last = vec.scalar_tensor_tensor(out=xb, in0=pbank(for_vec, key)[:, t * P:(t + 1) * P], scalar=rms[:, 2 * b + t:2 * b + t + 1],
                                                        in1=xb, op0=ALU.mult, op1=ALU.add)
                    last.then_inc(vec_free, 1)
                    own(key)
                    var(2, b, x)
                elif kind == "rows2":
                    rows(2, b, x)
                elif kind == "halves":
                    vec.wait_ge(f_in, 16)
                    for g, w in enumerate(("uf", "ui", "uc", "uo")):
                        vec.tensor_scalar(uh[:, g, :], F[w], 0.5, None, ALU.mult)
                    vec.tensor_scalar(halfb[:, 0:1], F["bf"], 0.5, None, ALU.mult)
                    vec.tensor_scalar(halfb[:, 1:2], F["bi"], 0.5, None, ALU.mult).then_inc(halves_ready, 1)
                    vec.tensor_scalar(cell[:, 0, :], F["in_c"].broadcast_to([P, 256]), 2.0, None, ALU.mult).then_inc(cell_ready, 1)
                    vec.wait_ge(cell_ready, 1)
                elif kind == "latent":
                    key = ("uT", 2, b)
                    full(key)
                    vec.tensor_scalar(uT[0][:, b, :], pbank(for_vec, key, S), X0["lnl_w"], X0["lnl_b"], ALU.mult, ALU.add).then_inc(vec_free, 1)
                elif kind == "pv" and h % 2:
                    n, v = b * XH + h, h // 2 % 2
                    vec.wait_ge(den_ready, n + 1)
                    full(("pv", n))
                    if n > 1:
                        own(("pv", n - 2))
                    after(vec.reciprocal(rec, den[:, v, :]))
                    for r in (0, 64):
                        vec.tensor_tensor(oT[r:r + 64, (XC * b + h // 2) % 5, :], pbank(for_vec, ("pv", n - 1 + r // 64), S)[r:r + 64, :],
                                          rec[r:r + 64, :], ALU.mult).then_inc(vec_free, 1)
                elif kind == "result":
                    key = ("out1", b)
                    full(key)
                    o = pbank(for_vec, key, 256).rearrange("p (q n) -> p q n", q=2)
                    vec.bn_stats(ostat[:, 2 * b, :], o[:, 0, :])
                    after(vec.bn_stats(ostat[:, 2 * b + 1, :], o[:, 1, :]))
                    vec.bn_aggr(omv[:, 2 * b, :], ostat[:, 2 * b, :])
                    vec.bn_aggr(omv[:, 2 * b + 1, :], ostat[:, 2 * b + 1, :]).then_inc(ovar_ready, 1)
                    vec.wait_ge(orstd_ready, b + 1)
                    for q in range(2):
                        last = vec.tensor_scalar(on[:, q, :], o[:, q, :], omv[:, 2 * b + q, 0:1], ort[:, 1, 2 * b + q:2 * b + q + 1],
                                                 ALU.subtract, ALU.mult)
                    last.then_inc(vec_free, 1)
                    own(key)
                    xb = x[:, 2 * b:2 * b + 2, :]
                    after(vec.tensor_tensor(on, on, X0["lno_w"].unsqueeze(1).broadcast_to([P, 2, P]), ALU.mult))
                    after(vec.tensor_tensor(on, on, X0["lno_b"].unsqueeze(1).broadcast_to([P, 2, P]), ALU.add))
                    after(vec.tensor_tensor(xb, xb, on, ALU.add))
                    var(3, b, x)
                elif kind == "rows3":
                    rows(3, b, x)
                elif kind == "turn3":
                    key = ("uT", 3, b)
                    full(key)
                    vec.tensor_copy(uT[1][:, b, :], pbank(for_vec, key, S)).then_inc(vec_free, 1)
                elif kind == "cell":
                    act_read(("g", b))
                    g = gat[:, b % 2]
                    vec.scalar_tensor_tensor(out=mixa, in0=g[:, 0, :], scalar=1.0, in1=cell[:, b % 2, :], op0=ALU.add, op1=ALU.mult)
                    after(vec.scalar_tensor_tensor(out=mixb, in0=g[:, 1, :], scalar=1.0, in1=g[:, 2, :], op0=ALU.add, op1=ALU.mult))
                    vec.scalar_tensor_tensor(out=cell[:, (b + 1) % 2, :], in0=mixa, scalar=0.5, in1=mixb, op0=ALU.mult, op1=ALU.add)\
                       .then_inc(cell_ready, 1)
                    vec.wait_ge(cell_ready, b + 2)

            for b in range(B):
                residual(("hrow", b), b)
                var(4, b, x)

            vec.wait_ge(a_in, 16)
            vec.tensor_copy(wa32, w_a)
            turned, plain = wrot.rearrange("p (n s) -> p n s", s=2), w_a[:, 0:256].rearrange("p (n s) -> p n s", s=2)
            vec.tensor_scalar(turned[:, :, 0], plain[:, :, 1], -1.0, None, ALU.mult)
            vec.tensor_copy(turned[:, :, 1], plain[:, :, 0]).then_inc(wa_ready, 1)
            for b in range(B):
                rows(4, b, x)
            vec.wait_ge(r_in, 16)
            for p in range(2):
                for k in range(2):
                    if p == 1:
                        vec.wait_ge(rest_ready, k + 1)
                    for s, table in enumerate((R["cos"], R["sin"])):
                        key = ("qk", p, k, s)
                        full(key)
                        vec.tensor_tensor(rot[:, k, s, :].rearrange("p (b t) -> p b t", b=2), pbank(for_vec, key).rearrange("p (b t) -> p b t", b=2),
                                          table.unsqueeze(1).broadcast_to([P, 2, S]), ALU.mult).then_inc(vec_free, 1)
                    own(("qk", p, k, 1))
                    vec.tensor_tensor(rot[:, k, 0, :], rot[:, k, 0, :], rot[:, k, 1, :], ALU.add).then_inc(rope_ready, 1)
            for p in range(2):
                for j in range(4):
                    full(("st", p, 1, j))
                    vec.tensor_scalar(kst[:, j, p * 512:(p + 1) * 512], pbank(for_vec, ("st", p, 1, j)), K["sixteen"], None, ALU.add).then_inc(vec_free, 1)
            vec.wait_ge(mneg_zero, 1)
            ups = 0
            for kind, b, i in LORDER:
                p, c, pair = b, i, (2 * b, 2 * b + 1)
                two, tiles = slice(2 * p, 2 * p + 2), slice(4 * p, 4 * p + 4)
                n = 4 * b + i
                if kind == "row":
                    for part in range(3):
                        key, heads = ("row", b, i, part), (4, 2, 2)[part]
                        full(key)
                        dst = mx[:, b, 0, i, :] if part == 0 else mx[:, b, 1, i, 2 * part - 2:2 * part]
                        vec.tensor_reduce(dst, pbank(for_vec, key).rearrange("p (j k) -> p j k", j=heads), AX.X, ALU.max).then_inc(vec_free, 1)
                    if i == 3:
                        own(key)
                        if b >= 2:
                            vec.wait_ge(act_full, for_act.number[("st2", b - 2, 1)] + 1)
                        for q in range(2):
                            last = vec.tensor_scalar(mneg[:, b % 2, q, :, 24::32], mx[:, b, q, :, :].rearrange("p i j -> p j i"),
                                                     -1.0 / 16, None, ALU.mult)
                        last.then_inc(mneg_ready, 1)
                elif kind == "back":
                    key = ("aback", b, i)
                    full(key)
                    t = pbank(for_vec, key, 256).rearrange("p (q j n) -> p q j n", q=2, j=4)
                    d = rec1[:, b, :, 4 * i:4 * i + 4].unsqueeze(3)
                    after(vec.reciprocal(d, t[:, :, :, AD:AD + 1]))
                    o = or1[:, b % 2, :, :].rearrange("p q (j i d) -> p q j i d", j=4, i=4)[:, :, :, i, :]
                    vec.tensor_tensor(o, t[:, :, :, 0:AD], d.broadcast_to([P, 2, 4, AD]), ALU.mult).then_inc(vec_free, 1)
                elif kind == "out":
                    residual(("out4", b), b)
                    var(5, b, x)
                elif kind in ("rows5", "rows6"):
                    for b in pair:
                        rows(int(kind[-1]), b, x)
                elif kind == "spectra":
                    key, cols = ("fq", p), slice(p * S, (p + 1) * S)
                    full(key)
                    if p == 0:
                        act_read(("fk", 2))
                    aq, bq = pbank(for_vec, key)[:, 0:S], pbank(for_vec, key)[:, S:2 * S]
                    vec.tensor_tensor(sab[:, 0, cols], aq, pr[:, 0, cols], ALU.mult)
                    after(vec.scalar_tensor_tensor(out=sab[:, 1, cols], in0=bq, scalar=K["keep"], in1=pr[:, 1, cols], op0=ALU.mult, op1=ALU.mult))
                    after(vec.tensor_tensor(prod[:, 0, cols], sab[:, 0, cols], sab[:, 1, cols], ALU.add))
                    vec.scalar_tensor_tensor(out=sab[:, 0, cols], in0=aq, scalar=K["keep"], in1=pr[:, 1, cols], op0=ALU.mult, op1=ALU.mult)
                    vec.tensor_tensor(sab[:, 1, cols], bq, pr[:, 2, cols], ALU.mult).then_inc(vec_free, 1)
                    own(key)
                    vec.tensor_tensor(prod[:, 1, cols], sab[:, 1, cols], sab[:, 0, cols], ALU.subtract).then_inc(prod_ready, 1)
                elif kind == "delays":
                    key = ("corr", p)
                    full(key)
                    for b in pair:
                        row = pbank(for_vec, key)[:, b % 2 * S:(b % 2 + 1) * S]
                        after(vec.max(top[:, b, :], row))
                        last = vec.max_index(topi[:, b, :], top[:, b, :], row)
                    last.then_inc(vec_free, 1)
                    own(key)
                    vec.tensor_tensor(delta[:, two, 0:TOPC], top[:, two, 0:TOPC], top[:, two, 0:1].broadcast_to([P, 2, TOPC]), ALU.subtract)\
                       .then_inc(corr_diff, 1)
                    after(vec.tensor_scalar(delm[:, two, :], topi[:, two, :], 7, None, ALU.bitwise_and))
                    after(vec.tensor_copy(delf[:, two, :], delm[:, two, :]))
                    after(vec.tensor_tensor(hit[:, two], delf[:, two, 0:TOPC].unsqueeze(3).broadcast_to([P, 2, TOPC, 8]),
                                            K["jmod"].unsqueeze(1).unsqueeze(1).broadcast_to([P, 2, TOPC, 8]), ALU.is_equal))
                elif kind == "weights":
                    vec.wait_ge(corr_exp, p + 1)
                    after(vec.tensor_reduce(tsum[:, two], tope[:, two, 0:TOPC], AX.X, ALU.add))
                    vec.reciprocal(trec[:, two], tsum[:, two])
                    after(vec.tensor_tensor(hitw[:, two], hit[:, two], tope[:, two, 0:TOPC].unsqueeze(3).broadcast_to([P, 2, TOPC, 8]), ALU.mult))
                    after(vec.tensor_reduce(roll[:, two], hitw[:, two].rearrange("p b k j -> p b j k"), AX.X, ALU.add))
                    after(vec.tensor_tensor(roll[:, two], roll[:, two], trec[:, two].unsqueeze(2).broadcast_to([P, 2, 8]), ALU.mult))
                    for b in pair:
                        last = vec.tensor_tensor(mbd[:, b, :, :], roll[:, b, :].unsqueeze(1).broadcast_to([P, 16, 8]),
                                                 K["bd"].rearrange("p (h j) -> p h j", h=16), ALU.mult)
                    last.then_inc(mbd_ready, 1)
                elif kind == "out5":
                    for b in pair:
                        residual(("out5", b), b)
                        var(6, b, x)
                elif kind == "choice":
                    act_read(("gl", p))
                    after(vec.tensor_scalar(gde[:, tiles], gex[:, tiles], 1.0, None, ALU.add))
                    vec.wait_ge(gpad_set, 1)
                    after(vec.reciprocal(gpad[:, tiles, 0:E], gde[:, tiles]))
                    for t in range(4 * p, 4 * p + 4):
                        last = vec.max(gtop[:, t, :], gpad[:, t, :])
                    after(last)
                    vec.tensor_copy(gfind[:, tiles, 0:TOPE], gtop[:, tiles, 0:TOPE])
                    after(vec.tensor_reduce(gsum[:, tiles], gtop[:, tiles, 0:TOPE], AX.X, ALU.add))
                    for t in range(4 * p, 4 * p + 4):
                        vec.match_replace(grep[:, t, :], gfind[:, t, :], gpad[:, t, :], 0.0)
                    after(vec.reciprocal(grec[:, tiles], gsum[:, tiles]))
                    share, rest = comb[:, tiles], comr[:, :, tiles]
                    after(vec.tensor_tensor(share, gpad[:, tiles, 0:E], grep[:, tiles, 0:E], ALU.subtract))
                    after(vec.tensor_tensor(share, share, grec[:, tiles].unsqueeze(2).broadcast_to([P, 4, E]), ALU.mult))
                    after(vec.tensor_copy(comb3[:, tiles, 0, :], share))
                    after(vec.tensor_tensor(rest[:, 0], share, comb3[:, tiles, 0, :], ALU.subtract))
                    after(vec.tensor_copy(comb3[:, tiles, 1, :], rest[:, 0]))
                    after(vec.tensor_tensor(rest[:, 1], rest[:, 0], comb3[:, tiles, 1, :], ALU.subtract))
                    vec.tensor_copy(comb3[:, tiles, 2, :], rest[:, 1]).then_inc(comb_ready, 1)
                    key = ("cbT", p)
                    full(key)
                    vec.tensor_copy(combT[0:48, p * 512:(p + 1) * 512], pbank(for_vec, key, 256).bitcast(BF16)[0:48, :]).then_inc(vec_free, 1)
                elif kind == "up":
                    o = hid[:, c, p * 512:(p + 1) * 512]
                    full(("vin", p, c))
                    act_read(("hin", p, c))
                    if c == 8:
                        vec.tensor_tensor(o, sil[:, ups % 2, :], pbank(for_vec, ("vin", p, c)), ALU.mult).then_inc(vec_free, 1)
                    else:
                        vec.tensor_tensor(hmul[:, ups % 2, :], sil[:, ups % 2, :], pbank(for_vec, ("vin", p, c)), ALU.mult).then_inc(vec_free, 1)
                        full(("cw", p, c))
                        own(("vin", p, c))
                        vec.tensor_tensor(o, hmul[:, ups % 2, :], pbank(for_vec, ("cw", p, c)), ALU.mult).then_inc(vec_free, 1)
                    ups += 1
                elif kind == "down":
                    residual(("out6", c), c)
                    vec.sem_inc(res_ready, 1)

        @block.gpsimd
        def _(pool):
            steps = 0

            def after(ins):
                nonlocal steps
                steps += 1
                ins.then_inc(pool_step, 1)
                pool.wait_ge(pool_step, steps)

            def root(dst, tmp, src, n, eps, done):
                after(pool.tensor_scalar(tmp, src, eps, None, ALU.add))
                pool.tensor_tensor(dst, tmp, half[:, 0:n], ALU.pow).then_inc(done, 1)

            def norm_root(k, b):
                pool.wait_ge(ln6_var if k == 6 else ln_var, norm_count(k, b))
                root(rstd[:, k, 2 * b:2 * b + 2], rtmp[:, k, 2 * b:2 * b + 2], mv[:, k, 2 * b:2 * b + 2, 1], 2, EPS, ln6_rstd if k == 6 else ln_rstd)

            def head_root(s, tile):
                u = UNIT[s, tile]
                pool.wait_ge(ssq_ready, u + 1)
                after(pool.tensor_scalar(ssq[:, s, tile, :], ssq[:, s, tile, :], 1e-24, 1.0 / 1024, ALU.max, ALU.mult))
                pool.tensor_tensor(rnk[:, s, tile, :], ssq[:, s, tile, :], half[:, 0:XH], ALU.pow).then_inc(rnk_ready, 1)

            after(pool.memset(half[:], -0.5))
            for b in range(B):
                norm_root(0, b)
            for b in range(B):
                norm_root(1, b)
            pool.wait_ge(mask_in, 16)
            after(pool.tensor_copy(maskf, mask8[:]))
            pool.tensor_copy(vac[:, :, :, 64:128], maskf[:].unsqueeze(2).unsqueeze(3).broadcast_to([P, NT, XC, 64])).then_inc(vac_mask, 1)
            pool.memset(val[:, :, :, 64:128], 1.0).then_inc(val_ones, 1)
            for kind, b, c in ORDER:
                if kind == "head":
                    head_root(b, c)
                elif kind == "out":
                    pool.wait_ge(msq_ready, b + 1)
                    pool.tensor_tensor(rms[:, 2 * b:2 * b + 2], msq[:, 2 * b:2 * b + 2], half[:, 0:2], ALU.pow).then_inc(rms_ready, 1)
                    pool.wait_ge(ln_var, 4 * 2 + b + 1)
                    r, t, v = rstd[:, 2, 2 * b:2 * b + 2], rtmp[:, 2, 2 * b:2 * b + 2], mv[:, 2, 2 * b:2 * b + 2, 1]
                    after(pool.tensor_scalar(t, v, EPS, None, ALU.add))
                    after(pool.tensor_tensor(r, t, half[:, 0:2], ALU.pow))
                    after(pool.tensor_tensor(t, r, r, ALU.mult))
                    after(pool.tensor_tensor(t, t, v, ALU.mult))
                    after(pool.tensor_scalar(t, t, EPS, None, ALU.add))
                    after(pool.tensor_tensor(t, t, half[:, 0:2], ALU.pow))
                    pool.tensor_tensor(r, r, t, ALU.mult).then_inc(ln_rstd, 1)
                elif kind == "result":
                    pool.wait_ge(ovar_ready, b + 1)
                    root(ort[:, 1, 2 * b:2 * b + 2], ort[:, 0, 2 * b:2 * b + 2], omv[:, 2 * b:2 * b + 2, 1], 2, EPS, orstd_ready)
                    norm_root(3, b)
            for b in range(B):
                norm_root(4, b)
            for n in range(4):
                pool.wait_ge(lead_ready, n + 1)
                p, k = n // 2, n % 2
                pool.tensor_tensor(qh[:, k, 1, p * 512:(p + 1) * 512], rot[:, k, 0, :], qh[:, k, 0, p * 512:(p + 1) * 512], ALU.subtract)\
                    .then_inc(rest_ready, 1)
            after(pool.memset(mneg, 0.0))
            pool.sem_inc(mneg_zero, 1)
            pool.memset(va1[:, :, :, 2 * AD:32], 0.0)
            pool.memset(va1[:, :, :, AD:2 * AD], 1.0).then_inc(va1_ones, 1)
            after(pool.memset(place, 0.0))
            pool.sem_inc(place_zero, 1)
            after(pool.memset(gpad[:, :, E:PADE], -1.0))
            after(pool.memset(gfind[:, :, TOPE:8], -1.0))
            pool.sem_inc(gpad_set, 1)
            for kind, b, i in LORDER:
                if kind == "out":
                    norm_root(5, b)
                elif kind == "out5":
                    norm_root(6, 2 * b)
                    norm_root(6, 2 * b + 1)

        @block.sync
        def _(sp):
            for dst, src, done in ((x, "x", x_in), (w_k, "k", k_in), (w_m, "m", m_in), (cx, "ctx", c_in), (w_x, "xw", xw_in),
                                   (mask8, "mask", mask_in), (w_f, "f", f_in)):
                sp.dma_start(dst[:], io[src]).then_inc(done, 16)
            sp.wait_ge(ln_var, 4 * 2 + B)
            for dst, src, done in ((w_c, "c", c1_in), (w_a, "a", a_in), (w_r, "r", r_in), (w_h, "h", h_in), (w_b, "b", b_in)):
                sp.dma_start(dst, io[src]).then_inc(done, 16)
            sp.wait_ge(vec_full, for_vec.number[("out1", B - 1)] + 1)
            sp.dma_start(w_e, io["e"]).then_inc(e_in, 16)
            for b in range(B):
                sp.wait_ge(res_ready, b + 1)
                sp.dma_start(io["out"][:, 2 * b:2 * b + 2, :], x[:, 2 * b:2 * b + 2, :]).then_inc(stored, 16)
            sp.wait_ge(stored, 16 * B)


def program(nc, arrays):
    io = {}
    for name, a in arrays.items():
        io[name] = nc.dram_tensor("in_" + name, a.shape, mybir.dt.from_np(a.dtype), kind="ExternalInput").ap()
    for name in ("x", "ctx"):
        io[name] = io[name].rearrange("b (h p) d -> p (b h) d", p=P)
    out = nc.dram_tensor("out_rows", (B, S, D), F32, kind="ExternalOutput").ap()
    io["out"] = out.rearrange("b (h p) d -> p (b h) d", p=P)
    decoder(nc, io)


def kernel(**inputs):
    import concourse.bacc as _bacc
    import ml_dtypes
    import numpy as np
    from concourse.bass_utils import run_bass_kernel_spmd

    w = {name: np.asarray(a) for name, a in inputs.items()}

    def pack(spec, parts):
        cols = []
        for name, n in spec:
            a = parts[name]
            assert a.size in (P * n, n), (name, a.shape)
            cols.append(a.reshape(P, n) if a.size == P * n else np.broadcast_to(a.reshape(1, n), (P, n)))
        return np.ascontiguousarray(np.concatenate(cols, axis=1))

    def chunks(a):
        return a.reshape(-1, P, a.shape[1]).transpose(1, 0, 2)

    def col(a):
        return a.reshape(-1, P).T

    m = "L0_attn_"
    mamba = pack(SPEC_M, {
        "in_w": w[m + "in_proj_w"], "conv_w": chunks(w[m + "conv_w"][:, 0, :]), "conv_b": col(w[m + "conv_b"]),
        "dt_bias": w[m + "dt_bias"], "a_log": w[m + "A_log"], "skip": col(np.repeat(w[m + "D"], 64)), "norm_w": col(w[m + "norm_w"]),
        "out_w": chunks(w[m + "out_proj_w"])})
    m = "L0_xattn_"
    cross = pack(SPEC_X, {
        "lnx_w": w[m + "ln_x_w"].reshape(P, 1), "lnx_b": w[m + "ln_x_b"].reshape(P, 1), "lnl_w": w[m + "ln_l_w"].reshape(P, 1),
        "lnl_b": w[m + "ln_l_b"].reshape(P, 1), "q_scale": np.tile(w[m + "q_scale"], 2).reshape(P, 1), "k_scale": np.tile(w[m + "k_scale"], 2).reshape(P, 1),
        "wq": w[m + "Wq"], "wkv": w[m + "Wkv"], "wo": chunks(w[m + "Wo"]), "lno_w": w[m + "ln_o_w"], "lno_b": w[m + "ln_o_b"],
        "q_scale_row": w[m + "q_scale"], "k_scale_row": w[m + "k_scale"]})
    m = "L0_ffn_"
    rec = pack(SPEC_F, {n: w[m + n].T if w[m + n].ndim == 2 else w[m + n].reshape(P, 1) for n, _ in SPEC_F})
    attn = pack(SPEC_A, {n: w["L1_attn_" + n] for n, _ in SPEC_A})
    corr = pack(SPEC_C, {n: w["L1_xattn_" + n] for n, _ in SPEC_C})
    m = "L1_ffn_"
    moe = pack(SPEC_E, {
        "gate": w[m + "gate_w"].T, "ws_in": w[m + "ws_in"], "vs_in": w[m + "vs_in"],
        "e_win": w[m + "e_win"].transpose(1, 0, 2), "e_vin": w[m + "e_vin"].transpose(1, 0, 2),
        "w_out": chunks(np.concatenate([w[m + "e_wout"].reshape(-1, D), w[m + "ws_out"]]))})

    eye, i, f = np.eye(P), np.arange(P), np.arange(P)
    tri = (i[:, None] <= i[None, :]).astype(np.float64)
    t, tau = np.arange(S), np.arange(S)
    cos = np.cos(2 * np.pi * np.outer(t, f) / S)
    sin = np.sin(2 * np.pi * np.outer(t, f) / S)
    mid = np.where(t % 2 == 0, 1.0, -1.0)
    cos_mid, sin_mid = cos.copy(), sin.copy()
    cos_mid[:, 0] = mid
    sin_mid[:, 0] = mid
    dft = np.stack([cos, sin_mid, cos_mid], axis=1).reshape(2, P, 3, P).transpose(1, 0, 2, 3)
    weight = np.where(f == 0, 1.0, 2.0)[:, None] / S
    icos = weight * np.cos(2 * np.pi * np.outer(f, tau) / S)
    isin = weight * np.sin(2 * np.pi * np.outer(f, tau) / S)
    isin[0] = mid / S
    freq = (np.arange(S, dtype=np.float32)[:, None] * (1.0 / np.float32(10000.0) ** (np.arange(0, AD, 2, dtype=np.float32) / np.float32(AD)))[None, :]).T
    freq = np.tile(np.repeat(freq, 2, axis=0), (AH, 1))
    rope = pack(SPEC_R, {"cos": np.cos(freq), "sin": np.sin(freq)}).astype(np.float32)
    heads = (i[:, None] // 8 == i[None, :] // 8).astype(np.float64)
    consts = pack(SPEC_K, {
        "ident": eye, "ones": np.ones((P, P)), "tri": tri, "gmask": np.concatenate([tri, np.ones((P, P)), tri], axis=1), "dft": dft,
        "idft": np.concatenate([icos, isin], axis=1), "keep": (f > 0).astype(np.float64).reshape(P, 1),
        "sixteen": np.where(i % 32 == 24, 16.0, 0.0).reshape(P, 1), "jmod": (i[:, None] - np.arange(8)[None, :]) % 8, "bd": heads, "permute": (i[:, None] == (i[None, :] % AH) * AD + i[None, :] // AH).astype(np.float64)}).astype(np.float32)
    sel = np.zeros((4, P, 4, P))
    for j in range(4):
        for g in range(4):
            for d in range(8):
                for r, (qp, kp) in enumerate(((0, 0), (0, 1), (1, 0))):
                    sel[qp, 8 * (4 * j + g) + d, j, 32 * g + 8 * r + d] = 1.0
                    sel[2 + kp, 8 * (4 * j + g) + d, j, 32 * g + 8 * r + d] = 1.0
    halves = pack(SPEC_H, {"ident": eye, "selq1": sel[0], "selq2": sel[1], "selk1": sel[2], "selk2": sel[3]}).astype(np.float16)
    far = np.float64(-1e30)
    expand = np.zeros((P, 8, P))
    for part in range(3):
        for e in range(E):
            expand[part * E + e, e // 2, e % 2 * 64:e % 2 * 64 + 64] = 1.0
    brain = pack(SPEC_B, {
        "ident": eye, "mask_row": np.where(i[None, :] > i[:, None], far, 0.0), "mask_col": np.where(i[:, None] > i[None, :], far, 0.0),
        "expand": expand}).astype(ml_dtypes.bfloat16)

    arrays = {
        "x": np.ascontiguousarray(w["x"]), "ctx": np.ascontiguousarray(w["ctx_1024"]),
        "mask": np.ascontiguousarray(w["mask_BxS2_bk0"].reshape(NT, P).T), "m": mamba, "xw": cross, "f": rec, "a": attn, "c": corr,
        "e": moe, "k": consts, "h": halves, "r": rope, "b": brain}
    nc = _bacc.Bacc("TRN2", target_bir_lowering=False, num_devices=1)
    program(nc, arrays)
    return run_bass_kernel_spmd(nc, [{"in_" + name: a for name, a in arrays.items()}], core_ids=[0]).results[0]["out_rows"]
```
